# Optimizing a Trainium2 kernel written in Bass

```python
import numpy as np
import jax
import jax.numpy as jnp

def _softmax(x, axis=-1):
    return jax.nn.softmax(x, axis=axis)

def _gelu(x):
    return jax.nn.gelu(x, approximate=True)

def _silu(x):
    return jax.nn.silu(x)

def _sigmoid(x):
    return jax.nn.sigmoid(x)

def _layernorm(x, axis=-1, eps=1e-05):
    m = jnp.mean(x, axis=axis, keepdims=True)
    v = jnp.var(x, axis=axis, keepdims=True)
    return (x - m) / jnp.sqrt(v + eps)

def _scatter_add(tgt, idx, src, axis=0):
    return tgt.at[idx].add(src)

def _segment_sum(src, seg, n):
    return jax.ops.segment_sum(src, seg, n)
kernel_name = 'mk_hybrid_d1_jaxref_r8_64bb93'

def setup_inputs(seed: int=0):
    np.random.seed(seed)
    _w = jnp.asarray

    def _L0_attn_a_setup():
        import jax, jax.numpy as jnp
        import numpy as np
        HIDDEN = 128
        NHEADS = 16
        HEAD_DIM = HIDDEN // NHEADS
        CONV_K = 4
        EPS = 1e-06

        def _short_conv(x, w):
            K = w.shape[-1]
            L = x.shape[1]
            xp = jnp.pad(x, ((0, 0), (K - 1, 0), (0, 0)))
            y = jnp.zeros_like(x)
            for k in range(K):
                y = y + xp[:, k:k + L, :] * w[:, k]
            return y

        def _l2norm(x):
            n = jnp.sqrt(jnp.sum(x * x, axis=-1, keepdims=True))
            return x / jnp.maximum(n, EPS)

        def _delta_rule(q, k, v, beta):
            b, h, l, dk = q.shape
            dv = v.shape[-1]
            q = q * dk ** (-0.5)
            S0 = jnp.zeros((b, h, dk, dv), dtype=v.dtype)

            def step(S, inp):
                q_t, k_t, v_t, b_t = inp
                v_new = (v_t - jnp.einsum('bhd,bhdm->bhm', k_t, S)) * b_t[..., None]
                S = S + jnp.einsum('bhd,bhm->bhdm', k_t, v_new)
                o_t = jnp.einsum('bhd,bhdm->bhm', q_t, S)
                return (S, o_t)
            ql, kl, vl = (t.transpose(2, 0, 1, 3) for t in (q, k, v))
            bl = beta.transpose(2, 0, 1)
            S, o = jax.lax.scan(step, S0, (ql, kl, vl, bl))
            return (o.transpose(1, 2, 0, 3), S)

        def _reference_tuple_inner(x, Wq, Wk, Wv, Wb, Wo, conv_q, conv_k, conv_v, o_norm_w):
            b, l, _ = x.shape
            q = x @ Wq.T
            k = x @ Wk.T
            v = x @ Wv.T
            beta = jax.nn.sigmoid(x @ Wb.T)
            q = jax.nn.silu(_short_conv(q, conv_q))
            k = jax.nn.silu(_short_conv(k, conv_k))
            v = jax.nn.silu(_short_conv(v, conv_v))

            def to_heads(t):
                return t.reshape(b, l, NHEADS, HEAD_DIM).transpose(0, 2, 1, 3)
            q, k, v = (to_heads(q), to_heads(k), to_heads(v))
            beta = beta.transpose(0, 2, 1)
            q = _l2norm(q)
            k = _l2norm(k)
            o, S = _delta_rule(q, k, v, beta)
            o = o * jax.lax.rsqrt(jnp.mean(o * o, axis=-1, keepdims=True) + EPS) * o_norm_w
            out = o.transpose(0, 2, 1, 3).reshape(b, l, HIDDEN) @ Wo.T
            return (out, S)
        key = jax.random.key(seed)
        ks = jax.random.split(key, 10)
        b, l = (4, 128)
        init = 0.02
        return {'x': jax.random.normal(ks[0], (b, l, HIDDEN), dtype=jnp.float32), 'Wq': jax.random.normal(ks[1], (HIDDEN, HIDDEN), dtype=jnp.float32) * init, 'Wk': jax.random.normal(ks[2], (HIDDEN, HIDDEN), dtype=jnp.float32) * init, 'Wv': jax.random.normal(ks[3], (HIDDEN, HIDDEN), dtype=jnp.float32) * init, 'Wb': jax.random.normal(ks[4], (NHEADS, HIDDEN), dtype=jnp.float32) * init, 'Wo': jax.random.normal(ks[5], (HIDDEN, HIDDEN), dtype=jnp.float32) * init, 'conv_q': jax.random.normal(ks[6], (HIDDEN, CONV_K), dtype=jnp.float32) * 0.3, 'conv_k': jax.random.normal(ks[7], (HIDDEN, CONV_K), dtype=jnp.float32) * 0.3, 'conv_v': jax.random.normal(ks[8], (HIDDEN, CONV_K), dtype=jnp.float32) * 0.3, 'o_norm_w': jnp.ones((HEAD_DIM,), dtype=jnp.float32)}
    _L0_attn_a_in = _L0_attn_a_setup()

    def _L0_attn_b_setup():
        import jax, jax.numpy as jnp
        import numpy as np
        NUM_HEADS = 16
        EPS = 1e-05
        CHUNK = 128

        def _linear_attention(x, Wq, Wk, Wv, Wo, bo):
            B, T, E = x.shape
            H = NUM_HEADS
            d = E // H

            def proj(W):
                return (x @ W.T).reshape(B, T, H, d).transpose(0, 2, 1, 3)
            phi_q = jax.nn.elu(proj(Wq)) + 1.0
            phi_k = jax.nn.elu(proj(Wk)) + 1.0
            V = proj(Wv)
            nC = T // CHUNK

            def to_chunks(a):
                return a.reshape(B, H, nC, CHUNK, d).transpose(2, 0, 1, 3, 4)
            qc, kc, vc = (to_chunks(phi_q), to_chunks(phi_k), to_chunks(V))
            mask = jnp.tril(jnp.ones((CHUNK, CHUNK), x.dtype))
            S0 = jnp.zeros((B, H, d, d), x.dtype)
            z0 = jnp.zeros((B, H, d), x.dtype)

            def step(carry, inp):
                S, z = carry
                q, k, v = inp
                A = jnp.einsum('bhid,bhjd->bhij', q, k) * mask
                num = jnp.einsum('bhij,bhjd->bhid', A, v) + jnp.einsum('bhid,bhde->bhie', q, S)
                den = jnp.sum(A, axis=-1) + jnp.einsum('bhid,bhd->bhi', q, z) + EPS
                out = num / den[..., None]
                S = S + jnp.einsum('bhjd,bhje->bhde', k, v)
                z = z + jnp.sum(k, axis=2)
                return ((S, z), out)
            _, outs = jax.lax.scan(step, (S0, z0), (qc, kc, vc))
            out = outs.transpose(1, 2, 0, 3, 4).reshape(B, H, T, d)
            out = out.transpose(0, 2, 1, 3).reshape(B, T, E)
            return out @ Wo.T + bo
        key = jax.random.key(seed)
        ks = jax.random.split(key, 6)
        B, T, E = (2, 256, 128)
        s = 1.0 / np.sqrt(E)
        return {'x': jax.random.normal(ks[0], (B, T, E), jnp.float32), 'Wq': jax.random.normal(ks[1], (E, E), jnp.float32) * s, 'Wk': jax.random.normal(ks[2], (E, E), jnp.float32) * s, 'Wv': jax.random.normal(ks[3], (E, E), jnp.float32) * s, 'Wo': jax.random.normal(ks[4], (E, E), jnp.float32) * s, 'bo': jnp.zeros((E,), jnp.float32)}
    _L0_attn_b_in = _L0_attn_b_setup()

    def _L0_ffn_setup():
        import jax, jax.numpy as jnp
        import numpy as np
        TOP_K = 2
        key = jax.random.key(seed)
        k1, k2, k3, k4 = jax.random.split(key, 4)
        B, T, D, F, E = (2, 128, 128, 256, 8)
        x = jax.random.normal(k1, (B, T, D), dtype=jnp.float32)
        Wg = jax.random.normal(k2, (D, E), dtype=jnp.float32) * 0.02
        W1 = jax.random.normal(k3, (E, D, F), dtype=jnp.float32) * 0.02
        W2 = jax.random.normal(k4, (E, F, D), dtype=jnp.float32) * 0.02
        return {'x': x, 'Wg': Wg, 'W1': W1, 'W2': W2}
    _L0_ffn_in = _L0_ffn_setup()
    _d = {'L0_attn_a_x': _L0_attn_a_in['x'], 'L0_attn_a_Wq': _L0_attn_a_in['Wq'], 'L0_attn_a_Wk': _L0_attn_a_in['Wk'], 'L0_attn_a_Wv': _L0_attn_a_in['Wv'], 'L0_attn_a_Wb': _L0_attn_a_in['Wb'], 'L0_attn_a_Wo': _L0_attn_a_in['Wo'], 'L0_attn_a_conv_q': _L0_attn_a_in['conv_q'], 'L0_attn_a_conv_k': _L0_attn_a_in['conv_k'], 'L0_attn_a_conv_v': _L0_attn_a_in['conv_v'], 'L0_attn_a_o_norm_w': _L0_attn_a_in['o_norm_w'], 'L0_attn_b_Wq': _L0_attn_b_in['Wq'], 'L0_attn_b_Wk': _L0_attn_b_in['Wk'], 'L0_attn_b_Wv': _L0_attn_b_in['Wv'], 'L0_attn_b_Wo': _L0_attn_b_in['Wo'], 'L0_attn_b_bo': _L0_attn_b_in['bo'], 'L0_ffn_Wg': _L0_ffn_in['Wg'], 'L0_ffn_W1': _L0_ffn_in['W1'], 'L0_ffn_W2': _L0_ffn_in['W2']}
    _x0 = _d['L0_attn_a_x']
    _d['L0_attn_a_x'] = jax.random.normal(jax.random.fold_in(jax.random.key(seed), 1), (8, 512, 128), dtype=_x0.dtype)
    del _x0
    return _d

def reference(L0_attn_a_x, L0_attn_a_Wq, L0_attn_a_Wk, L0_attn_a_Wv, L0_attn_a_Wb, L0_attn_a_Wo, L0_attn_a_conv_q, L0_attn_a_conv_k, L0_attn_a_conv_v, L0_attn_a_o_norm_w, L0_attn_b_Wq, L0_attn_b_Wk, L0_attn_b_Wv, L0_attn_b_Wo, L0_attn_b_bo, L0_ffn_Wg, L0_ffn_W1, L0_ffn_W2):

    def _L0_attn_a_ref(x, Wq, Wk, Wv, Wb, Wo, conv_q, conv_k, conv_v, o_norm_w):
        import jax, jax.numpy as jnp
        import numpy as np
        HIDDEN = 128
        NHEADS = 16
        HEAD_DIM = HIDDEN // NHEADS
        CONV_K = 4
        EPS = 1e-06

        def _short_conv(x, w):
            K = w.shape[-1]
            L = x.shape[1]
            xp = jnp.pad(x, ((0, 0), (K - 1, 0), (0, 0)))
            y = jnp.zeros_like(x)
            for k in range(K):
                y = y + xp[:, k:k + L, :] * w[:, k]
            return y

        def _l2norm(x):
            n = jnp.sqrt(jnp.sum(x * x, axis=-1, keepdims=True))
            return x / jnp.maximum(n, EPS)

        def _delta_rule(q, k, v, beta):
            b, h, l, dk = q.shape
            dv = v.shape[-1]
            q = q * dk ** (-0.5)
            S0 = jnp.zeros((b, h, dk, dv), dtype=v.dtype)

            def step(S, inp):
                q_t, k_t, v_t, b_t = inp
                v_new = (v_t - jnp.einsum('bhd,bhdm->bhm', k_t, S)) * b_t[..., None]
                S = S + jnp.einsum('bhd,bhm->bhdm', k_t, v_new)
                o_t = jnp.einsum('bhd,bhdm->bhm', q_t, S)
                return (S, o_t)
            ql, kl, vl = (t.transpose(2, 0, 1, 3) for t in (q, k, v))
            bl = beta.transpose(2, 0, 1)
            S, o = jax.lax.scan(step, S0, (ql, kl, vl, bl))
            return (o.transpose(1, 2, 0, 3), S)

        def _reference_tuple_inner(x, Wq, Wk, Wv, Wb, Wo, conv_q, conv_k, conv_v, o_norm_w):
            b, l, _ = x.shape
            q = x @ Wq.T
            k = x @ Wk.T
            v = x @ Wv.T
            beta = jax.nn.sigmoid(x @ Wb.T)
            q = jax.nn.silu(_short_conv(q, conv_q))
            k = jax.nn.silu(_short_conv(k, conv_k))
            v = jax.nn.silu(_short_conv(v, conv_v))

            def to_heads(t):
                return t.reshape(b, l, NHEADS, HEAD_DIM).transpose(0, 2, 1, 3)
            q, k, v = (to_heads(q), to_heads(k), to_heads(v))
            beta = beta.transpose(0, 2, 1)
            q = _l2norm(q)
            k = _l2norm(k)
            o, S = _delta_rule(q, k, v, beta)
            o = o * jax.lax.rsqrt(jnp.mean(o * o, axis=-1, keepdims=True) + EPS) * o_norm_w
            out = o.transpose(0, 2, 1, 3).reshape(b, l, HIDDEN) @ Wo.T
            return (out, S)
        return _reference_tuple_inner(x, Wq, Wk, Wv, Wb, Wo, conv_q, conv_k, conv_v, o_norm_w)[0]

    def _L0_attn_b_ref(x, Wq, Wk, Wv, Wo, bo):
        import jax, jax.numpy as jnp
        import numpy as np
        NUM_HEADS = 16
        EPS = 1e-05
        CHUNK = 128

        def _linear_attention(x, Wq, Wk, Wv, Wo, bo):
            B, T, E = x.shape
            H = NUM_HEADS
            d = E // H

            def proj(W):
                return (x @ W.T).reshape(B, T, H, d).transpose(0, 2, 1, 3)
            phi_q = jax.nn.elu(proj(Wq)) + 1.0
            phi_k = jax.nn.elu(proj(Wk)) + 1.0
            V = proj(Wv)
            nC = T // CHUNK

            def to_chunks(a):
                return a.reshape(B, H, nC, CHUNK, d).transpose(2, 0, 1, 3, 4)
            qc, kc, vc = (to_chunks(phi_q), to_chunks(phi_k), to_chunks(V))
            mask = jnp.tril(jnp.ones((CHUNK, CHUNK), x.dtype))
            S0 = jnp.zeros((B, H, d, d), x.dtype)
            z0 = jnp.zeros((B, H, d), x.dtype)

            def step(carry, inp):
                S, z = carry
                q, k, v = inp
                A = jnp.einsum('bhid,bhjd->bhij', q, k) * mask
                num = jnp.einsum('bhij,bhjd->bhid', A, v) + jnp.einsum('bhid,bhde->bhie', q, S)
                den = jnp.sum(A, axis=-1) + jnp.einsum('bhid,bhd->bhi', q, z) + EPS
                out = num / den[..., None]
                S = S + jnp.einsum('bhjd,bhje->bhde', k, v)
                z = z + jnp.sum(k, axis=2)
                return ((S, z), out)
            _, outs = jax.lax.scan(step, (S0, z0), (qc, kc, vc))
            out = outs.transpose(1, 2, 0, 3, 4).reshape(B, H, T, d)
            out = out.transpose(0, 2, 1, 3).reshape(B, T, E)
            return out @ Wo.T + bo
        return _linear_attention(x, Wq, Wk, Wv, Wo, bo)

    def _L0_ffn_ref(x, Wg, W1, W2):
        import jax, jax.numpy as jnp
        import numpy as np
        TOP_K = 2
        B, T, D = x.shape
        E = Wg.shape[-1]
        xt = x.reshape(B * T, D)
        logits = xt @ Wg
        probs = jax.nn.softmax(logits, axis=-1)
        topw, topi = jax.lax.top_k(probs, TOP_K)
        topw = topw / jnp.sum(topw, axis=-1, keepdims=True)
        combine = jnp.sum(jax.nn.one_hot(topi, E, dtype=xt.dtype) * topw[..., None], axis=1)
        h = jax.nn.relu(jnp.einsum('nd,edf->enf', xt, W1))
        y = jnp.einsum('enf,efd->end', h, W2)
        out = jnp.einsum('ne,end->nd', combine, y)
        return out.reshape(B, T, D)
    x = L0_attn_a_x
    x = x + _L0_attn_a_ref(_layernorm(x, axis=-1), L0_attn_a_Wq, L0_attn_a_Wk, L0_attn_a_Wv, L0_attn_a_Wb, L0_attn_a_Wo, L0_attn_a_conv_q, L0_attn_a_conv_k, L0_attn_a_conv_v, L0_attn_a_o_norm_w)
    x = x + _L0_ffn_ref(_layernorm(x, axis=-1), L0_ffn_Wg, L0_ffn_W1, L0_ffn_W2)
    x = x + _L0_attn_b_ref(_layernorm(x, axis=-1), L0_attn_b_Wq, L0_attn_b_Wk, L0_attn_b_Wv, L0_attn_b_Wo, L0_attn_b_bo)
    x = x + _L0_ffn_ref(_layernorm(x, axis=-1), L0_ffn_Wg, L0_ffn_W1, L0_ffn_W2)
    return x

_drawn_inputs = setup_inputs


def setup_inputs(seed=0):
    import zlib

    import numpy as np

    out = dict(_drawn_inputs(seed))
    spreads = {'L0_attn_a_o_norm_w': (1.0, 0.2), 'L0_attn_b_bo': (0.0, 0.1)}
    factors = {'L0_attn_b_Wq': 2.769}
    for name, (base, spread) in spreads.items():
        noise = np.random.default_rng([zlib.crc32(name.encode()), seed]).standard_normal(out[name].shape)
        drawn = base * np.exp(spread * noise) if base else spread * noise
        out[name] = jnp.asarray(drawn.astype(out[name].dtype))
    for name, factor in factors.items():
        out[name] = (out[name] * factor).astype(out[name].dtype)
    return out
```

```python
from contextlib import ExitStack

import concourse.bass as bass
from concourse import mybir

F32 = mybir.dt.float32
ALU = mybir.AluOpType
ACT = mybir.ActivationFunctionType
AX_X = mybir.AxisListType.X

B, L, D = 8, 512, 128
H, HD = 16, 8
KC = 4
E, FF = 8, 256
CH = 64
NCH = L // CH
NT = B * CH
J = NT // 128
NB = CH // 2
FC = FF // 128
HV = HD + 1
NP = H // 2
LN_EPS, DELTA_EPS, LIN_EPS = 1e-5, 1e-6, 1e-5
QSCALE = float(HD) ** -0.5


def due(count):
    return not isinstance(count, int) or count > 0


def held(eng, count):
    return count if isinstance(count, int) else eng.snap(eng.to_reg(count))


def bc(ap, axis, n):
    ap = ap.unsqueeze(axis)
    shape = list(ap.shape)
    shape[axis] = n
    return ap.to_broadcast(shape)


def build(nc, d, out):
    with ExitStack() as ctx:
        def sb(name, shape):
            return ctx.enter_context(nc.sbuf_tensor(name, shape, F32))

        def sem(name):
            return ctx.enter_context(nc.semaphore(name))

        ident = sb("ident", [128, 128])
        ones_block = sb("ones_block", [128, 128])
        causal = sb("causal", [128, CH])
        lower = sb("lower", [128, E, E])
        state_mask = sb("state_mask", [128, H, HV])
        head_mask = sb("head_mask", [128, HD])
        wqkv = sb("wqkv", [128, 3, D])
        conv = sb("conv", [128, 3, KC, D])
        wtap = sb("wtap", [128, 3, KC, D])
        wbeta = sb("wbeta", [128, H])
        wo_a = sb("wo_a", [128, D])
        onorm = sb("onorm", [128, 1])
        wo_n = sb("wo_n", [128, D])
        wqk_b = sb("wqk_b", [128, 2, D])
        wv_b = sb("wv_b", [128, 2, NP * HD])
        wo_b = sb("wo_b", [128, D])
        bo_row = sb("bo_row", [1, D])
        ones_row = sb("ones_row", [1, 128])
        wg = sb("wg", [128, E])
        w1 = sb("w1", [128, E, FF])
        w2 = sb("w2", [128, E, FC, D])
        eps_ln = sb("eps_ln", [128, 1])
        eps_on = sb("eps_on", [128, 1])
        one_col = sb("one_col", [128, 1])

        x_in = sb("x_in", [128, J, D])
        bn6 = sb("bn6", [128, J, 6])
        mv = sb("mv", [128, J, 2])
        rstd = sb("rstd", [128, J])
        xn = sb("xn", [128, J, D])
        xnT = sb("xnT", [128, B, KC - 1 + CH])
        sig = sb("sig", [128, 3, NT])
        qkv = sb("qkv", [128, 3, NT])
        beta_T = sb("beta_T", [H, NT])
        sq = sb("sq", [128, 2, NT])
        rqk = sb("rqk", [128, 2, NT])
        pin = sb("pin", [128, 3, HD, CH])
        beta_p = sb("beta_p", [128, CH])
        q_p = sb("q_p", [128, HD, CH])
        k_p = sb("k_p", [128, HD, CH])
        nkb = sb("nkb", [128, HD, CH])
        prod_mem = sb("prod_mem", [128, CH * HD * HV])
        prod = prod_mem[:].rearrange("p (t m e) -> p t m e", t=CH, m=HD)
        u = sb("u", [128, NB, 2, HD])
        hist_mem = sb("hist_mem", [128, (NB + 1) * HD * HD * 3])
        hist = hist_mem[:].rearrange("p (n m d s) -> p n m d s", n=NB + 1, m=HD, d=HD)
        dots = sb("dots", [128, 2, NB, HD])
        ng = sb("ng", [128, NB])
        nqk = sb("nqk", [128, NB])
        oq_mem = sb("oq_mem", [128, NB * HD * HD])
        oq = oq_mem[:].rearrange("p (n m d) -> p n m d", n=NB, m=HD)
        ofix = sb("ofix", [128, NB, HD])
        o_p = sb("o_p", [128, HD, CH])
        o_T = sb("o_T", [128, NT])
        osq = sb("osq", [128, NT])
        orn = sb("orn", [128, NT])
        on = sb("on", [128, NT])
        x_r = sb("x_r", [128, J, D])
        bn6f = sb("bn6f", [128, J, 6])
        mvf = sb("mvf", [128, J, 2])
        rstdf = sb("rstdf", [128, J])
        x1 = sb("x1", [128, J, D])
        xf = sb("xf", [128, J, D])
        xfT = sb("xfT", [128, NT])
        logit = sb("logit", [128, J, E])
        lmax = sb("lmax", [128, J])
        lsub = sb("lsub", [128, J, E])
        above = sb("above", [128, J, E, E])
        same = sb("same", [128, J, E, E])
        rank = sb("rank", [128, J, E])
        chosen = sb("chosen", [128, J, E])
        pexp = sb("pexp", [128, J, E])
        pick = sb("pick", [128, J, E])
        psum = sb("psum", [128, J])
        rsum = sb("rsum", [128, J])
        gate = sb("gate", [128, J, E])
        xe = sb("xe", [128, E, J, D])
        xeT = sb("xeT", [128, 2, NT])
        hid = sb("hid", [128, 2, FC, NT])
        yT = sb("yT", [128, NT])
        x2 = sb("x2", [128, J, D])
        x_b = sb("x_b", [128, J, D])
        phi_min = sb("phi_min", [128, 2, NT])
        phi_q = sb("phi_q", [128, NT])
        phi_k = sb("phi_k", [128, B, 2, CH])
        q_bd = hist_mem[:, 0:HD * NT].rearrange("p (h t) -> p h t", h=HD)
        v_bd = sb("v_bd", [128, B, NP, 2, HV])
        att_size, ktok_size, state_size = 2 * NP * 2 * CH, B * D, B * H * HV
        att = prod_mem[:, 0:att_size].rearrange("p (k r b i t) -> p k r b i t", k=2, r=2, b=2, i=4)
        k_tok = prod_mem[:, att_size:att_size + ktok_size].rearrange("p (b f) -> p b f", b=B)
        dstate = prod_mem[:, att_size + ktok_size:att_size + ktok_size + state_size].rearrange(
            "p (b h e) -> p b h e", b=B, h=H)
        state = sb("state", [128, B, H, HV])
        den = sb("den", [128, J, H])
        rden = sb("rden", [128, J, H])
        lin = oq_mem[:, 0:NT].rearrange("p (j d) -> p j d", j=J)
        linT = oq_mem[:, NT:2 * NT]
        x3 = oq_mem[:, 2 * NT:3 * NT].rearrange("p (j d) -> p j d", j=J)

        bank = ctx.enter_context(nc.psum_tensor("bank", [128, 8, 512], F32))
        TB, QB, KB, MB, XB, ZB, YB = 0, 1, 2, 3, 4, 5, 7

        s_qkv = nc.dram_tensor("s_qkv", [3, B, D, CH], F32, kind="Internal").ap()
        s_beta = nc.dram_tensor("s_beta", [B, H, CH], F32, kind="Internal").ap()
        s_o = nc.dram_tensor("s_o", [B, H, HD, CH], F32, kind="Internal").ap()
        s_x = nc.dram_tensor("s_x", [NCH, 128, J * D], F32, kind="Internal").ap()

        go, w_loaded, taps_ready = sem("go"), sem("w_loaded"), sem("taps_ready")
        pool_ready = sem("pool_ready")
        x_loaded, bn_done, mv_ready = sem("x_loaded"), sem("bn_done"), sem("mv_ready")
        rstd_log, rstd_ready, xn_ready = sem("rstd_log"), sem("rstd_ready"), sem("xn_ready")
        xn_transposed, xnT_ready, halo_kept = sem("xn_transposed"), sem("xnT_ready"), sem("halo_kept")
        projected, sig_exp, sig_log = sem("projected"), sem("sig_exp"), sem("sig_log")
        sig_ready, beta_exp, beta_log = sem("sig_ready"), sem("beta_exp"), sem("beta_log")
        beta_ready, silu_ready = sem("beta_ready"), sem("silu_ready")
        squared, norms, norm_max = sem("squared"), sem("norms"), sem("norm_max")
        norm_log, norm_ready, qk_ready = sem("norm_log"), sem("norm_ready"), sem("qk_ready")
        qkv_stored, pairs_loaded = sem("qkv_stored"), sem("pairs_loaded")
        pairs_taken, dot_ready = sem("pairs_taken"), sem("dot_ready")
        scal_ready, step, o_part = sem("scal_ready"), sem("step"), sem("o_part")
        o_ready, o_stored, o_loaded = sem("o_ready"), sem("o_stored"), sem("o_loaded")
        o_squared, o_norms, o_log = sem("o_squared"), sem("o_norms"), sem("o_log")
        o_rnorm, on_ready, o_projected = sem("o_rnorm"), sem("on_ready"), sem("o_projected")
        xr_loaded = sem("xr_loaded")
        x1_ready, bnf_done, mvf_ready = sem("x1_ready"), sem("bnf_done"), sem("mvf_ready")
        rstdf_log, rstdf_ready, xf_ready = sem("rstdf_log"), sem("rstdf_ready"), sem("xf_ready")
        xf_transposed, xfT_ready = sem("xf_transposed"), sem("xfT_ready")
        routed, route, lsub_ready = sem("routed"), sem("route"), sem("lsub_ready")
        pexp_ready, gate_ready, xe_ready = sem("pexp_ready"), sem("gate_ready"), sem("xe_ready")
        xe_transposed, xeT_ready = sem("xe_transposed"), sem("xeT_ready")
        z_ready, hid_ready, y_part = sem("z_ready"), sem("hid_ready"), sem("y_part")
        yT_ready, y_transposed, x2_ready = sem("yT_ready"), sem("y_transposed"), sem("x2_ready")
        x2_stored = sem("x2_stored")
        xb_loaded, qk_projected, phi_low = sem("xb_loaded"), sem("qk_projected"), sem("phi_low")
        phi_exp, phi_ready, v_projected = sem("phi_exp"), sem("phi_ready"), sem("v_projected")
        v_ready, qbd_ready = sem("v_ready"), sem("qbd_ready")
        k_transposed, ktok_ready, scores = sem("k_transposed"), sem("ktok_ready"), sem("scores")
        att_ready, numer, den_ready = sem("att_ready"), sem("numer"), sem("den_ready")
        rden_ready, lin_ready = sem("rden_ready"), sem("lin_ready")
        state_parts, state_masked, state_ready = sem("state_parts"), sem("state_masked"), sem("state_ready")
        lin_transposed, linT_ready, lin_projected = sem("lin_transposed"), sem("linT_ready"), sem("lin_projected")
        x3_ready = sem("x3_ready")
        psum_inv = sem("psum_inv")

        WEIGHTS = [(ident, d["ident"]), (wqkv, d["wqkv"]), (conv, d["conv"]), (wbeta, d["wbeta"]),
                   (ones_block, d["ones_block"]), (wo_a, d["wo_a"]), (onorm, d["onorm"]), (wg, d["wg"]),
                   (lower, d["lower"]), (w1, d["w1"]), (w2, d["w2"]), (causal, d["causal"]),
                   (state_mask, d["state_mask"]), (head_mask, d["head_mask"]), (wqk_b, d["wqk_b"]),
                   (wv_b, d["wv_b"]), (wo_b, d["wo_b"]), (bo_row, d["bo_row"])]
        ALL_W = 16 * len(WEIGHTS)

        block = ctx.enter_context(nc.Block())

        @block.sync
        def _(sp):
            def load_x(c):
                taken = held(sp, J * c)
                sp.wait_ge(go, 1)
                if due(taken):
                    sp.wait_ge(xn_ready, taken)
                sp.dma_start(x_in[:].rearrange("p j d -> p (j d)"), d["x"][c]).then_inc(x_loaded, 16)

            def pairs(c):
                one, two, three = held(sp, c + 1), held(sp, 2 * (c + 1)), held(sp, 3 * (c + 1))
                read, stored, taken = held(sp, 16 * 4 * c), held(sp, 16 * 4 * (c + 1)), held(sp, 5 * c)
                sp.wait_ge(go, 1)
                sp.wait_ge(qk_ready, two)
                sp.wait_ge(silu_ready, three)
                sp.wait_ge(beta_ready, one)
                if due(read):
                    sp.wait_ge(pairs_loaded, read)
                for z in range(3):
                    sp.dma_start(s_qkv[z].rearrange("b p t -> p b t"),
                                 qkv[:, z, :].rearrange("p (b t) -> p b t", b=B)).then_inc(qkv_stored, 16)
                sp.dma_start(s_beta.rearrange("b h t -> h b t"),
                             beta_T[:].rearrange("h (b t) -> h b t", b=B)).then_inc(qkv_stored, 16)
                sp.wait_ge(go, 1)
                sp.wait_ge(qkv_stored, stored)
                if due(taken):
                    sp.wait_ge(pairs_taken, taken)
                for z in range(3):
                    sp.dma_start(pin[:, z].rearrange("p d t -> p (d t)"),
                                 s_qkv[z].rearrange("b (h d) t -> (b h) (d t)", h=H)).then_inc(pairs_loaded, 16)
                sp.dma_start(beta_p[:], s_beta.rearrange("b h t -> (b h) t")).then_inc(pairs_loaded, 16)

            def heads_out(c):
                last, this, stored = held(sp, c), held(sp, c + 1), held(sp, 16 * (c + 1))
                sp.wait_ge(go, 1)
                sp.wait_ge(o_ready, this)
                sp.dma_start(s_o.rearrange("b h m t -> (b h) (m t)"),
                             o_p[:].rearrange("p m t -> p (m t)")).then_inc(o_stored, 16)
                sp.wait_ge(go, 1)
                if due(last):
                    sp.wait_ge(x1_ready, last)
                sp.dma_start(x_r[:].rearrange("p j d -> p (j d)"), d["x"][c]).then_inc(xr_loaded, 16)
                sp.wait_ge(go, 1)
                sp.wait_ge(o_stored, stored)
                if due(last):
                    sp.wait_ge(on_ready, last)
                sp.dma_start(o_T[:].rearrange("p (b t) -> p b t", b=B),
                             s_o.rearrange("b h m t -> (h m) b t")).then_inc(o_loaded, 16)

            def store_mid(c):
                this = held(sp, c + 1)
                sp.wait_ge(go, 1)
                sp.wait_ge(x2_ready, this)
                sp.dma_start(s_x[c], x2[:].rearrange("p j d -> p (j d)")).then_inc(x2_stored, 16)

            def load_mid(c):
                last, stored = held(sp, c), held(sp, 16 * (c + 1))
                sp.wait_ge(go, 1)
                sp.wait_ge(x2_stored, stored)
                if due(last):
                    sp.wait_ge(x3_ready, last)
                sp.dma_start(x_b[:].rearrange("p j d -> p (j d)"), s_x[c]).then_inc(xb_loaded, 16)

            def store_out(c):
                this = held(sp, NCH + c + 1)
                sp.wait_ge(go, 1)
                sp.wait_ge(x2_ready, this)
                sp.dma_start(out[c], x2[:].rearrange("p j d -> p (j d)")).then_inc(x2_stored, 16)

            load_x(0)
            for dst, src in WEIGHTS:
                sp.dma_start(dst[:], src).then_inc(w_loaded, 16)
            load_x(1)
            pairs(0)
            load_x(2)
            pairs(1)
            heads_out(0)
            load_x(3)
            pairs(2)
            store_mid(0)
            with sp.Fori(2, NCH - 2) as i:
                heads_out(i - 1)
                load_x(i + 2)
                pairs(i + 1)
                store_mid(i - 1)
            heads_out(NCH - 3)
            pairs(NCH - 1)
            store_mid(NCH - 3)
            heads_out(NCH - 2)
            store_mid(NCH - 2)
            heads_out(NCH - 1)
            store_mid(NCH - 1)
            load_mid(0)
            load_mid(1)
            with sp.Fori(1, NCH - 1) as i:
                store_out(i - 1)
                load_mid(i + 1)
            store_out(NCH - 2)
            store_out(NCH - 1)
            sp.wait_ge(x2_stored, 16 * 2 * NCH)

        @block.gpsimd
        def _(pool):
            nc.gpsimd.memset(one_col[:], 1.0).then_inc(go, 1)
            nc.gpsimd.memset(xnT[:, :, 0:KC - 1], 0.0).then_inc(pool_ready, 1)
            nc.gpsimd.memset(eps_ln[:], LN_EPS).then_inc(pool_ready, 1)
            nc.gpsimd.memset(eps_on[:], DELTA_EPS).then_inc(pool_ready, 1)
            nc.gpsimd.memset(ones_row[:], 1.0).then_inc(pool_ready, 1)
            nc.gpsimd.memset(state[:].rearrange("p b h e -> p (b h e)"), 0.0).then_inc(pool_ready, 1)
            nc.gpsimd.memset(v_bd[:].rearrange("p b n r e -> p (b n r e)"), 0.0).then_inc(pool_ready, 1)
            pool.wait_ge(pool_ready, 6)
            for par in range(2):
                nc.gpsimd.memset(v_bd[64 * par:64 * par + 64, :, :, par, HD], 1.0).then_inc(pool_ready, 1)

        POOL_ALL = 8

        @block.scalar
        def _(act):
            def prep_rstd(c):
                act.wait_ge(mv_ready, J * (c + 1))
                nc.scalar.activation(rstd[:], mv[:, :, 1], ACT.Ln, bias=eps_ln[:]).then_inc(rstd_log, 1)
                act.wait_ge(rstd_log, c + 1)
                nc.scalar.activation(rstd[:], rstd[:], ACT.Exp, scale=-0.5).then_inc(rstd_ready, 1)

            def prep_xnT(c, first=False):
                act.wait_ge(xn_transposed, c + 1)
                if due(4 * c):
                    act.wait_ge(projected, 4 * c)
                if not first:
                    nc.scalar.copy(xnT[:, :, 0:KC - 1], xnT[:, :, CH:CH + KC - 1]).then_inc(halo_kept, 1)
                    if due(c):
                        act.wait_ge(halo_kept, c)
                nc.scalar.copy(xnT[:, :, KC - 1:], bank[:, TB, :].rearrange("p (b t) -> p b t", b=B)
                               ).then_inc(xnT_ready, 1)

            def prep_sigmoid(c, z):
                src = bank[:, (QB, KB, QB)[z], :]
                act.wait_ge(projected, 4 * c + z + 1)
                nc.scalar.activation(sig[:, z], src, ACT.Exp, scale=-1.0).then_inc(sig_exp, 1)
                act.wait_ge(sig_exp, 3 * c + z + 1)
                nc.scalar.activation(sig[:, z], sig[:, z], ACT.Ln, bias=one_col[:]).then_inc(sig_log, 1)
                act.wait_ge(sig_log, 3 * c + z + 1)
                nc.scalar.activation(sig[:, z], sig[:, z], ACT.Exp, scale=-1.0).then_inc(sig_ready, 1)

            def prep_beta(c):
                act.wait_ge(projected, 4 * c + 4)
                if due(16 * 4 * c):
                    act.wait_ge(qkv_stored, 16 * 4 * c)
                nc.scalar.activation(beta_T[:], bank[0:H, KB, :], ACT.Exp, scale=-1.0).then_inc(beta_exp, 1)
                act.wait_ge(beta_exp, c + 1)
                nc.scalar.activation(beta_T[:], beta_T[:], ACT.Ln, bias=one_col[0:H]).then_inc(beta_log, 1)
                act.wait_ge(beta_log, c + 1)
                nc.scalar.activation(beta_T[:], beta_T[:], ACT.Exp, scale=-1.0).then_inc(beta_ready, 1)

            def prep_square(c):
                act.wait_ge(silu_ready, 3 * c + 2)
                nc.scalar.activation(sq[:], qkv[:, 0:2], ACT.Square).then_inc(squared, 1)

            def prep_norm(c):
                act.wait_ge(norm_max, c + 1)
                nc.scalar.activation(rqk[:], rqk[:], ACT.Ln).then_inc(norm_log, 1)
                act.wait_ge(norm_log, c + 1)
                nc.scalar.activation(rqk[:], rqk[:], ACT.Exp, scale=-0.5).then_inc(norm_ready, 1)

            def out_square(c):
                act.wait_ge(o_loaded, 16 * (c + 1))
                nc.scalar.activation(osq[:], o_T[:], ACT.Square).then_inc(o_squared, 1)

            def out_norm(c):
                act.wait_ge(o_norms, c + 1)
                nc.scalar.activation(orn[:], bank[:, MB, :], ACT.Ln, bias=eps_on[:], scale=1.0 / HD).then_inc(o_log, 1)
                act.wait_ge(o_log, c + 1)
                nc.scalar.activation(orn[:], orn[:], ACT.Exp, scale=-0.5).then_inc(o_rnorm, 1)

            def moe_rstd(n):
                act.wait_ge(mvf_ready, J * (n + 1))
                nc.scalar.activation(rstdf[:], mvf[:, :, 1], ACT.Ln, bias=eps_ln[:]).then_inc(rstdf_log, 1)
                act.wait_ge(rstdf_log, n + 1)
                nc.scalar.activation(rstdf[:], rstdf[:], ACT.Exp, scale=-0.5).then_inc(rstdf_ready, 1)

            def moe_xfT(n):
                act.wait_ge(xf_transposed, n + 1)
                nc.scalar.copy(xfT[:], bank[:, MB, :]).then_inc(xfT_ready, 1)

            def moe_exp(n):
                act.wait_ge(lsub_ready, n + 1)
                nc.scalar.activation(pexp[:].rearrange("p j e -> p (j e)"), lsub[:].rearrange("p j e -> p (j e)"),
                                     ACT.Exp).then_inc(pexp_ready, 1)

            def moe_scale(n, e):
                if e == 0:
                    act.wait_ge(gate_ready, n + 1)
                if due(E * (n - 1) + e + 1):
                    act.wait_ge(xe_transposed, E * (n - 1) + e + 1)
                for j in range(J):
                    last = nc.scalar.activation(xe[:, e, j], xf[:, j], ACT.Copy, scale=gate[:, j, e:e + 1])
                last.then_inc(xe_ready, 1)

            def moe_xeT(n, e):
                act.wait_ge(xe_transposed, E * n + e + 1)
                if due(FC * (E * n + e - 1)):
                    act.wait_ge(z_ready, FC * (E * n + e - 1))
                nc.scalar.copy(xeT[:, e % 2], bank[:, XB, :]).then_inc(xeT_ready, 1)

            def moe_relu(n, e):
                if due(E * n + e - 1):
                    act.wait_ge(y_part, E * n + e - 1)
                for f in range(FC):
                    act.wait_ge(z_ready, FC * (E * n + e) + f + 1)
                    nc.scalar.activation(hid[:, e % 2, f], bank[:, ZB + f, :], ACT.Relu).then_inc(hid_ready, 1)

            def moe_start(n):
                moe_scale(n, 0)
                moe_scale(n, 1)
                moe_xeT(n, 0)

            def moe_expert(n, e):
                if e + 2 < E:
                    moe_scale(n, e + 2)
                moe_relu(n, e)
                if e + 1 < E:
                    moe_xeT(n, e + 1)

            def moe_end(n):
                act.wait_ge(y_part, E * (n + 1))
                nc.scalar.copy(yT[:], bank[:, YB, :]).then_inc(yT_ready, 1)

            def prep(c, first=False):
                prep_rstd(c)
                prep_xnT(c, first)
                for z in range(3):
                    prep_sigmoid(c, z)
                prep_beta(c)
                prep_square(c)
                prep_norm(c)

            def out_moe(c):
                out_square(c)
                out_norm(c)
                moe_rstd(c)
                moe_xfT(c)
                moe_exp(c)
                moe_start(c)
                for e in range(E):
                    moe_expert(c, e)
                moe_end(c)

            def both(i):
                c, n = i + 1, i - 1
                prep_rstd(c)
                prep_xnT(c)
                out_square(n)
                prep_sigmoid(c, 0)
                out_norm(n)
                prep_sigmoid(c, 1)
                moe_rstd(n)
                prep_sigmoid(c, 2)
                moe_xfT(n)
                prep_beta(c)
                prep_square(c)
                moe_exp(n)
                prep_norm(c)
                moe_start(n)
                for e in range(E):
                    moe_expert(n, e)
                moe_end(n)

            def lin_xT(c):
                act.wait_ge(xn_transposed, NCH + c + 1)
                if due(c):
                    act.wait_ge(v_projected, c)
                nc.scalar.copy(linT, bank[:, TB, :]).then_inc(xnT_ready, 1)

            def lin_exp(c):
                act.wait_ge(phi_low, c + 1)
                nc.scalar.activation(phi_min[:], phi_min[:], ACT.Exp).then_inc(phi_exp, 1)

            def lin_v(c):
                act.wait_ge(v_projected, c + 1)
                if due(c):
                    act.wait_ge(state_parts, c)
                for par in range(2):
                    h = slice(64 * par, 64 * par + 64)
                    nc.scalar.copy(v_bd[h, :, :, par, 0:HD], bank[h, MB, :].rearrange(
                        "p (b n e) -> p b n e", b=B, n=NP)).then_inc(v_ready, 1)

            def lin_ktok(c):
                for half in range(2):
                    act.wait_ge(k_transposed, 2 * c + half + 1)
                    if half == 0:
                        if due(c):
                            act.wait_ge(state_parts, c)
                    nc.scalar.copy(k_tok[:, 4 * half:4 * half + 4], bank[:, (TB, MB)[half], :].rearrange(
                        "p (b f) -> p b f", b=4)).then_inc(ktok_ready, 1)

            def lin_outT(c):
                act.wait_ge(lin_transposed, c + 1)
                nc.scalar.copy(yT[:], bank[:, MB, :]).then_inc(linT_ready, 1)

            act.wait_ge(go, 1)
            act.wait_ge(pool_ready, POOL_ALL)
            prep(0, first=True)
            prep(1)
            both(1)
            with act.Fori(2, NCH - 1) as i:
                both(i)
            out_moe(NCH - 2)
            out_moe(NCH - 1)

            def lin_pre(c):
                prep_rstd(NCH + c)
                lin_xT(c)

            def lin_all(c):
                lin_exp(c)
                lin_v(c)
                lin_ktok(c)
                lin_outT(c)
                moe_rstd(NCH + c)
                moe_xfT(NCH + c)
                moe_exp(NCH + c)

            def step2(i, last=False):
                n = NCH + i - 1
                moe_start(n)
                moe_expert(n, 0)
                if not last:
                    lin_exp(i)
                    lin_v(i)
                moe_expert(n, 1)
                if not last:
                    lin_ktok(i)
                for e in range(2, 5):
                    moe_expert(n, e)
                if not last:
                    lin_outT(i)
                moe_expert(n, 5)
                if not last:
                    moe_rstd(n + 1)
                moe_expert(n, 6)
                if not last:
                    moe_xfT(n + 1)
                moe_expert(n, 7)
                moe_end(n)
                if not last:
                    moe_exp(n + 1)

            lin_pre(0)
            lin_all(0)
            lin_pre(1)
            with act.Fori(1, NCH - 1) as i:
                step2(i)
                lin_pre(i + 1)
            step2(NCH - 1)
            step2(NCH, last=True)

        @block.tensor
        def _(pe):
            def prep_transpose(c):
                pe.wait_ge(xn_ready, J * (c + 1))
                if due(c):
                    pe.wait_ge(xnT_ready, c)
                for j in range(J):
                    last = nc.tensor.transpose(bank[:, TB, 128 * j:128 * j + 128], xn[:, j], ident[:])
                last.then_inc(xn_transposed, 1)

            def prep_project(c, z):
                if z == 0:
                    pe.wait_ge(xnT_ready, c + 1)
                if z < 2:
                    if due(c):
                        pe.wait_ge(norm_max, c)
                else:
                    pe.wait_ge(silu_ready, 3 * c + 1)
                for k in range(KC):
                    last = nc.tensor.matmul(bank[:, (QB, KB, QB)[z], :], wtap[:, z, k], xnT[:, :, k:k + CH],
                                            start=(k == 0), stop=(k == KC - 1))
                last.then_inc(projected, 1)

            def prep_beta(c):
                pe.wait_ge(silu_ready, 3 * c + 2)
                nc.tensor.matmul(bank[0:H, KB, :], wbeta[:], xnT[:, :, KC - 1:], start=True, stop=True
                                 ).then_inc(projected, 1)

            def prep_norms(c):
                pe.wait_ge(squared, c + 1)
                pe.wait_ge(silu_ready, 3 * c + 3)
                pe.wait_ge(beta_exp, c + 1)
                for z in range(2):
                    last = nc.tensor.matmul(bank[:, QB + z, :], ones_block[:], sq[:, z], start=True, stop=True)
                last.then_inc(norms, 1)

            def out_norms(c):
                pe.wait_ge(o_squared, c + 1)
                if due(c):
                    pe.wait_ge(routed, c)
                if due(c):
                    pe.wait_ge(lsub_ready, c)
                nc.tensor.matmul(bank[:, MB, :], ones_block[:], osq[:], start=True, stop=True).then_inc(o_norms, 1)

            def out_project(c):
                pe.wait_ge(on_ready, c + 1)
                for j in range(J):
                    last = nc.tensor.matmul(bank[:, MB, 128 * j:128 * j + 128], on[:, 128 * j:128 * j + 128], wo_n[:],
                                            start=True, stop=True)
                last.then_inc(o_projected, 1)

            def moe_transpose(n):
                pe.wait_ge(xf_ready, J * (n + 1))
                for j in range(J):
                    last = nc.tensor.transpose(bank[:, MB, 128 * j:128 * j + 128], xf[:, j], ident[:])
                last.then_inc(xf_transposed, 1)

            def moe_route(n):
                pe.wait_ge(xfT_ready, n + 1)
                for j in range(J):
                    last = nc.tensor.matmul(bank[:, MB, E * j:E * j + E], xfT[:, 128 * j:128 * j + 128], wg[:],
                                            start=True, stop=True)
                last.then_inc(routed, 1)

            def moe_xe(n, e):
                pe.wait_ge(xe_ready, E * n + e + 1)
                if due(E * n + e):
                    pe.wait_ge(xeT_ready, E * n + e)
                for j in range(J):
                    last = nc.tensor.transpose(bank[:, XB, 128 * j:128 * j + 128], xe[:, e, j], ident[:])
                last.then_inc(xe_transposed, 1)

            def moe_up(n, e):
                pe.wait_ge(xeT_ready, E * n + e + 1)
                for f in range(FC):
                    if due(FC * (E * n + e - 1) + f + 1):
                        pe.wait_ge(hid_ready, FC * (E * n + e - 1) + f + 1)
                    nc.tensor.matmul(bank[:, ZB + f, :], w1[:, e, 128 * f:128 * f + 128], xeT[:, e % 2],
                                     start=True, stop=True).then_inc(z_ready, 1)

            def moe_down(n, e):
                if e == 0:
                    if due(n):
                        pe.wait_ge(x2_ready, n)
                if due(FC * (E * n + e + 1)):
                    pe.wait_ge(hid_ready, FC * (E * n + e + 1))
                for f in range(FC):
                    last = nc.tensor.matmul(bank[:, YB, :], w2[:, e, f], hid[:, e % 2, f],
                                            start=(e == 0 and f == 0), stop=(e == E - 1 and f == FC - 1))
                last.then_inc(y_part, 1)

            def moe_expert(n, e):
                moe_up(n, e)
                if e + 1 < E:
                    moe_xe(n, e + 1)
                if e >= 1:
                    moe_down(n, e - 1)

            def moe_end(n):
                moe_down(n, E - 1)
                pe.wait_ge(yT_ready, n + 1)
                for j in range(J):
                    last = nc.tensor.transpose(bank[:, YB, 128 * j:128 * j + 128], yT[:, 128 * j:128 * j + 128], ident[:])
                last.then_inc(y_transposed, 1)

            def prep(c):
                prep_transpose(c)
                for z in range(3):
                    prep_project(c, z)
                prep_beta(c)
                prep_norms(c)

            def out_moe(c):
                out_norms(c)
                out_project(c)
                moe_transpose(c)
                moe_route(c)
                moe_xe(c, 0)
                for e in range(E):
                    moe_expert(c, e)
                moe_end(c)

            def both(i):
                c, n = i + 1, i - 1
                prep_transpose(c)
                out_norms(n)
                prep_project(c, 0)
                out_project(n)
                prep_project(c, 1)
                moe_transpose(n)
                prep_project(c, 2)
                moe_route(n)
                prep_beta(c)
                prep_norms(c)
                moe_xe(n, 0)
                for e in range(E):
                    moe_expert(n, e)
                moe_end(n)

            pe.wait_ge(w_loaded, ALL_W)
            pe.wait_ge(pool_ready, POOL_ALL)
            pe.wait_ge(taps_ready, 2)
            prep(0)
            prep(1)
            both(1)
            with pe.Fori(2, NCH - 1) as i:
                both(i)
            out_moe(NCH - 2)
            out_moe(NCH - 1)

            def lin_project(c):
                pe.wait_ge(xnT_ready, NCH + c + 1)
                if due(3 * c):
                    pe.wait_ge(state_masked, 3 * c)
                if due(c):
                    pe.wait_ge(x3_ready, c)
                for z in range(2):
                    last = nc.tensor.matmul(bank[:, QB + z, :], wqk_b[:, z], linT, start=True, stop=True)
                last.then_inc(qk_projected, 1)
                for b in range(B):
                    for par in range(2):
                        last = nc.tensor.matmul(bank[64 * par:64 * par + 64, MB, 64 * b:64 * b + 64],
                                                linT[:, CH * b:CH * b + CH], wv_b[:, par], start=True, stop=True)
                last.then_inc(v_projected, 1)

            def lin_ktok(c):
                pe.wait_ge(phi_ready, 3 * (c + 1))
                for half in range(2):
                    if half == 1:
                        pe.wait_ge(v_ready, 2 * (c + 1))
                    for q in range(4):
                        b = 4 * half + q
                        last = nc.tensor.transpose(bank[:, (TB, MB)[half], 128 * q:128 * q + 128],
                                                   phi_k[:, b].rearrange("p r t -> p (r t)"), ident[:])
                    last.then_inc(k_transposed, 1)

            def lin_scores(c, j):
                if j == 0:
                    taken = held(pe, c + 1)
                    pe.wait_ge(go, 1)
                    pe.wait_ge(qbd_ready, taken)
                else:
                    read = held(pe, J * c + j)
                    pe.wait_ge(go, 1)
                    pe.wait_ge(att_ready, read)
                for p in range(2):
                    b = 2 * j + p
                    for par in range(2):
                        for r in range(2):
                            h = slice(64 * r, 64 * r + 64)
                            last = nc.tensor.matmul(
                                bank[64 * par:64 * par + 64, QB + r, 256 * p:256 * p + 256],
                                phi_k[h, b, 0], q_bd[h, par::2, CH * b:CH * b + CH],
                                start=True, stop=True)
                last.then_inc(scores, 1)

            def lin_numer(c, j):
                pe.wait_ge(att_ready, J * c + j + 1)
                if j == 0:
                    pe.wait_ge(v_ready, 2 * (c + 1))
                    pe.wait_ge(ktok_ready, 2 * (c + 1))
                    if due(c):
                        pe.wait_ge(state_ready, c)
                if j >= 2:
                    if due(J * c + j - 1):
                        pe.wait_ge(lin_ready, J * c + j - 1)
                for p in range(2):
                    b = 2 * j + p
                    o = bank[64 * p:64 * p + 64, (TB, MB)[j % 2], 0:H * HV]
                    for r in range(2):
                        for i4 in range(4):
                            n = 4 * r + i4
                            nc.tensor.matmul(o[:, 2 * HV * n:2 * HV * n + 2 * HV], att[:, j % 2, r, p, i4],
                                             v_bd[:, b, n].rearrange("p r e -> p (r e)"), start=(n == 0), stop=False,
                                             skip_group_check=True)
                    last = nc.tensor.matmul(o, phi_q[:, CH * b:CH * b + CH], state[:, b].rearrange("p h e -> p (h e)"),
                                            start=False, stop=True, skip_group_check=True)
                last.then_inc(numer, 1)

            def lin_state(c):
                pe.wait_ge(lin_ready, J * (c + 1))
                for b in range(B):
                    o = bank[:, b // 3, H * HV * (b % 3):H * HV * (b % 3) + H * HV]
                    last = nc.tensor.matmul(o, k_tok[:, b], v_bd[:, b].rearrange("p n r e -> p (n r e)"),
                                            start=True, stop=True)
                last.then_inc(state_parts, 1)

            def lin_transpose(c):
                for j in range(J):
                    last = nc.tensor.transpose(bank[:, MB, 128 * j:128 * j + 128], lin[:, j], ident[:])
                last.then_inc(lin_transposed, 1)

            def lin_project_out(c):
                pe.wait_ge(linT_ready, c + 1)
                for j in range(J):
                    o = bank[:, MB, 128 * j:128 * j + 128]
                    nc.tensor.matmul(o, ones_row[:], bo_row[:], start=True, stop=False)
                    last = nc.tensor.matmul(o, yT[:, 128 * j:128 * j + 128], wo_b[:], start=False, stop=True)
                last.then_inc(lin_projected, 1)

            def lin_pre(c):
                prep_transpose(NCH + c)

            def lin_all(c):
                lin_project(c)
                lin_ktok(c)
                lin_scores(c, 0)
                for j in range(J):
                    if j + 1 < J:
                        lin_scores(c, j + 1)
                    lin_numer(c, j)
                lin_state(c)
                lin_transpose(c)
                lin_project_out(c)
                moe_transpose(NCH + c)
                moe_route(NCH + c)

            def step2(i, last=False):
                n = NCH + i - 1
                moe_xe(n, 0)
                moe_expert(n, 0)
                if not last:
                    lin_project(i)
                moe_expert(n, 1)
                if not last:
                    lin_ktok(i)
                    lin_scores(i, 0)
                moe_expert(n, 2)
                if not last:
                    lin_scores(i, 1)
                    lin_numer(i, 0)
                    lin_scores(i, 2)
                moe_expert(n, 3)
                if not last:
                    lin_numer(i, 1)
                    lin_scores(i, 3)
                    lin_numer(i, 2)
                moe_expert(n, 4)
                if not last:
                    lin_numer(i, 3)
                    lin_state(i)
                    lin_transpose(i)
                moe_expert(n, 5)
                if not last:
                    lin_project_out(i)
                moe_expert(n, 6)
                if not last:
                    moe_transpose(n + 1)
                moe_expert(n, 7)
                moe_end(n)
                if not last:
                    moe_route(n + 1)

            lin_pre(0)
            lin_all(0)
            lin_pre(1)
            with pe.Fori(1, NCH - 1) as i:
                step2(i)
                lin_pre(i + 1)
            step2(NCH - 1)
            step2(NCH, last=True)

        @block.vector
        def _(dve):
            tt, ts, stt, red = (nc.vector.tensor_tensor, nc.vector.tensor_scalar, nc.vector.scalar_tensor_tensor,
                                nc.vector.tensor_reduce)

            def stats(src, b6, out_mv, bn_done, mv_ready, c):
                for j in range(J):
                    nc.vector.bn_stats(b6[:, j], src[:, j]).then_inc(bn_done, 1)
                done = held(dve, J * (c + 1))
                dve.wait_ge(go, 1)
                dve.wait_ge(bn_done, done)
                for j in range(J):
                    nc.vector.bn_aggr(out_mv[:, j], b6[:, j]).then_inc(mv_ready, 1)

            def normed(dst, src, mvt, r, done):
                for j in range(J):
                    ts(dst[:, j], src[:, j], mvt[:, j, 0:1], r[:, j:j + 1], ALU.subtract, ALU.mult).then_inc(done, 1)

            def prep_stats(c):
                dve.wait_ge(x_loaded, 16 * (c + 1))
                stats(x_in, bn6, mv, bn_done, mv_ready, c)

            def prep_xn(c):
                dve.wait_ge(rstd_ready, c + 1)
                if due(c):
                    dve.wait_ge(xn_transposed, c)
                normed(xn, x_in, mv, rstd, xn_ready)

            def prep_silu(c, z):
                dve.wait_ge(sig_ready, 3 * c + z + 1)
                if z == 0:
                    if due(16 * 4 * c):
                        dve.wait_ge(qkv_stored, 16 * 4 * c)
                tt(qkv[:, z], bank[:, (QB, KB, QB)[z], :], sig[:, z], ALU.mult).then_inc(silu_ready, 1)

            def prep_norm_max(c):
                dve.wait_ge(norms, c + 1)
                ts(rqk[:], bank[:, QB:QB + 2, :], DELTA_EPS ** 2, None, ALU.max).then_inc(norm_max, 1)

            def prep_qk(c):
                dve.wait_ge(norm_ready, c + 1)
                stt(qkv[:, 0], qkv[:, 0], QSCALE, rqk[:, 0], ALU.mult, ALU.mult).then_inc(qk_ready, 1)
                tt(qkv[:, 1], qkv[:, 1], rqk[:, 1], ALU.mult).then_inc(qk_ready, 1)

            def delta_pre(c, first=False):
                dve.wait_ge(pairs_loaded, 16 * 4 * (c + 1))
                nc.vector.tensor_copy(q_p[:], pin[:, 0]).then_inc(pairs_taken, 1)
                nc.vector.tensor_copy(k_p[:], pin[:, 1]).then_inc(pairs_taken, 1)
                stt(nkb[:], pin[:, 1], -1.0, bc(beta_p[:], 1, HD), ALU.mult, ALU.mult).then_inc(pairs_taken, 1)
                tt(prod[:, :, :, HD].rearrange("p t m -> p m t"), pin[:, 2], bc(beta_p[:], 1, HD), ALU.mult
                   ).then_inc(pairs_taken, 1)
                if first:
                    nc.vector.memset(hist[:, 0, :, :, 2], 0.0).then_inc(pairs_taken, 1)
                else:
                    nc.vector.tensor_copy(hist[:, 0, :, :, 2], hist[:, NB, :, :, 2]).then_inc(pairs_taken, 1)
                dve.wait_ge(pairs_taken, 5 * c + 3)
                tt(dots[:, 0], nkb[:, :, 1::2].rearrange("p d n -> p n d"), k_p[:, :, 0::2].rearrange("p d n -> p n d"),
                   ALU.mult).then_inc(dot_ready, 1)
                tt(dots[:, 1], q_p[:, :, 0::2].rearrange("p d n -> p n d"), k_p[:, :, 1::2].rearrange("p d n -> p n d"),
                   ALU.mult).then_inc(dot_ready, 1)
                dve.wait_ge(dot_ready, 2 * c + 1)
                red(ng[:], dots[:, 0], AX_X, ALU.add).then_inc(scal_ready, 1)
                dve.wait_ge(dot_ready, 2 * c + 2)
                red(nqk[:], dots[:, 1], AX_X, ALU.add, negate=True).then_inc(scal_ready, 1)
                dve.wait_ge(pairs_taken, 5 * (c + 1))
                dve.wait_ge(scal_ready, 2 * (c + 1))

            def delta_block(c, n):
                at = 5 * (NB * c + n)
                s_in = hist[:, n, :, :, 2]
                if n:
                    if due(at):
                        dve.wait_ge(step, at)
                t = slice(2 * n, 2 * n + 2)
                tt(prod[:, t, :, 0:HD], bc(s_in, 1, 2), bc(nkb[:, :, t].rearrange("p d t -> p t d"), 2, HD), ALU.mult
                   ).then_inc(step, 1)
                dve.wait_ge(step, at + 1)
                red(u[:, n], prod[:, t], AX_X, ALU.add).then_inc(step, 1)
                dve.wait_ge(step, at + 2)
                stt(u[:, n, 1], u[:, n, 0], ng[:, n:n + 1], u[:, n, 1], ALU.mult, ALU.add).then_inc(step, 1)
                dve.wait_ge(step, at + 3)
                tt(hist[:, n, :, :, 0:2].rearrange("p m d s -> p s m d"), bc(u[:, n], 3, HD),
                   bc(k_p[:, :, t].rearrange("p d t -> p t d"), 2, HD), ALU.mult).then_inc(step, 1)
                dve.wait_ge(step, at + 4)
                red(hist[:, n + 1, :, :, 2], hist[:, n], AX_X, ALU.add).then_inc(step, 1)

            def delta_out(c):
                dve.wait_ge(step, 5 * NB * (c + 1))
                if due(16 * c):
                    dve.wait_ge(o_stored, 16 * c)
                for s in range(2):
                    if s:
                        dve.wait_ge(o_part, 5 * c + 3)
                    tt(oq, hist[:, 1:, :, :, 2], bc(q_p[:, :, s::2].rearrange("p d n -> p n d"), 2, HD), ALU.mult
                       ).then_inc(o_part, 1)
                    if s == 0:
                        tt(ofix[:], u[:, :, 1], bc(nqk[:], 2, HD), ALU.mult).then_inc(o_part, 1)
                    dve.wait_ge(o_part, 5 * c + (1, 4)[s])
                    red(o_p[:, :, s::2].rearrange("p m n -> p n m"), oq, AX_X, ALU.add).then_inc(o_part, 1)
                dve.wait_ge(o_part, 5 * (c + 1))
                o0 = o_p[:, :, 0::2].rearrange("p m n -> p n m")
                tt(o0, o0, ofix[:], ALU.add).then_inc(o_ready, 1)

            def out_on(c):
                dve.wait_ge(o_rnorm, c + 1)
                tt(on[:], o_T[:], orn[:], ALU.mult).then_inc(on_ready, 1)

            def out_residual(c):
                dve.wait_ge(o_projected, c + 1)
                dve.wait_ge(xr_loaded, 16 * (c + 1))
                tt(x1[:], x_r[:], bank[:, MB, :].rearrange("p (j d) -> p j d", j=J), ALU.add).then_inc(x1_ready, 1)
                dve.wait_ge(x1_ready, c + 1)
                stats(x1, bn6f, mvf, bnf_done, mvf_ready, c)

            def moe_xn(n, src):
                dve.wait_ge(rstdf_ready, n + 1)
                if due(E * n):
                    dve.wait_ge(xe_ready, E * n)
                normed(xf, src, mvf, rstdf, xf_ready)

            def moe_rank(n):
                dve.wait_ge(routed, n + 1)
                lp = bank[:, MB, 0:J * E].rearrange("p (j e) -> p j e", j=J)
                nc.vector.tensor_copy(logit[:], lp).then_inc(route, 1)
                red(lmax[:], lp, AX_X, ALU.max).then_inc(route, 1)
                dve.wait_ge(route, 9 * n + 2)
                tt(lsub[:], logit[:], bc(lmax[:], 2, E), ALU.subtract).then_inc(lsub_ready, 1)
                other, own = bc(logit[:], 2, E), bc(logit[:], 3, E)
                tt(above[:], other, own, ALU.is_gt).then_inc(route, 1)
                tt(same[:], other, own, ALU.is_equal).then_inc(route, 1)
                dve.wait_ge(route, 9 * n + 4)
                tt(same[:], same[:], bc(lower[:], 1, J), ALU.mult).then_inc(route, 1)
                dve.wait_ge(route, 9 * n + 5)
                tt(above[:], above[:], same[:], ALU.add).then_inc(route, 1)
                dve.wait_ge(route, 9 * n + 6)
                red(rank[:], above[:], AX_X, ALU.add).then_inc(route, 1)

            def moe_gate(n):
                dve.wait_ge(pexp_ready, n + 1)
                dve.wait_ge(route, 9 * n + 7)
                stt(pick[:], rank[:], 1.5, pexp[:], ALU.is_lt, ALU.mult).then_inc(route, 1)
                dve.wait_ge(route, 9 * n + 8)
                red(psum[:], pick[:], AX_X, ALU.add).then_inc(route, 1)
                dve.wait_ge(route, 9 * n + 9)
                nc.vector.reciprocal(rsum[:], psum[:]).then_inc(psum_inv, 1)
                dve.wait_ge(psum_inv, n + 1)
                if due(E * n):
                    dve.wait_ge(xe_ready, E * n)
                tt(gate[:], pick[:], bc(rsum[:], 2, E), ALU.mult).then_inc(gate_ready, 1)

            def moe_residual(n, stored):
                dve.wait_ge(y_transposed, n + 1)
                if due(stored):
                    dve.wait_ge(x2_stored, stored)
                tt(x2[:], x1[:], bank[:, YB, :].rearrange("p (j d) -> p j d", j=J), ALU.add).then_inc(x2_ready, 1)

            dve.wait_ge(w_loaded, ALL_W)
            tt(wtap[:], bc(wqkv[:], 2, KC), conv[:], ALU.mult).then_inc(taps_ready, 1)
            ts(wo_n[:], wo_a[:], onorm[:], None, ALU.mult).then_inc(taps_ready, 1)
            dve.wait_ge(pool_ready, POOL_ALL)

            def prep_all(c):
                prep_stats(c)
                prep_xn(c)
                for z in range(3):
                    prep_silu(c, z)
                prep_norm_max(c)
                prep_qk(c)

            def step1(i, prep=True, moe=True, first=False):
                c, n = i + 1, i - 1
                delta_pre(i, first)
                for blk in range(NB):
                    delta_block(i, blk)
                    if prep:
                        if blk == 0:
                            prep_stats(c)
                        elif blk == 1:
                            prep_xn(c)
                        elif blk in (5, 7, 10):
                            prep_silu(c, (5, 7, 10).index(blk))
                        elif blk == 13:
                            prep_norm_max(c)
                        elif blk == 15:
                            prep_qk(c)
                    if moe:
                        if blk == 4:
                            out_on(n)
                        elif blk == 6:
                            out_residual(n)
                        elif blk == 8:
                            moe_xn(n, x1)
                        elif blk == 11:
                            moe_rank(n)
                        elif blk == 12:
                            moe_gate(n)
                delta_out(i)
                if moe:
                    moe_residual(n, 16 * n)

            prep_all(0)
            step1(0, moe=False, first=True)
            step1(1)
            with dve.Fori(2, NCH - 1) as i:
                step1(i)
            step1(NCH - 1, prep=False)
            n = NCH - 1
            out_on(n)
            out_residual(n)
            moe_xn(n, x1)
            moe_rank(n)
            moe_gate(n)
            moe_residual(n, 16 * n)

            def lin_pre(c):
                dve.wait_ge(xb_loaded, 16 * (c + 1))
                stats(x_b, bn6, mv, bn_done, mv_ready, NCH + c)

            def lin_xn(c):
                dve.wait_ge(rstd_ready, NCH + c + 1)
                if due(NCH + c):
                    dve.wait_ge(xn_transposed, NCH + c)
                normed(xn, x_b, mv, rstd, xn_ready)

            def lin_phi(c):
                dve.wait_ge(qk_projected, c + 1)
                ts(phi_min[:], bank[:, QB:QB + 2, :], 0.0, None, ALU.min).then_inc(phi_low, 1)
                dve.wait_ge(phi_exp, c + 1)
                stt(phi_q[:], bank[:, QB, :], 0.0, phi_min[:, 0], ALU.max, ALU.add).then_inc(phi_ready, 1)
                for r in range(2):
                    stt(phi_k[:, :, r], bank[:, KB, :].rearrange("p (b t) -> p b t", b=B), 0.0,
                        phi_min[:, 1].rearrange("p (b t) -> p b t", b=B), ALU.max, ALU.add).then_inc(phi_ready, 1)
                dve.wait_ge(phi_ready, 3 * c + 1)
                for h in range(HD):
                    last = ts(q_bd[:, h], phi_q[:], head_mask[:, h:h + 1], None, ALU.mult)
                last.then_inc(qbd_ready, 1)

            def lin_att(c, j):
                dve.wait_ge(scores, J * c + j + 1)
                if due(J * c + j - 1):
                    dve.wait_ge(numer, J * c + j - 1)
                tt(att[:, j % 2].rearrange("p r b i t -> p (r b i) t"),
                   bank[:, QB:QB + 2, :].rearrange("p r (n t) -> p (r n) t", t=CH),
                   bc(causal[:], 1, 16), ALU.mult).then_inc(att_ready, 1)

            def lin_out(c, j):
                dve.wait_ge(numer, J * c + j + 1)
                src = bank[:, (TB, MB)[j % 2], 0:H * HV].rearrange("p (h e) -> p h e", h=H)
                ts(den[:, j], src[:, :, HD], LIN_EPS, None, ALU.add).then_inc(den_ready, 1)
                dve.wait_ge(den_ready, J * c + j + 1)
                nc.vector.reciprocal(rden[:, j], den[:, j]).then_inc(rden_ready, 1)
                dve.wait_ge(rden_ready, J * c + j + 1)
                tt(lin[:, j].rearrange("p (h e) -> p h e", h=H), src[:, :, 0:HD], bc(rden[:, j], 2, HD), ALU.mult
                   ).then_inc(lin_ready, 1)

            def lin_state(c):
                dve.wait_ge(state_parts, c + 1)
                for k in range(3):
                    nb = min(3, B - 3 * k)
                    tt(dstate[:, 3 * k:3 * k + nb].rearrange("p b h e -> p b (h e)"),
                       bank[:, k, 0:nb * H * HV].rearrange("p (b f) -> p b f", b=nb),
                       bc(state_mask[:].rearrange("p h e -> p (h e)"), 1, nb), ALU.mult).then_inc(state_masked, 1)
                dve.wait_ge(state_masked, 3 * (c + 1))
                tt(state[:], state[:], dstate, ALU.add).then_inc(state_ready, 1)

            def lin_residual(c):
                dve.wait_ge(lin_projected, c + 1)
                tt(x3, x_b[:], bank[:, MB, :].rearrange("p (j d) -> p j d", j=J), ALU.add).then_inc(x3_ready, 1)
                dve.wait_ge(x3_ready, c + 1)
                stats(x3, bn6f, mvf, bnf_done, mvf_ready, NCH + c)

            def lin_all(c):
                lin_phi(c)
                for j in range(J):
                    lin_att(c, j)
                    if j:
                        lin_out(c, j - 1)
                lin_out(c, J - 1)
                lin_state(c)
                lin_residual(c)
                moe_xn(NCH + c, x3)
                moe_rank(NCH + c)
                moe_gate(NCH + c)

            def take_x1(n):
                if due(n):
                    dve.wait_ge(x2_ready, n)
                nc.vector.tensor_copy(x1[:], x3).then_inc(x1_ready, 1)
                dve.wait_ge(x1_ready, n + 1)

            def step2(i, last=False):
                n = NCH + i - 1
                if not last:
                    lin_phi(i)
                    for j in range(J):
                        lin_att(i, j)
                        if j:
                            lin_out(i, j - 1)
                    lin_out(i, J - 1)
                    lin_state(i)
                    lin_residual(i)
                    moe_xn(n + 1, x3)
                moe_residual(n, 16 * n)
                if not last:
                    take_x1(n + 1)
                    moe_rank(n + 1)
                    moe_gate(n + 1)

            lin_pre(0)
            lin_xn(0)
            lin_all(0)
            take_x1(NCH)
            lin_pre(1)
            lin_xn(1)
            with dve.Fori(1, NCH - 1) as i:
                step2(i)
                lin_pre(i + 1)
                lin_xn(i + 1)
            step2(NCH - 1)
            step2(NCH, last=True)


def kernel(**inputs):
    import numpy as np
    import concourse.bacc as bacc
    from concourse.bass_utils import run_bass_kernel_spmd

    def a(name):
        return np.asarray(inputs["L0_" + name])

    f = np.float32

    def rows(x):
        x = x.reshape(J, 2, NCH, CH, D).transpose(2, 1, 3, 0, 4)
        return np.ascontiguousarray(x.reshape(NCH, 128, J * D))

    p = np.arange(128)
    convs = np.stack([a("attn_a_conv_q").T, a("attn_a_conv_k").T, a("attn_a_conv_v").T])
    arrays = {
        "x": rows(a("attn_a_x")),
        "wqkv": np.stack([a("attn_a_Wq").T, a("attn_a_Wk").T, a("attn_a_Wv").T], axis=1),
        "conv": np.broadcast_to(convs[None], (128, 3, KC, D)),
        "wbeta": a("attn_a_Wb").T,
        "wo_a": a("attn_a_Wo").T,
        "onorm": np.tile(a("attn_a_o_norm_w"), H)[:, None],
        "wqk_b": np.stack([a("attn_b_Wq").T, a("attn_b_Wk").T], axis=1),
        "wv_b": a("attn_b_Wv").T.reshape(D, NP, 2, HD).transpose(0, 2, 1, 3).reshape(D, 2, NP * HD),
        "wo_b": a("attn_b_Wo").T,
        "bo_row": a("attn_b_bo")[None],
        "wg": a("ffn_Wg"),
        "w1": a("ffn_W1").transpose(1, 0, 2),
        "w2": a("ffn_W2").reshape(E, FC, 128, D).transpose(2, 0, 1, 3),
        "ident": np.eye(128, dtype=f),
        "ones_block": (p[:, None] // HD == p[None] // HD).astype(f),
        "causal": (p[:, None] % CH <= np.arange(CH)[None]).astype(f),
        "lower": np.broadcast_to((np.arange(E)[None] < np.arange(E)[:, None]).astype(f), (128, E, E)),
        "state_mask": np.broadcast_to((p[:, None, None] // HD == np.arange(H)[None, :, None]), (128, H, HV)).astype(f),
        "head_mask": (p[:, None] // HD % HD == np.arange(HD)[None]).astype(f),
    }
    arrays = {k: np.ascontiguousarray(v) for k, v in arrays.items()}
    nc = bacc.Bacc("TRN2", target_bir_lowering=False, num_devices=1)
    d = {k: nc.dram_tensor("in_" + k, v.shape, mybir.dt.from_np(v.dtype), kind="ExternalInput").ap()
         for k, v in arrays.items()}
    out = nc.dram_tensor("out_x", (NCH, 128, J * D), F32, kind="ExternalOutput").ap()
    build(nc, d, out)
    r = run_bass_kernel_spmd(nc, [{"in_" + k: v for k, v in arrays.items()}], core_ids=[0])
    y = r.results[0]["out_x"].reshape(NCH, 2, CH, J, D).transpose(3, 1, 0, 2, 4)
    return np.ascontiguousarray(y.reshape(B, L, D))
```

```python
from contextlib import ExitStack

import concourse.bass as bass
from concourse import mybir

F32 = mybir.dt.float32
F32R = mybir.dt.float32r
ALU = mybir.AluOpType
ACT = mybir.ActivationFunctionType
AX_X = mybir.AxisListType.X

B, L, D = 8, 512, 128
H, HD = 16, 8
KC = 4
E, FF = 8, 256
CH = 64
NCH = L // CH
NT = B * CH
J = NT // 128
BS = 4
NB = CH // BS
O_GROUPS = ((0, 8), (8, 13), (13, 16))
PAIRS = BS * (BS - 1) // 2
FC = FF // 128
HV = HD + 1
NP = H // 2
LN_EPS, DELTA_EPS, LIN_EPS = 1e-5, 1e-6, 1e-5
QSCALE = float(HD) ** -0.5


def due(count):
    return not isinstance(count, int) or count > 0


def held(eng, count):
    return count if isinstance(count, int) else eng.snap(eng.to_reg(count))


def bc(ap, axis, n):
    ap = ap.unsqueeze(axis)
    shape = list(ap.shape)
    shape[axis] = n
    return ap.to_broadcast(shape)


def build(nc, d, out):
    with ExitStack() as ctx:
        def sb(name, shape, dtype=F32):
            return ctx.enter_context(nc.sbuf_tensor(name, shape, dtype))

        def sem(name):
            return ctx.enter_context(nc.semaphore(name))

        ident = sb("ident", [128, 128])
        ones_block = sb("ones_block", [128, 128])
        causal = sb("causal", [128, CH])
        lower = sb("lower", [128, E, E])
        state_mask = sb("state_mask", [128, H, HV])
        head_mask = sb("head_mask", [128, HD])
        wqkv = sb("wqkv", [128, 3, D])
        wtap_h = sb("wtap_h", [128, 3 * KC + 1, D], F32R)
        wtap_l = sb("wtap_l", [128, 3 * KC + 1, D], F32R)
        wo_a = sb("wo_a", [128, D])
        onorm = sb("onorm", [128, 1])
        wo_n = sb("wo_n", [128, D])
        wqk_b = sb("wqk_b", [128, 2, D])
        wv_b = sb("wv_b", [128, 2, NP * HD])
        wo_b = sb("wo_b", [128, D])
        bo_row = sb("bo_row", [1, D])
        ones_row = sb("ones_row", [1, 128])
        wg = sb("wg", [128, E])
        w1_h = sb("w1_h", [128, E, FF], F32R)
        w1_l = sb("w1_l", [128, E, FF], F32R)
        w2 = sb("w2", [128, E, FC, D])
        eps_ln = sb("eps_ln", [128, 1])
        eps_on = sb("eps_on", [128, 1])
        eps_l2 = sb("eps_l2", [128, 1])
        neg_l2 = sb("neg_l2", [128, 1])
        one_col = sb("one_col", [128, 1])

        x_in = sb("x_in", [128, J, D])
        bn6 = sb("bn6", [128, J, 6])
        mv = sb("mv", [128, J, 2])
        rstd = sb("rstd", [128, J])
        xn = sb("xn", [128, J, D])
        xnT_h = sb("xnT_h", [128, B, KC - 1 + CH], F32R)
        xnT_l = sb("xnT_l", [128, B, KC - 1 + CH], F32R)
        sig = sb("sig", [128, 3, NT])
        qkv = sb("qkv", [128, 3, NT])
        beta_T = sb("beta_T", [H, NT])
        sq = sb("sq", [128, 2, NT])
        rqk = sb("rqk", [128, 2, NT])
        pin = sb("pin", [128, 2, HD, CH])
        beta_p = sb("beta_p", [128, CH])
        q_p = sb("q_p", [128, HD, CH])
        k_p = sb("k_p", [128, HD, CH])
        wv = sb("wv", [128, 2 * HD, CH])
        kk = sb("kk", [128, HD, PAIRS, NB])
        wv_part = sb("wv_part", [128, 2 * HD, BS - 1, NB])
        nw = sb("nw", [128, HD, CH])
        prod_mem = sb("prod_mem", [128, CH * HD * HV])
        prod = prod_mem[:].rearrange("p (t m e) -> p t m e", t=CH, m=HD)
        wtap = prod_mem[:, 0:(3 * KC + 1) * D].rearrange("p (k f) -> p k f", f=D)
        u = sb("u", [128, NB, BS, HD])
        hist_mem = sb("hist_mem", [128, (NB + 1) * HD * HD * (BS + 1)])
        hist = hist_mem[:].rearrange("p (n m d s) -> p n m d s", n=NB + 1, m=HD, d=HD)
        qk = sb("qk", [128, HD, BS, NB])
        oq_mem = sb("oq_mem", [128, 8 * BS * HD * HD])
        w1 = oq_mem[:, 0:E * FF].rearrange("p (e f) -> p e f", e=E)
        ofix = sb("ofix", [128, BS, NB, HD])
        o_p = sb("o_p", [128, HD, CH])
        o_T = sb("o_T", [128, NT])
        osq = sb("osq", [128, NT])
        orn = sb("orn", [128, NT])
        on = sb("on", [128, NT])
        x_r = sb("x_r", [128, J, D])
        bn6f = sb("bn6f", [128, J, 6])
        mvf = sb("mvf", [128, J, 2])
        rstdf = sb("rstdf", [128, J])
        xf = sb("xf", [128, J, D])
        xfT = sb("xfT", [128, NT])
        logit = sb("logit", [128, J, E])
        lmax = sb("lmax", [128, J])
        lsub = sb("lsub", [128, J, E])
        above = sb("above", [128, J, E, E])
        same = sb("same", [128, J, E, E])
        rank = sb("rank", [128, J, E])
        chosen = sb("chosen", [128, J, E])
        pexp = sb("pexp", [128, J, E])
        pick = sb("pick", [128, J, E])
        psum = sb("psum", [128, J])
        rsum = sb("rsum", [128, J])
        gate = sb("gate", [128, J, E])
        gate_now = sb("gate_now", [128, J, E])
        xT_h = sb("xT_h", [128, NT], F32R)
        xT_l = sb("xT_l", [128, NT], F32R)
        hid = sb("hid", [128, 2, FC, NT])
        x2 = sb("x2", [128, J, D])
        x_b = sb("x_b", [128, J, D])
        x_keep = x_in
        phi_min = sb("phi_min", [128, 2, NT])
        phi_q = sb("phi_q", [128, NT])
        phi_k = sb("phi_k", [128, B, 2, CH])
        q_bd = hist_mem[:, 0:HD * NT].rearrange("p (h t) -> p h t", h=HD)
        v_bd = sb("v_bd", [128, B, NP, 2, HV])
        att_size, ktok_size, state_size = 2 * NP * 2 * CH, B * D, B * H * HV
        att = prod_mem[:, 0:att_size].rearrange("p (k r b i t) -> p k r b i t", k=2, r=2, b=2, i=4)
        k_tok = prod_mem[:, att_size:att_size + ktok_size].rearrange("p (b f) -> p b f", b=B)
        dstate = prod_mem[:, att_size + ktok_size:att_size + ktok_size + state_size].rearrange(
            "p (b h e) -> p b h e", b=B, h=H)
        state = sb("state", [128, B, H, HV])
        den = sb("den", [128, J, H])
        rden = sb("rden", [128, J, H])
        lin = oq_mem[:, 0:NT].rearrange("p (j d) -> p j d", j=J)
        linT = oq_mem[:, NT:2 * NT]
        x3 = oq_mem[:, 2 * NT:3 * NT].rearrange("p (j d) -> p j d", j=J)

        bank = ctx.enter_context(nc.psum_tensor("bank", [128, 8, 512], F32))
        TB, QB, KB, MB, XB, ZB, YB = 0, 1, 2, 3, 4, 5, 7

        s_qkv = nc.dram_tensor("s_qkv", [NCH, 3, B, D, CH], F32, kind="Internal").ap()
        s_beta = nc.dram_tensor("s_beta", [NCH, B, H, CH], F32, kind="Internal").ap()
        s_o = nc.dram_tensor("s_o", [B, H, HD, CH], F32, kind="Internal").ap()
        s_x = nc.dram_tensor("s_x", [NCH, 128, J * D], F32, kind="Internal").ap()

        go, w_loaded, taps_ready = sem("go"), sem("w_loaded"), sem("taps_ready")
        pool_ready = sem("pool_ready")
        x_loaded, bn_done, mv_ready = sem("x_loaded"), sem("bn_done"), sem("mv_ready")
        rstd_log, rstd_ready, xn_ready = sem("rstd_log"), sem("rstd_ready"), sem("xn_ready")
        xn_transposed, xnT_ready, halo_kept = sem("xn_transposed"), sem("xnT_ready"), sem("halo_kept")
        xnT_rest, taps_scaled, prep_loaded = sem("xnT_rest"), sem("taps_scaled"), sem("prep_loaded")
        taps_split, w1_split = sem("taps_split"), sem("w1_split")
        projected, sig_exp, sig_log = sem("projected"), sem("sig_exp"), sem("sig_log")
        sig_ready, beta_exp, beta_log = sem("sig_ready"), sem("beta_exp"), sem("beta_log")
        beta_ready, silu_ready = sem("beta_ready"), sem("silu_ready")
        squared, norms, norm_max = sem("squared"), sem("norms"), sem("norm_max")
        norm_log, norm_ready, qk_ready = sem("norm_log"), sem("norm_ready"), sem("qk_ready")
        qkv_stored, kv_loaded, q_loaded = sem("qkv_stored"), sem("kv_loaded"), sem("q_loaded")
        pre, taken, step, o_part = sem("pre"), sem("taken"), sem("step"), sem("o_part")
        o_stored, o_loaded = sem("o_stored"), sem("o_loaded")
        o_squared, o_norms, o_log = sem("o_squared"), sem("o_norms"), sem("o_log")
        o_rnorm, on_ready, o_projected = sem("o_rnorm"), sem("on_ready"), sem("o_projected")
        xr_loaded = sem("xr_loaded")
        xr_ready, bnf_done, mvf_ready = sem("xr_ready"), sem("bnf_done"), sem("mvf_ready")
        rstdf_log, rstdf_ready, xf_ready = sem("rstdf_log"), sem("rstdf_ready"), sem("xf_ready")
        xf_transposed, xfT_ready, xT_ready, xT_rest = sem("xf_transposed"), sem("xfT_ready"), sem("xT_ready"), sem("xT_rest")
        routed, route, lsub_ready = sem("routed"), sem("route"), sem("lsub_ready")
        pexp_ready, gate_ready, gate_taken = sem("pexp_ready"), sem("gate_ready"), sem("gate_taken")
        z_ready, hid_ready, y_part = sem("z_ready"), sem("hid_ready"), sem("y_part")
        added, x2_stored, kept = sem("added"), sem("x2_stored"), sem("kept")
        xb_loaded, qk_projected, phi_low = sem("xb_loaded"), sem("qk_projected"), sem("phi_low")
        phi_exp, phi_ready, v_projected = sem("phi_exp"), sem("phi_ready"), sem("v_projected")
        v_ready, qbd_ready = sem("v_ready"), sem("qbd_ready")
        k_transposed, ktok_ready, scores = sem("k_transposed"), sem("ktok_ready"), sem("scores")
        att_ready, numer, den_ready = sem("att_ready"), sem("numer"), sem("den_ready")
        rden_ready, lin_ready = sem("rden_ready"), sem("lin_ready")
        state_parts, state_masked, state_ready = sem("state_parts"), sem("state_masked"), sem("state_ready")
        lin_transposed, linT_ready, lin_projected = sem("lin_transposed"), sem("linT_ready"), sem("lin_projected")
        x3_ready = sem("x3_ready")
        psum_inv = sem("psum_inv")

        WEIGHTS = [(ident[:], d["ident"]), (wqkv[:], d["wqkv"]), (wtap[:, 0:3 * KC], d["conv"]), (wtap[:, 3 * KC], d["wbeta"]),
                   (ones_block[:], d["ones_block"]),
                   (w1, d["w1"]), (wo_a[:], d["wo_a"]), (onorm[:], d["onorm"]), (wg[:], d["wg"]),
                   (lower[:], d["lower"]), (w2[:], d["w2"]), (causal[:], d["causal"]),
                   (state_mask[:], d["state_mask"]), (head_mask[:], d["head_mask"]), (wqk_b[:], d["wqk_b"]),
                   (wv_b[:], d["wv_b"]), (wo_b[:], d["wo_b"]), (bo_row[:], d["bo_row"])]
        PREP_W = 5

        POOL_ALL = 11
        TAKES = 4
        FIRST = [i * (BS - 1) - i * (i - 1) // 2 for i in range(BS)]
        PRE_OPS = 2 + (BS - 1) + 3 + 2 * (BS - 1)
        OUT_OPS = 3 + 3 + 13 * len(O_GROUPS)

        block = ctx.enter_context(nc.Block())

        @block.sync
        def _(sp):
            def load_x(c):
                taken = held(sp, J * c)
                sp.wait_ge(go, 1)
                if due(taken):
                    sp.wait_ge(xn_ready, taken)
                sp.dma_start(x_in[:].rearrange("p j d -> p (j d)"), d["x"][c]).then_inc(x_loaded, 16)

            def pairs_out(c):
                one, two, three = held(sp, c + 1), held(sp, 2 * (c + 1)), held(sp, 3 * (c + 1))
                sp.wait_ge(go, 1)
                sp.wait_ge(qk_ready, two)
                sp.wait_ge(silu_ready, three)
                sp.wait_ge(beta_ready, one)
                for z in range(3):
                    sp.dma_start(s_qkv[c, z].rearrange("b p t -> p b t"),
                                 qkv[:, z, :].rearrange("p (b t) -> p b t", b=B)).then_inc(qkv_stored, 16)
                sp.dma_start(s_beta[c].rearrange("b h t -> h b t"),
                             beta_T[:].rearrange("h (b t) -> h b t", b=B)).then_inc(qkv_stored, 16)

            def pairs_in(c):
                stored, last = held(sp, 16 * 4 * (c + 1)), held(sp, TAKES * c)
                sp.wait_ge(go, 1)
                sp.wait_ge(qkv_stored, stored)
                if due(last):
                    sp.wait_ge(taken, last)
                for z in range(2):
                    sp.dma_start(pin[:, z].rearrange("p d t -> p (d t)"),
                                 s_qkv[c, z + 1].rearrange("b (h d) t -> (b h) (d t)", h=H)).then_inc(kv_loaded, 16)
                sp.dma_start(beta_p[:], s_beta[c].rearrange("b h t -> (b h) t")).then_inc(kv_loaded, 16)

            def q_in(c):
                last, stored = held(sp, OUT_OPS * c), held(sp, 16 * 4 * (c + 1))
                sp.wait_ge(go, 1)
                sp.wait_ge(qkv_stored, stored)
                if due(last):
                    sp.wait_ge(o_part, last)
                sp.dma_start(q_p[:].rearrange("p d t -> p (d t)"),
                             s_qkv[c, 0].rearrange("b (h d) t -> (b h) (d t)", h=H)).then_inc(q_loaded, 16)

            def heads_out(c):
                last, this, stored = held(sp, c), held(sp, OUT_OPS * (c + 1)), held(sp, 16 * (c + 1))
                added_to = held(sp, E * (c - 1) + 1)
                sp.wait_ge(go, 1)
                sp.wait_ge(o_part, this)
                sp.dma_start(s_o.rearrange("b h m t -> (b h) (m t)"),
                             o_p[:].rearrange("p m t -> p (m t)")).then_inc(o_stored, 16)
                sp.wait_ge(go, 1)
                sp.wait_ge(o_stored, stored)
                if due(last):
                    sp.wait_ge(on_ready, last)
                sp.dma_start(o_T[:].rearrange("p (b t) -> p b t", b=B),
                             s_o.rearrange("b h m t -> (h m) b t")).then_inc(o_loaded, 16)
                sp.wait_ge(go, 1)
                if due(added_to):
                    sp.wait_ge(added, added_to)
                sp.dma_start(x_r[:].rearrange("p j d -> p (j d)"), d["x"][c]).then_inc(xr_loaded, 16)

            def store_mid(c):
                this = held(sp, E * (c + 1))
                sp.wait_ge(go, 1)
                sp.wait_ge(added, this)
                sp.dma_start(s_x[c], x2[:].rearrange("p j d -> p (j d)")).then_inc(x2_stored, 16)

            def load_mid(c):
                last, stored = held(sp, c), held(sp, 16 * (c + 1))
                sp.wait_ge(go, 1)
                sp.wait_ge(x2_stored, stored)
                if due(last):
                    sp.wait_ge(kept, last)
                sp.dma_start(x_b[:].rearrange("p j d -> p (j d)"), s_x[c]).then_inc(xb_loaded, 16)

            def store_out(c):
                this = held(sp, E * (NCH + c + 1))
                sp.wait_ge(go, 1)
                sp.wait_ge(added, this)
                sp.dma_start(out[c], x2[:].rearrange("p j d -> p (j d)")).then_inc(x2_stored, 16)

            load_x(0)
            for k, (dst, src) in enumerate(WEIGHTS):
                sp.dma_start(dst, src).then_inc(prep_loaded if k < PREP_W else w_loaded, 16)
            load_x(1)
            pairs_out(0)
            pairs_in(0)
            load_x(2)
            pairs_out(1)
            pairs_in(1)
            q_in(0)
            load_x(3)
            pairs_out(2)
            for i in (1, 2):
                pairs_in(i + 1)
                q_in(i)
                heads_out(i - 1)
                load_x(i + 3)
                pairs_out(i + 2)
            with sp.Fori(3, NCH - 3) as i:
                pairs_in(i + 1)
                store_mid(i - 3)
                q_in(i)
                heads_out(i - 1)
                load_x(i + 3)
                pairs_out(i + 2)
            pairs_in(NCH - 2)
            store_mid(NCH - 6)
            q_in(NCH - 3)
            heads_out(NCH - 4)
            pairs_out(NCH - 1)
            pairs_in(NCH - 1)
            store_mid(NCH - 5)
            q_in(NCH - 2)
            heads_out(NCH - 3)
            store_mid(NCH - 4)
            q_in(NCH - 1)
            heads_out(NCH - 2)
            store_mid(NCH - 3)
            heads_out(NCH - 1)
            load_mid(0)
            store_mid(NCH - 2)
            load_mid(1)
            store_mid(NCH - 1)
            load_mid(2)
            with sp.Fori(2, NCH - 1) as i:
                store_out(i - 2)
                load_mid(i + 1)
            for c in range(NCH - 3, NCH):
                store_out(c)
            sp.wait_ge(x2_stored, 16 * 2 * NCH)

        @block.gpsimd
        def _(pool):
            nc.gpsimd.memset(one_col[:], 1.0).then_inc(go, 1)
            nc.gpsimd.memset(xnT_h[:, :, 0:KC - 1].bitcast(F32), 0.0).then_inc(pool_ready, 1)
            nc.gpsimd.memset(xnT_l[:, :, 0:KC - 1].bitcast(F32), 0.0).then_inc(pool_ready, 1)
            nc.gpsimd.memset(eps_ln[:], LN_EPS).then_inc(pool_ready, 1)
            nc.gpsimd.memset(eps_on[:], DELTA_EPS).then_inc(pool_ready, 1)
            nc.gpsimd.memset(eps_l2[:], DELTA_EPS ** 2).then_inc(pool_ready, 1)
            nc.gpsimd.memset(neg_l2[:], -DELTA_EPS ** 2).then_inc(pool_ready, 1)
            nc.gpsimd.memset(ones_row[:], 1.0).then_inc(pool_ready, 1)
            nc.gpsimd.memset(state[:].rearrange("p b h e -> p (b h e)"), 0.0).then_inc(pool_ready, 1)
            nc.gpsimd.memset(v_bd[:].rearrange("p b n r e -> p (b n r e)"), 0.0).then_inc(pool_ready, 1)
            pool.wait_ge(pool_ready, 9)
            for par in range(2):
                nc.gpsimd.memset(v_bd[64 * par:64 * par + 64, :, :, par, HD], 1.0).then_inc(pool_ready, 1)

            tt = nc.gpsimd.tensor_tensor

            def delta_pre(c):
                base = PRE_OPS * c
                keys, values = wv[:, 0:HD], wv[:, HD:2 * HD]
                by_step = wv[:].rearrange("p f (n j) -> p f j n", j=BS)
                k_step = pin[:, 0].rearrange("p d (n j) -> p d j n", j=BS)
                pool.wait_ge(kv_loaded, 16 * 3 * (c + 1))
                if due(c):
                    pool.wait_ge(taken, TAKES * c)
                tt(keys, pin[:, 0], bc(beta_p[:], 1, HD), ALU.mult).then_inc(pre, 1)
                tt(values, pin[:, 1], bc(beta_p[:], 1, HD), ALU.mult).then_inc(pre, 1)
                pool.wait_ge(pre, base + 1)
                for i in range(BS - 1):
                    tt(kk[:, :, FIRST[i]:FIRST[i + 1]], by_step[:, 0:HD, i + 1:], bc(k_step[:, :, i], 2, BS - 1 - i), ALU.mult
                       ).then_inc(pre, 1)
                for k in range(3):
                    pool.wait_ge(pre, base + 2 + BS - 1 + k)
                    half = HD >> (k + 1)
                    tt(kk[:, 0:half], kk[:, 0:half], kk[:, half:2 * half], ALU.add).then_inc(pre, 1)
                for i in range(BS - 1):
                    part = wv_part[:, :, 0:BS - 1 - i]
                    pool.wait_ge(pre, base + 2 + BS + 2 + 2 * i)
                    tt(part, bc(by_step[:, :, i], 2, BS - 1 - i), bc(kk[:, 0, FIRST[i]:FIRST[i + 1]], 1, 2 * HD), ALU.mult
                       ).then_inc(pre, 1)
                    pool.wait_ge(pre, base + 2 + BS + 3 + 2 * i)
                    tt(by_step[:, :, i + 1:], by_step[:, :, i + 1:], part, ALU.subtract).then_inc(pre, 1)

            def delta_out(c):
                base = OUT_OPS * c
                q_step = q_p[:].rearrange("p d (n j) -> p d j n", j=BS)
                k_step = k_p[:].rearrange("p d (n j) -> p d j n", j=BS)
                o_step = o_p[:].rearrange("p m (n j) -> p m n j", j=BS)
                pool.wait_ge(q_loaded, 16 * (c + 1))
                pool.wait_ge(taken, TAKES * (c + 1))
                tt(qk[:, :, 0], q_step[:, :, 0], k_step[:, :, 0], ALU.mult).then_inc(o_part, 1)
                tt(qk[:, :, 1:3], bc(q_step[:, :, 1], 2, 2), k_step[:, :, 2:4], ALU.mult).then_inc(o_part, 1)
                tt(qk[:, :, 3], q_step[:, :, 2], k_step[:, :, 3], ALU.mult).then_inc(o_part, 1)
                for k in range(3):
                    pool.wait_ge(o_part, base + 3 + k)
                    half = HD >> (k + 1)
                    tt(qk[:, 0:half], qk[:, 0:half], qk[:, half:2 * half], ALU.add).then_inc(o_part, 1)
                if due(c):
                    pool.wait_ge(o_stored, 16 * c)
                for g, (first, end) in enumerate(O_GROUPS):
                    at, n = base + 6 + 13 * g, slice(first, end)
                    oq = oq_mem[:, 0:(end - first) * BS * HD * HD].rearrange("p (n j m d) -> p n j m d", j=BS, m=HD, d=HD)
                    flat = oq_mem[:, 0:(end - first) * BS * HD * HD].rearrange("p (x d) -> p x d", d=HD)
                    pool.wait_ge(step, BS * (NB * c + end))
                    pool.wait_ge(o_part, at - 3 if g else at)
                    for j in range(BS):
                        s_at = hist[:, first + (j > 0):end + (j > 0), :, :, BS]
                        tt(oq[:, :, j], s_at, bc(q_step[:, :, j, n].rearrange("p d n -> p n d"), 2, HD), ALU.mult
                           ).then_inc(o_part, 1)
                    fix = ofix[:, :, n]
                    tt(fix[:, 0], u[:, n, 0], bc(qk[:, 0, 0, n], 2, HD), ALU.mult).then_inc(o_part, 1)
                    tt(fix[:, 1:3], u[:, n, 2:4].rearrange("p n j m -> p j n m"), bc(qk[:, 0, 1:3, n], 3, HD), ALU.mult
                       ).then_inc(o_part, 1)
                    tt(fix[:, 3], u[:, n, 3], bc(qk[:, 0, 3, n], 2, HD), ALU.mult).then_inc(o_part, 1)
                    pool.wait_ge(o_part, at + 4)
                    tt(flat[:, :, 0:4], flat[:, :, 0:4], flat[:, :, 4:8], ALU.add).then_inc(o_part, 1)
                    pool.wait_ge(o_part, at + 8)
                    tt(flat[:, :, 0:2], flat[:, :, 0:2], flat[:, :, 2:4], ALU.add).then_inc(o_part, 1)
                    pool.wait_ge(o_part, at + 9)
                    tt(o_p[:, :, BS * first:BS * end].rearrange("p m t -> p t m"),
                       flat[:, :, 0].rearrange("p (t m) -> p t m", m=HD), flat[:, :, 1].rearrange("p (t m) -> p t m", m=HD),
                       ALU.add).then_inc(o_part, 1)
                    pool.wait_ge(o_part, at + 10)
                    tt(o_step[:, :, n, 0], o_step[:, :, n, 0], fix[:, 0].rearrange("p n m -> p m n"), ALU.add
                       ).then_inc(o_part, 1)
                    tt(o_step[:, :, n, 1:3].rearrange("p m n j -> p j m n"),
                       o_step[:, :, n, 1:3].rearrange("p m n j -> p j m n"), fix[:, 1::2].rearrange("p j n m -> p j m n"),
                       ALU.subtract).then_inc(o_part, 1)
                    pool.wait_ge(o_part, at + 12)
                    last = tt(o_step[:, :, n, 1], o_step[:, :, n, 1], fix[:, 2].rearrange("p n m -> p m n"), ALU.subtract)
                    last.then_inc(o_part, 1)

            delta_pre(0)
            delta_pre(1)
            pool.wait_ge(w1_split, 2)
            delta_out(0)
            with pool.Fori(1, NCH - 1) as i:
                delta_pre(i + 1)
                delta_out(i)
            delta_out(NCH - 1)


        @block.scalar
        def _(act):
            def prep_rstd(c):
                act.wait_ge(mv_ready, J * (c + 1))
                nc.scalar.activation(rstd[:], mv[:, :, 1], ACT.Ln, bias=eps_ln[:]).then_inc(rstd_log, 1)
                act.wait_ge(rstd_log, c + 1)
                nc.scalar.activation(rstd[:], rstd[:], ACT.Exp, scale=-0.5).then_inc(rstd_ready, 1)

            def prep_xnT(c, first=False):
                act.wait_ge(xn_transposed, c + 1)
                if due(4 * c):
                    act.wait_ge(projected, 4 * c)
                if not first:
                    for x in (xnT_h, xnT_l):
                        nc.scalar.copy(x[:, :, 0:KC - 1], x[:, :, CH:CH + KC - 1]).then_inc(halo_kept, 1)
                    act.wait_ge(halo_kept, 2 * c)
                nc.scalar.copy(xnT_h[:, :, KC - 1:], bank[:, TB, :].rearrange("p (b t) -> p b t", b=B)
                               ).then_inc(xnT_ready, 1)

            def prep_sigmoid(c, z):
                src = bank[:, (QB, KB, QB)[z], :]
                act.wait_ge(projected, 4 * c + z + 1)
                nc.scalar.activation(sig[:, z], src, ACT.Exp, scale=-1.0).then_inc(sig_exp, 1)
                act.wait_ge(sig_exp, 3 * c + z + 1)
                nc.scalar.activation(sig[:, z], sig[:, z], ACT.Ln, bias=one_col[:]).then_inc(sig_log, 1)
                act.wait_ge(sig_log, 3 * c + z + 1)
                nc.scalar.activation(sig[:, z], sig[:, z], ACT.Exp, scale=-1.0).then_inc(sig_ready, 1)

            def prep_beta(c):
                act.wait_ge(projected, 4 * c + 4)
                if due(16 * 4 * c):
                    act.wait_ge(qkv_stored, 16 * 4 * c)
                nc.scalar.activation(beta_T[:], bank[0:H, KB, :], ACT.Exp, scale=-1.0).then_inc(beta_exp, 1)
                act.wait_ge(beta_exp, c + 1)
                nc.scalar.activation(beta_T[:], beta_T[:], ACT.Ln, bias=one_col[0:H]).then_inc(beta_log, 1)
                act.wait_ge(beta_log, c + 1)
                nc.scalar.activation(beta_T[:], beta_T[:], ACT.Exp, scale=-1.0).then_inc(beta_ready, 1)

            def prep_square(c):
                act.wait_ge(silu_ready, 3 * c + 2)
                nc.scalar.activation(sq[:], qkv[:, 0:2], ACT.Square).then_inc(squared, 1)

            def prep_norm(c):
                act.wait_ge(norms, c + 1)
                nc.scalar.activation(rqk[:], bank[:, QB:QB + 2, :], ACT.Relu, bias=neg_l2[:]).then_inc(norm_max, 1)
                act.wait_ge(norm_max, c + 1)
                nc.scalar.activation(rqk[:], rqk[:], ACT.Ln, bias=eps_l2[:]).then_inc(norm_log, 1)
                act.wait_ge(norm_log, c + 1)
                nc.scalar.activation(rqk[:], rqk[:], ACT.Exp, scale=-0.5).then_inc(norm_ready, 1)

            def out_square(c):
                act.wait_ge(o_loaded, 16 * (c + 1))
                nc.scalar.activation(osq[:], o_T[:], ACT.Square).then_inc(o_squared, 1)

            def out_norm(c):
                act.wait_ge(o_norms, c + 1)
                nc.scalar.activation(orn[:], bank[:, MB, :], ACT.Ln, bias=eps_on[:], scale=1.0 / HD).then_inc(o_log, 1)
                act.wait_ge(o_log, c + 1)
                nc.scalar.activation(orn[:], orn[:], ACT.Exp, scale=-0.5).then_inc(o_rnorm, 1)

            def moe_rstd(n):
                act.wait_ge(mvf_ready, J * (n + 1))
                nc.scalar.activation(rstdf[:], mvf[:, :, 1], ACT.Ln, bias=eps_ln[:]).then_inc(rstdf_log, 1)
                act.wait_ge(rstdf_log, n + 1)
                nc.scalar.activation(rstdf[:], rstdf[:], ACT.Exp, scale=-0.5).then_inc(rstdf_ready, 1)

            def moe_xfT(n):
                act.wait_ge(xf_transposed, n + 1)
                if due(n):
                    act.wait_ge(xT_rest, n)
                nc.scalar.copy(xfT[:], bank[:, MB, :]).then_inc(xfT_ready, 1)

            def moe_exp(n):
                act.wait_ge(lsub_ready, n + 1)
                nc.scalar.activation(pexp[:].rearrange("p j e -> p (j e)"), lsub[:].rearrange("p j e -> p (j e)"),
                                     ACT.Exp).then_inc(pexp_ready, 1)

            def moe_split(n):
                act.wait_ge(xfT_ready, n + 1)
                if due(FC * E * n):
                    act.wait_ge(z_ready, FC * E * n)
                nc.scalar.copy(xT_h[:], xfT[:]).then_inc(xT_ready, 1)

            def moe_expert(n, e):
                if due(E * n + e - 1):
                    act.wait_ge(y_part, E * n + e - 1)
                for f in range(FC):
                    act.wait_ge(z_ready, FC * (E * n + e) + f + 1)
                    nc.scalar.activation(hid[:, e % 2, f], bank[:, ZB + f, :], ACT.Relu).then_inc(hid_ready, 1)

            def prep(c, first=False):
                prep_rstd(c)
                prep_xnT(c, first)
                for z in range(3):
                    prep_sigmoid(c, z)
                prep_beta(c)
                prep_square(c)
                prep_norm(c)

            def step1(i, prep=True, out=True, moe=True):
                c, o, n = i + 2, i - 1, i - 2
                for e in range(E):
                    if prep and e == 0:
                        prep_rstd(c)
                    if moe:
                        moe_expert(n, e)
                    if out:
                        if e == 0:
                            out_square(o)
                        elif e == 1:
                            out_norm(o)
                        elif e == 2:
                            moe_rstd(o)
                        elif e == 3:
                            moe_xfT(o)
                        elif e == 5:
                            moe_exp(o)
                    if prep:
                        if e == 0:
                            prep_xnT(c)
                        elif e == 1:
                            prep_sigmoid(c, 0)
                        elif e == 2:
                            prep_sigmoid(c, 1)
                        elif e == 3:
                            prep_sigmoid(c, 2)
                        elif e == 4:
                            prep_beta(c)
                            prep_square(c)
                        elif e == 5:
                            prep_norm(c)
                if out:
                    moe_split(o)

            def lin_xT(c):
                act.wait_ge(xn_transposed, NCH + c + 1)
                if due(c):
                    act.wait_ge(lin_projected, c)
                nc.scalar.copy(linT, bank[:, TB, :]).then_inc(xnT_ready, 1)

            def lin_exp(c):
                act.wait_ge(phi_low, c + 1)
                nc.scalar.activation(phi_min[:], phi_min[:], ACT.Exp).then_inc(phi_exp, 1)

            def lin_v(c):
                act.wait_ge(v_projected, c + 1)
                if due(c):
                    act.wait_ge(state_parts, c)
                for par in range(2):
                    h = slice(64 * par, 64 * par + 64)
                    nc.scalar.copy(v_bd[h, :, :, par, 0:HD], bank[h, TB, :].rearrange(
                        "p (b n e) -> p b n e", b=B, n=NP)).then_inc(v_ready, 1)

            def lin_ktok(c):
                for half in range(2):
                    act.wait_ge(k_transposed, 2 * c + half + 1)
                    if half == 0:
                        if due(c):
                            act.wait_ge(state_parts, c)
                    nc.scalar.copy(k_tok[:, 4 * half:4 * half + 4], bank[:, (MB, TB)[half], :].rearrange(
                        "p (b f) -> p b f", b=4)).then_inc(ktok_ready, 1)

            def lin_outT(c):
                act.wait_ge(lin_transposed, c + 1)
                nc.scalar.copy(linT, bank[:, MB, :]).then_inc(linT_ready, 1)

            nc.scalar.preload_act_table_set("natural_log_exp_and_others")
            act.wait_ge(go, 1)
            act.wait_ge(pool_ready, POOL_ALL)
            act.wait_ge(prep_loaded, 16 * PREP_W)
            act.wait_ge(taps_scaled, 1)
            nc.scalar.copy(wtap_h[:], wtap).then_inc(taps_split, 1)
            prep(0, first=True)
            act.wait_ge(w_loaded, 16 * (len(WEIGHTS) - PREP_W))
            nc.scalar.copy(w1_h[:], w1).then_inc(w1_split, 1)
            prep(1)
            step1(0, out=False, moe=False)
            step1(1, moe=False)
            step1(2)
            with act.Fori(3, NCH - 2) as i:
                step1(i)
            for i in range(NCH - 2, NCH):
                step1(i, prep=False)

            def lin_pre(c):
                prep_rstd(NCH + c)
                lin_xT(c)

            def step2(i, lin=True, pre=True):
                n = NCH + i - 1
                if lin:
                    lin_exp(i)
                moe_expert(n, 0)
                if lin:
                    lin_v(i)
                    lin_ktok(i)
                for e in range(1, 5):
                    moe_expert(n, e)
                if pre:
                    prep_rstd(NCH + i + 1)
                moe_expert(n, 5)
                if lin:
                    lin_outT(i)
                moe_expert(n, 6)
                if lin:
                    moe_rstd(n + 1)
                moe_expert(n, 7)
                if pre:
                    lin_xT(i + 1)
                if lin:
                    moe_xfT(n + 1)
                    moe_split(n + 1)
                    moe_exp(n + 1)

            step1(NCH, prep=False)
            lin_pre(0)
            step2(0)
            with act.Fori(1, NCH - 1) as i:
                step2(i)
            step2(NCH - 1, pre=False)
            step2(NCH, lin=False, pre=False)

        @block.tensor
        def _(pe):
            def prep_transpose(c):
                pe.wait_ge(xn_ready, J * (c + 1))
                if due(c):
                    pe.wait_ge(xnT_ready, c)
                for j in range(J):
                    last = nc.tensor.transpose(bank[:, TB, 128 * j:128 * j + 128], xn[:, j], ident[:])
                last.then_inc(xn_transposed, 1)

            def split_matmul(out_bank, terms):
                passes = [(wt, x, k, times) for k, times in terms
                          for wt, x in ((wtap_h, xnT_h), (wtap_h, xnT_l), (wtap_l, xnT_h))]
                for p, (wt, x, k, times) in enumerate(passes):
                    last = nc.tensor.matmul(out_bank, wt[:, k], x[:, :, times], start=(p == 0), stop=(p == len(passes) - 1))
                return last

            def prep_project(c, z):
                if z == 0:
                    pe.wait_ge(xnT_ready, c + 1)
                    pe.wait_ge(xnT_rest, c + 1)
                if z < 2:
                    if due(c):
                        pe.wait_ge(norm_max, c)
                else:
                    pe.wait_ge(silu_ready, 3 * c + 1)
                split_matmul(bank[:, (QB, KB, QB)[z], :],
                             [(KC * z + k, slice(k, k + CH)) for k in range(KC)]).then_inc(projected, 1)

            def prep_beta(c):
                pe.wait_ge(silu_ready, 3 * c + 2)
                split_matmul(bank[:, KB, :], [(3 * KC, slice(KC - 1, KC - 1 + CH))]).then_inc(projected, 1)

            def prep_norms(c):
                pe.wait_ge(squared, c + 1)
                pe.wait_ge(silu_ready, 3 * c + 3)
                pe.wait_ge(beta_exp, c + 1)
                for z in range(2):
                    last = nc.tensor.matmul(bank[:, QB + z, :], ones_block[:], sq[:, z], start=True, stop=True)
                last.then_inc(norms, 1)

            def out_norms(c):
                pe.wait_ge(o_squared, c + 1)
                if due(c):
                    pe.wait_ge(routed, c)
                if due(c):
                    pe.wait_ge(lsub_ready, c)
                nc.tensor.matmul(bank[:, MB, :], ones_block[:], osq[:], start=True, stop=True).then_inc(o_norms, 1)

            def out_project(c):
                pe.wait_ge(on_ready, c + 1)
                for j in range(J):
                    last = nc.tensor.matmul(bank[:, MB, 128 * j:128 * j + 128], on[:, 128 * j:128 * j + 128], wo_n[:],
                                            start=True, stop=True)
                last.then_inc(o_projected, 1)

            def moe_transpose(n):
                pe.wait_ge(xf_ready, J * (n + 1))
                for j in range(J):
                    last = nc.tensor.transpose(bank[:, MB, 128 * j:128 * j + 128], xf[:, j], ident[:])
                last.then_inc(xf_transposed, 1)

            def moe_route(n):
                pe.wait_ge(xfT_ready, n + 1)
                for j in range(J):
                    last = nc.tensor.matmul(bank[:, MB, E * j:E * j + E], xfT[:, 128 * j:128 * j + 128], wg[:],
                                            start=True, stop=True)
                last.then_inc(routed, 1)

            def moe_up(n, e):
                if e == 0:
                    pe.wait_ge(xT_ready, n + 1)
                    pe.wait_ge(xT_rest, n + 1)
                for f in range(FC):
                    if due(FC * (E * n + e - 1) + f + 1):
                        pe.wait_ge(hid_ready, FC * (E * n + e - 1) + f + 1)
                    part = slice(128 * f, 128 * f + 128)
                    nc.tensor.matmul(bank[:, ZB + f, :], w1_h[:, e, part], xT_h[:], start=True, stop=False)
                    nc.tensor.matmul(bank[:, ZB + f, :], w1_h[:, e, part], xT_l[:], start=False, stop=False)
                    nc.tensor.matmul(bank[:, ZB + f, :], w1_l[:, e, part], xT_h[:], start=False, stop=True
                                     ).then_inc(z_ready, 1)

            def moe_down(n, e):
                pe.wait_ge(hid_ready, FC * (E * n + e + 1))
                if due(E * n + e - 1):
                    pe.wait_ge(added, E * n + e - 1)
                for j in range(J):
                    tokens = slice(128 * j, 128 * j + 128)
                    for f in range(FC):
                        last = nc.tensor.matmul(bank[:, (XB, YB)[e % 2], tokens], hid[:, e % 2, f, tokens], w2[:, e, f],
                                                start=(f == 0), stop=(f == FC - 1))
                last.then_inc(y_part, 1)

            def moe_expert(n, e):
                moe_up(n, e)
                if e >= 1:
                    moe_down(n, e - 1)

            def prep(c):
                prep_transpose(c)
                for z in range(3):
                    prep_project(c, z)
                prep_beta(c)
                prep_norms(c)

            def step1(i, prep=True, out=True, moe=True):
                c, o, n = i + 2, i - 1, i - 2
                for e in range(E):
                    if moe:
                        moe_expert(n, e)
                    if prep:
                        if e == 0:
                            prep_transpose(c)
                        elif e <= 3:
                            prep_project(c, e - 1)
                        elif e == 4:
                            prep_beta(c)
                        elif e == 5:
                            prep_norms(c)
                    if out:
                        if e == 1:
                            out_norms(o)
                        elif e == 2:
                            out_project(o)
                        elif e == 3:
                            moe_transpose(o)
                        elif e == 5:
                            moe_route(o)
                if moe:
                    moe_down(n, E - 1)

            pe.wait_ge(prep_loaded, 16 * PREP_W)
            pe.wait_ge(pool_ready, POOL_ALL)
            pe.wait_ge(taps_split, 2)
            prep(0)
            prep(1)
            pe.wait_ge(w_loaded, 16 * (len(WEIGHTS) - PREP_W))
            pe.wait_ge(w1_split, 2)
            pe.wait_ge(taps_ready, 1)
            step1(0, out=False, moe=False)
            step1(1, moe=False)
            step1(2)
            with pe.Fori(3, NCH - 2) as i:
                step1(i)
            for i in range(NCH - 2, NCH + 1):
                step1(i, prep=False)

            def lin_project(c):
                pe.wait_ge(xnT_ready, NCH + c + 1)
                if due(3 * c):
                    pe.wait_ge(state_masked, 3 * c)
                for z in range(2):
                    last = nc.tensor.matmul(bank[:, QB + z, :], wqk_b[:, z], linT, start=True, stop=True)
                last.then_inc(qk_projected, 1)
                for b in range(B):
                    for par in range(2):
                        last = nc.tensor.matmul(bank[64 * par:64 * par + 64, TB, 64 * b:64 * b + 64],
                                                linT[:, CH * b:CH * b + CH], wv_b[:, par], start=True, stop=True)
                last.then_inc(v_projected, 1)

            def lin_ktok(c):
                pe.wait_ge(phi_ready, 3 * (c + 1))
                pe.wait_ge(lsub_ready, NCH + c)
                for half in range(2):
                    if half == 1:
                        pe.wait_ge(v_ready, 2 * (c + 1))
                    for q in range(4):
                        b = 4 * half + q
                        last = nc.tensor.transpose(bank[:, (MB, TB)[half], 128 * q:128 * q + 128],
                                                   phi_k[:, b].rearrange("p r t -> p (r t)"), ident[:])
                    last.then_inc(k_transposed, 1)

            def lin_scores(c, j):
                if j == 0:
                    taken = held(pe, c + 1)
                    pe.wait_ge(go, 1)
                    pe.wait_ge(qbd_ready, taken)
                else:
                    read = held(pe, J * c + j)
                    pe.wait_ge(go, 1)
                    pe.wait_ge(att_ready, read)
                for p in range(2):
                    b = 2 * j + p
                    for par in range(2):
                        for r in range(2):
                            h = slice(64 * r, 64 * r + 64)
                            last = nc.tensor.matmul(
                                bank[64 * par:64 * par + 64, QB + r, 256 * p:256 * p + 256],
                                phi_k[h, b, 0], q_bd[h, par::2, CH * b:CH * b + CH],
                                start=True, stop=True)
                last.then_inc(scores, 1)

            def lin_numer(c, j):
                pe.wait_ge(att_ready, J * c + j + 1)
                if j == 0:
                    pe.wait_ge(v_ready, 2 * (c + 1))
                    pe.wait_ge(ktok_ready, 2 * (c + 1))
                    if due(c):
                        pe.wait_ge(state_ready, c)
                if j >= 2:
                    if due(J * c + j - 1):
                        pe.wait_ge(lin_ready, J * c + j - 1)
                for p in range(2):
                    b = 2 * j + p
                    o = bank[64 * p:64 * p + 64, (TB, MB)[j % 2], 0:H * HV]
                    for r in range(2):
                        for i4 in range(4):
                            n = 4 * r + i4
                            nc.tensor.matmul(o[:, 2 * HV * n:2 * HV * n + 2 * HV], att[:, j % 2, r, p, i4],
                                             v_bd[:, b, n].rearrange("p r e -> p (r e)"), start=(n == 0), stop=False,
                                             skip_group_check=True)
                    last = nc.tensor.matmul(o, phi_q[:, CH * b:CH * b + CH], state[:, b].rearrange("p h e -> p (h e)"),
                                            start=False, stop=True, skip_group_check=True)
                last.then_inc(numer, 1)

            def lin_state(c):
                pe.wait_ge(lin_ready, J * c + J - 1)
                for b in range(B):
                    o = bank[:, b // 3, H * HV * (b % 3):H * HV * (b % 3) + H * HV]
                    last = nc.tensor.matmul(o, k_tok[:, b], v_bd[:, b].rearrange("p n r e -> p (n r e)"),
                                            start=True, stop=True)
                last.then_inc(state_parts, 1)

            def lin_transpose(c):
                pe.wait_ge(lin_ready, J * (c + 1))
                for j in range(J):
                    last = nc.tensor.transpose(bank[:, MB, 128 * j:128 * j + 128], lin[:, j], ident[:])
                last.then_inc(lin_transposed, 1)

            def lin_project_out(c):
                pe.wait_ge(linT_ready, c + 1)
                for j in range(J):
                    o = bank[:, MB, 128 * j:128 * j + 128]
                    nc.tensor.matmul(o, ones_row[:], bo_row[:], start=True, stop=False)
                    last = nc.tensor.matmul(o, linT[:, 128 * j:128 * j + 128], wo_b[:], start=False, stop=True)
                last.then_inc(lin_projected, 1)

            def lin_pre(c):
                if due(c):
                    pe.wait_ge(state_masked, 3 * c)
                prep_transpose(NCH + c)

            def step2(i, lin=True, pre=True):
                n = NCH + i - 1
                moe_expert(n, 0)
                if lin:
                    lin_ktok(i)
                moe_expert(n, 1)
                if lin:
                    lin_scores(i, 0)
                moe_expert(n, 2)
                if lin:
                    lin_scores(i, 1)
                    lin_numer(i, 0)
                moe_expert(n, 3)
                if lin:
                    lin_scores(i, 2)
                    lin_numer(i, 1)
                    lin_scores(i, 3)
                moe_expert(n, 4)
                if lin:
                    lin_numer(i, 2)
                    lin_numer(i, 3)
                moe_up(n, 5)
                if lin:
                    lin_state(i)
                    lin_transpose(i)
                moe_down(n, 4)
                moe_up(n, 6)
                if lin:
                    lin_project_out(i)
                moe_down(n, 5)
                moe_up(n, 7)
                if pre:
                    lin_pre(i + 1)
                moe_down(n, 6)
                if lin:
                    moe_transpose(n + 1)
                if pre:
                    lin_project(i + 1)
                if lin:
                    moe_route(n + 1)
                moe_down(n, 7)

            lin_pre(0)
            lin_project(0)
            step2(0)
            with pe.Fori(1, NCH - 1) as i:
                step2(i)
            step2(NCH - 1, pre=False)
            step2(NCH, lin=False, pre=False)

        @block.vector
        def _(dve):
            tt, ts, stt, red = (nc.vector.tensor_tensor, nc.vector.tensor_scalar, nc.vector.scalar_tensor_tensor,
                                nc.vector.tensor_reduce)

            def stats(src, b6, out_mv, bn_done, mv_ready, c):
                for j in range(J):
                    nc.vector.bn_stats(b6[:, j], src[:, j]).then_inc(bn_done, 1)
                done = held(dve, J * (c + 1))
                dve.wait_ge(go, 1)
                dve.wait_ge(bn_done, done)
                for j in range(J):
                    nc.vector.bn_aggr(out_mv[:, j], b6[:, j]).then_inc(mv_ready, 1)

            def normed(dst, src, mvt, r, done):
                for j in range(J):
                    ts(dst[:, j], src[:, j], mvt[:, j, 0:1], r[:, j:j + 1], ALU.subtract, ALU.mult).then_inc(done, 1)

            def prep_stats(c):
                dve.wait_ge(x_loaded, 16 * (c + 1))
                stats(x_in, bn6, mv, bn_done, mv_ready, c)

            def prep_xn(c):
                dve.wait_ge(rstd_ready, c + 1)
                if due(c):
                    dve.wait_ge(xn_transposed, c)
                normed(xn, x_in, mv, rstd, xn_ready)

            def prep_xnT_rest(c):
                dve.wait_ge(xnT_ready, c + 1)
                tt(xnT_l[:, :, KC - 1:], bank[:, TB, :].rearrange("p (b t) -> p b t", b=B),
                   xnT_h[:, :, KC - 1:].bitcast(F32), ALU.subtract).then_inc(xnT_rest, 1)

            def prep_silu(c, z):
                dve.wait_ge(sig_ready, 3 * c + z + 1)
                if z == 0:
                    if due(16 * 4 * c):
                        dve.wait_ge(qkv_stored, 16 * 4 * c)
                tt(qkv[:, z], bank[:, (QB, KB, QB)[z], :], sig[:, z], ALU.mult).then_inc(silu_ready, 1)

            def prep_qk(c):
                dve.wait_ge(norm_ready, c + 1)
                stt(qkv[:, 0], qkv[:, 0], QSCALE, rqk[:, 0], ALU.mult, ALU.mult).then_inc(qk_ready, 1)
                tt(qkv[:, 1], qkv[:, 1], rqk[:, 1], ALU.mult).then_inc(qk_ready, 1)

            def delta_take(c, first=False):
                dve.wait_ge(pre, PRE_OPS * (c + 1))
                if not first:
                    dve.wait_ge(step, 4 * NB * c)
                nc.vector.tensor_copy(prod[:, :, :, HD].rearrange("p t m -> p m t"), wv[:, HD:2 * HD]).then_inc(taken, 1)
                ts(nw[:], wv[:, 0:HD], -1.0, None, ALU.mult).then_inc(taken, 1)
                if first:
                    nc.vector.memset(hist[:, 0, :, :, BS], 0.0).then_inc(taken, 1)
                else:
                    dve.wait_ge(o_part, OUT_OPS * (c - 1) + 6 + 13)
                    nc.vector.tensor_copy(hist[:, 0, :, :, BS], hist[:, NB, :, :, BS]).then_inc(taken, 1)
                nc.vector.tensor_copy(k_p[:], pin[:, 0]).then_inc(taken, 1)
                dve.wait_ge(taken, TAKES * (c + 1))

            def delta_block(c, n, first=False):
                at = 4 * (NB * c + n)
                s_in = hist[:, n, :, :, BS]
                t = slice(BS * n, BS * n + BS)
                for g, (begin, _) in enumerate(O_GROUPS):
                    if g and n == begin - 1 and not first:
                        dve.wait_ge(o_part, OUT_OPS * (c - 1) + 6 + 13 * (g + 1))
                if n:
                    dve.wait_ge(step, at)
                tt(prod[:, t, :, 0:HD], bc(s_in, 1, BS), bc(nw[:, :, t].rearrange("p d t -> p t d"), 2, HD), ALU.mult
                   ).then_inc(step, 1)
                dve.wait_ge(step, at + 1)
                red(u[:, n], prod[:, t], AX_X, ALU.add).then_inc(step, 1)
                dve.wait_ge(step, at + 2)
                tt(hist[:, n, :, :, 0:BS].rearrange("p m d s -> p s m d"), bc(u[:, n], 3, HD),
                   bc(k_p[:, :, t].rearrange("p d t -> p t d"), 2, HD), ALU.mult).then_inc(step, 1)
                dve.wait_ge(step, at + 3)
                red(hist[:, n + 1, :, :, BS], hist[:, n], AX_X, ALU.add).then_inc(step, 1)

            def out_on(c):
                dve.wait_ge(o_rnorm, c + 1)
                tt(on[:], o_T[:], orn[:], ALU.mult).then_inc(on_ready, 1)

            def out_residual(c):
                dve.wait_ge(o_projected, c + 1)
                dve.wait_ge(xr_loaded, 16 * (c + 1))
                tt(x_r[:], x_r[:], bank[:, MB, :].rearrange("p (j d) -> p j d", j=J), ALU.add).then_inc(xr_ready, 1)
                dve.wait_ge(xr_ready, c + 1)
                stats(x_r, bn6f, mvf, bnf_done, mvf_ready, c)

            def moe_xn(n, src):
                dve.wait_ge(rstdf_ready, n + 1)
                if due(n):
                    dve.wait_ge(xf_transposed, n)
                normed(xf, src, mvf, rstdf, xf_ready)

            def moe_rank(n):
                dve.wait_ge(routed, n + 1)
                lp = bank[:, MB, 0:J * E].rearrange("p (j e) -> p j e", j=J)
                nc.vector.tensor_copy(logit[:], lp).then_inc(route, 1)
                red(lmax[:], lp, AX_X, ALU.max).then_inc(route, 1)
                dve.wait_ge(route, 9 * n + 2)
                tt(lsub[:], logit[:], bc(lmax[:], 2, E), ALU.subtract).then_inc(lsub_ready, 1)
                other, own = bc(logit[:], 2, E), bc(logit[:], 3, E)
                tt(above[:], other, own, ALU.is_gt).then_inc(route, 1)
                tt(same[:], other, own, ALU.is_equal).then_inc(route, 1)
                dve.wait_ge(route, 9 * n + 4)
                tt(same[:], same[:], bc(lower[:], 1, J), ALU.mult).then_inc(route, 1)
                dve.wait_ge(route, 9 * n + 5)
                tt(above[:], above[:], same[:], ALU.add).then_inc(route, 1)
                dve.wait_ge(route, 9 * n + 6)
                red(rank[:], above[:], AX_X, ALU.add).then_inc(route, 1)

            def moe_gate(n):
                dve.wait_ge(pexp_ready, n + 1)
                dve.wait_ge(route, 9 * n + 7)
                stt(pick[:], rank[:], 1.5, pexp[:], ALU.is_lt, ALU.mult).then_inc(route, 1)
                dve.wait_ge(route, 9 * n + 8)
                red(psum[:], pick[:], AX_X, ALU.add).then_inc(route, 1)
                dve.wait_ge(route, 9 * n + 9)
                nc.vector.reciprocal(rsum[:], psum[:]).then_inc(psum_inv, 1)
                dve.wait_ge(psum_inv, n + 1)
                if due(n):
                    dve.wait_ge(gate_taken, n)
                tt(gate[:], pick[:], bc(rsum[:], 2, E), ALU.mult).then_inc(gate_ready, 1)

            def moe_split(n):
                dve.wait_ge(xT_ready, n + 1)
                tt(xT_l[:], xfT[:], xT_h[:].bitcast(F32), ALU.subtract).then_inc(xT_rest, 1)

            def moe_take(n):
                dve.wait_ge(gate_ready, n + 1)
                if due(E * n):
                    dve.wait_ge(added, E * n)
                nc.vector.tensor_copy(gate_now[:], gate[:]).then_inc(gate_taken, 1)
                dve.wait_ge(gate_taken, n + 1)

            def moe_add(n, e, src=x2):
                dve.wait_ge(y_part, E * n + e + 1)
                if e:
                    dve.wait_ge(added, E * n + e)
                elif due(n):
                    dve.wait_ge(x2_stored, 16 * n)
                for j in range(J):
                    last = stt(x2[:, j], bank[:, (XB, YB)[e % 2], 128 * j:128 * j + 128], gate_now[:, j, e:e + 1],
                               src[:, j], ALU.mult, ALU.add)
                last.then_inc(added, 1)

            dve.wait_ge(prep_loaded, 16 * PREP_W)
            tt(wtap[:, 0:3 * KC].rearrange("p (z k) f -> p z k f", k=KC), bc(wqkv[:], 2, KC),
               wtap[:, 0:3 * KC].rearrange("p (z k) f -> p z k f", k=KC), ALU.mult).then_inc(taps_scaled, 1)
            dve.wait_ge(pool_ready, POOL_ALL)
            dve.wait_ge(taps_split, 1)
            tt(wtap_l[:], wtap, wtap_h[:].bitcast(F32), ALU.subtract).then_inc(taps_split, 1)

            def prep_all(c):
                prep_stats(c)
                prep_xn(c)
                prep_xnT_rest(c)
                for z in range(3):
                    prep_silu(c, z)
                prep_qk(c)

            def step1(i, prep=True, out=True, moe=True, tail=True, delta=True, first=False):
                c, o, n = i + 2, i - 1, i - 2
                if delta:
                    delta_take(i, first)
                for blk in range(NB):
                    if delta:
                        delta_block(i, blk, first)
                    if blk == 0:
                        if tail:
                            moe_add(n - 1, E - 1)
                        if moe:
                            moe_take(n)
                    if prep:
                        if blk == 0:
                            prep_stats(c)
                        elif blk == 1:
                            prep_xn(c)
                        elif blk == 2:
                            prep_xnT_rest(c)
                        elif blk in (5, 8, 10):
                            prep_silu(c, (5, 8, 10).index(blk))
                        elif blk == 14:
                            prep_qk(c)
                    if moe and blk in (3, 5, 7, 9, 11, 13, 14):
                        e = (3, 5, 7, 9, 11, 13, 14).index(blk)
                        moe_add(n, e, x2 if e else x_r)
                    if out:
                        if blk == 4:
                            out_on(o)
                        elif blk == 6:
                            out_residual(o)
                        elif blk == 8:
                            moe_xn(o, x_r)
                        elif blk == 12:
                            moe_rank(o)
                        elif blk == 13:
                            moe_gate(o)
                        elif blk == 15:
                            moe_split(o)

            prep_all(0)
            dve.wait_ge(w1_split, 1)
            tt(w1_l[:], w1, w1_h[:].bitcast(F32), ALU.subtract).then_inc(w1_split, 1)
            ts(wo_n[:], wo_a[:], onorm[:], None, ALU.mult).then_inc(taps_ready, 1)
            prep_all(1)
            dve.wait_ge(taps_split, 2)
            step1(0, out=False, moe=False, tail=False, first=True)
            step1(1, moe=False, tail=False)
            step1(2, tail=False)
            with dve.Fori(3, NCH - 2) as i:
                step1(i)
            for i in range(NCH - 2, NCH + 1):
                step1(i, prep=False, delta=(i < NCH))

            def lin_pre(c):
                dve.wait_ge(xb_loaded, 16 * (c + 1))
                stats(x_b, bn6, mv, bn_done, mv_ready, NCH + c)

            def lin_xn(c):
                dve.wait_ge(rstd_ready, NCH + c + 1)
                if due(NCH + c):
                    dve.wait_ge(xn_transposed, NCH + c)
                normed(xn, x_b, mv, rstd, xn_ready)

            def lin_phi_low(c):
                dve.wait_ge(qk_projected, c + 1)
                ts(phi_min[:], bank[:, QB:QB + 2, :], 0.0, None, ALU.min).then_inc(phi_low, 1)

            def lin_phi(c):
                dve.wait_ge(phi_exp, c + 1)
                stt(phi_q[:], bank[:, QB, :], 0.0, phi_min[:, 0], ALU.max, ALU.add).then_inc(phi_ready, 1)
                for r in range(2):
                    stt(phi_k[:, :, r], bank[:, KB, :].rearrange("p (b t) -> p b t", b=B), 0.0,
                        phi_min[:, 1].rearrange("p (b t) -> p b t", b=B), ALU.max, ALU.add).then_inc(phi_ready, 1)
                dve.wait_ge(phi_ready, 3 * c + 1)
                for h in range(HD):
                    last = ts(q_bd[:, h], phi_q[:], head_mask[:, h:h + 1], None, ALU.mult)
                last.then_inc(qbd_ready, 1)

            def lin_att(c, j):
                dve.wait_ge(scores, J * c + j + 1)
                if due(J * c + j - 1):
                    dve.wait_ge(numer, J * c + j - 1)
                tt(att[:, j % 2].rearrange("p r b i t -> p (r b i) t"),
                   bank[:, QB:QB + 2, :].rearrange("p r (n t) -> p (r n) t", t=CH),
                   bc(causal[:], 1, 16), ALU.mult).then_inc(att_ready, 1)

            def lin_out(c, j):
                dve.wait_ge(numer, J * c + j + 1)
                src = bank[:, (TB, MB)[j % 2], 0:H * HV].rearrange("p (h e) -> p h e", h=H)
                ts(den[:, j], src[:, :, HD], LIN_EPS, None, ALU.add).then_inc(den_ready, 1)
                dve.wait_ge(den_ready, J * c + j + 1)
                nc.vector.reciprocal(rden[:, j], den[:, j]).then_inc(rden_ready, 1)
                dve.wait_ge(rden_ready, J * c + j + 1)
                tt(lin[:, j].rearrange("p (h e) -> p h e", h=H), src[:, :, 0:HD], bc(rden[:, j], 2, HD), ALU.mult
                   ).then_inc(lin_ready, 1)

            def lin_state(c):
                dve.wait_ge(state_parts, c + 1)
                for k in range(3):
                    nb = min(3, B - 3 * k)
                    tt(dstate[:, 3 * k:3 * k + nb].rearrange("p b h e -> p b (h e)"),
                       bank[:, k, 0:nb * H * HV].rearrange("p (b f) -> p b f", b=nb),
                       bc(state_mask[:].rearrange("p h e -> p (h e)"), 1, nb), ALU.mult).then_inc(state_masked, 1)
                dve.wait_ge(state_masked, 3 * (c + 1))
                tt(state[:], state[:], dstate, ALU.add).then_inc(state_ready, 1)

            def lin_residual(c):
                dve.wait_ge(lin_projected, c + 1)
                dve.wait_ge(kept, c + 1)
                if due(c):
                    dve.wait_ge(added, E * (NCH + c - 1) + 1)
                tt(x3, x_keep[:], bank[:, MB, :].rearrange("p (j d) -> p j d", j=J), ALU.add).then_inc(x3_ready, 1)
                dve.wait_ge(x3_ready, c + 1)
                stats(x3, bn6f, mvf, bnf_done, mvf_ready, NCH + c)

            def lin_keep(c):
                if due(c):
                    dve.wait_ge(x3_ready, c)
                nc.vector.tensor_copy(x_keep[:], x_b[:]).then_inc(kept, 1)

            def step2(i, lin=True, pre=True, src=x3):
                n = NCH + i - 1
                if lin:
                    lin_phi_low(i)
                moe_add(n - 1, E - 1)
                moe_take(n)
                if lin:
                    lin_phi(i)
                    lin_att(i, 0)
                moe_add(n, 0, src)
                if lin:
                    lin_att(i, 1)
                    lin_out(i, 0)
                moe_add(n, 1)
                if lin:
                    lin_att(i, 2)
                    lin_out(i, 1)
                    lin_att(i, 3)
                moe_add(n, 2)
                if lin:
                    lin_out(i, 2)
                    lin_out(i, 3)
                moe_add(n, 3)
                if lin:
                    lin_state(i)
                if pre:
                    lin_pre(i + 1)
                    lin_xn(i + 1)
                moe_add(n, 4)
                if lin:
                    lin_residual(i)
                if pre:
                    lin_keep(i + 1)
                moe_add(n, 5)
                if lin:
                    moe_xn(n + 1, x3)
                moe_add(n, 6)
                if lin:
                    moe_split(n + 1)
                    moe_rank(n + 1)
                    moe_gate(n + 1)

            lin_pre(0)
            lin_xn(0)
            lin_keep(0)
            step2(0, src=x_r)
            with dve.Fori(1, NCH - 1) as i:
                step2(i)
            step2(NCH - 1, pre=False)
            step2(NCH, lin=False, pre=False)
            moe_add(2 * NCH - 1, E - 1)


def kernel(**inputs):
    import numpy as np
    import concourse.bacc as bacc
    from concourse.bass_utils import run_bass_kernel_spmd

    def a(name):
        return np.asarray(inputs["L0_" + name])

    f = np.float32

    def rows(x):
        x = x.reshape(J, 2, NCH, CH, D).transpose(2, 1, 3, 0, 4)
        return np.ascontiguousarray(x.reshape(NCH, 128, J * D))

    p = np.arange(128)
    convs = np.stack([a("attn_a_conv_q").T, a("attn_a_conv_k").T, a("attn_a_conv_v").T])
    arrays = {
        "x": rows(a("attn_a_x")),
        "wqkv": np.stack([a("attn_a_Wq").T, a("attn_a_Wk").T, a("attn_a_Wv").T], axis=1),
        "conv": np.broadcast_to(convs[None], (128, 3, KC, D)).reshape(128, 3 * KC, D),
        "wbeta": np.pad(a("attn_a_Wb").T, ((0, 0), (0, D - H))),
        "wo_a": a("attn_a_Wo").T,
        "onorm": np.tile(a("attn_a_o_norm_w"), H)[:, None],
        "wqk_b": np.stack([a("attn_b_Wq").T, a("attn_b_Wk").T], axis=1),
        "wv_b": a("attn_b_Wv").T.reshape(D, NP, 2, HD).transpose(0, 2, 1, 3).reshape(D, 2, NP * HD),
        "wo_b": a("attn_b_Wo").T,
        "bo_row": a("attn_b_bo")[None],
        "wg": a("ffn_Wg"),
        "w1": a("ffn_W1").transpose(1, 0, 2),
        "w2": a("ffn_W2").reshape(E, FC, 128, D).transpose(2, 0, 1, 3),
        "ident": np.eye(128, dtype=f),
        "ones_block": (p[:, None] // HD == p[None] // HD).astype(f),
        "causal": (p[:, None] % CH <= np.arange(CH)[None]).astype(f),
        "lower": np.broadcast_to((np.arange(E)[None] < np.arange(E)[:, None]).astype(f), (128, E, E)),
        "state_mask": np.broadcast_to((p[:, None, None] // HD == np.arange(H)[None, :, None]), (128, H, HV)).astype(f),
        "head_mask": (p[:, None] // HD % HD == np.arange(HD)[None]).astype(f),
    }
    arrays = {k: np.ascontiguousarray(v) for k, v in arrays.items()}
    nc = bacc.Bacc("TRN2", target_bir_lowering=False, num_devices=1)
    d = {k: nc.dram_tensor("in_" + k, v.shape, mybir.dt.from_np(v.dtype), kind="ExternalInput").ap()
         for k, v in arrays.items()}
    out = nc.dram_tensor("out_x", (NCH, 128, J * D), F32, kind="ExternalOutput").ap()
    build(nc, d, out)
    r = run_bass_kernel_spmd(nc, [{"in_" + k: v for k, v in arrays.items()}], core_ids=[0])
    y = r.results[0]["out_x"].reshape(NCH, 2, CH, J, D).transpose(3, 1, 0, 2, 4)
    return np.ascontiguousarray(y.reshape(B, L, D))
```

```python
from contextlib import ExitStack

import concourse.bass as bass
from concourse import mybir

F32 = mybir.dt.float32
F32R = mybir.dt.float32r
ALU = mybir.AluOpType
ACT = mybir.ActivationFunctionType
AX_X = mybir.AxisListType.X

B, L, D = 8, 512, 128
H, HD = 16, 8
KC = 4
E, FF = 8, 256
EV = E // 2
CH = 64
NCH = L // CH
NT = B * CH
J = NT // 128
BS = 4
NB = CH // BS
O_GROUPS = ((0, 6), (6, 12), (12, NB))
PAIRS = BS * (BS - 1) // 2
FC = FF // 128
HV = HD + 1
NP = H // 2
LN_EPS, DELTA_EPS, LIN_EPS = 1e-5, 1e-6, 1e-5
QSCALE = float(HD) ** -0.5


def due(count):
    return not isinstance(count, int) or count > 0


def held(eng, count):
    return count if isinstance(count, int) else eng.snap(eng.to_reg(count))


def bc(ap, axis, n):
    ap = ap.unsqueeze(axis)
    shape = list(ap.shape)
    shape[axis] = n
    return ap.to_broadcast(shape)


def build(nc, d, out):
    with ExitStack() as ctx:
        def sb(name, shape, dtype=F32):
            return ctx.enter_context(nc.sbuf_tensor(name, shape, dtype))

        def sem(name):
            return ctx.enter_context(nc.semaphore(name))

        ident = sb("ident", [128, 128])
        ones_block = sb("ones_block", [128, 128])
        causal = sb("causal", [128, CH])
        lower = sb("lower", [128, E, E])
        state_mask = sb("state_mask", [128, H, HV])
        head_mask = sb("head_mask", [128, HD])
        wqkv = sb("wqkv", [128, 3, D])
        wtap_h = sb("wtap_h", [128, 3 * KC + 1, D], F32R)
        wtap_l = sb("wtap_l", [128, 3 * KC + 1, D], F32R)
        wo_a = sb("wo_a", [128, D])
        onorm = sb("onorm", [128, 1])
        wo_n = sb("wo_n", [128, D])
        wqk_b = sb("wqk_b", [128, 2, D])
        wv_b = sb("wv_b", [128, 2, NP * HD])
        wo_b = sb("wo_b", [128, D])
        bo_rows = sb("bo_rows", [128, D])
        wg = sb("wg", [128, E])
        w1_h = sb("w1_h", [128, E, FF], F32R)
        w1_l = sb("w1_l", [128, E, FF], F32R)
        w2 = sb("w2", [128, E, FC, D])
        eps_ln = sb("eps_ln", [128, 1])
        eps_on = sb("eps_on", [128, 1])
        eps_l2 = sb("eps_l2", [128, 1])
        neg_l2 = sb("neg_l2", [128, 1])
        one_col = sb("one_col", [128, 1])

        x_in = sb("x_in", [128, J, D])
        bn6 = sb("bn6", [128, J, 6])
        mv = sb("mv", [128, J, 2])
        rstd = sb("rstd", [128, J])
        xn = sb("xn", [128, J, D])
        neg_mean = sb("neg_mean", [128, J])
        square_sum = sb("square_sum", [128, J])
        neg_meanf = sb("neg_meanf", [128, J])
        square_sumf = sb("square_sumf", [128, J])
        xnT_h = sb("xnT_h", [128, B, KC - 1 + CH], F32R)
        xnT_l = sb("xnT_l", [128, B, KC - 1 + CH], F32R)
        sig = sb("sig", [128, 3, NT])
        qkv = sb("qkv", [128, 3, NT])
        beta_T = sb("beta_T", [H, NT])
        squares = sig[:, 2].rearrange("p (j d) -> p j d", j=J)
        sq = sig[:, 0:2]
        rqk = sb("rqk", [128, 2, NT])
        pin = sb("pin", [128, 2, HD, CH])
        beta_p = sb("beta_p", [128, CH])
        q_p = sb("q_p", [128, HD, CH])
        k_p = sb("k_p", [128, HD, CH])
        wv = sb("wv", [128, 2 * HD, CH])
        kk = sb("kk", [128, HD, PAIRS, NB])
        kdot = sb("kdot", [128, PAIRS, NB])
        wv_part = sb("wv_part", [128, 2 * HD, BS - 1, NB])
        nw = sb("nw", [128, HD, CH])
        prod_mem = sb("prod_mem", [128, CH * HD * HV])
        prod = prod_mem[:].rearrange("p (t m e) -> p t m e", t=CH, m=HD)
        wtap = prod_mem[:, 0:(3 * KC + 1) * D].rearrange("p (k f) -> p k f", f=D)
        u = sb("u", [128, NB, BS, HD])
        hist_mem = sb("hist_mem", [128, (NB + 1) * HD * HD * (BS + 1)])
        hist = hist_mem[:].rearrange("p (n m d s) -> p n m d s", n=NB + 1, m=HD, d=HD)
        qk = sb("qk", [128, HD, BS, NB])
        qdot = sb("qdot", [128, BS, NB])
        group_size = max(end - first for first, end in O_GROUPS)
        oq_size = group_size * BS * HD * (HD + 1)
        oq_mem = sb("oq_mem", [128, 2 * oq_size])
        w1 = oq_mem[:, 0:E * FF].rearrange("p (e f) -> p e f", e=E)
        later_u = sb("later_u", [128, 2, group_size, HD])
        o_p = sb("o_p", [128, HD, CH])
        o_T = sb("o_T", [128, NT])
        orn = sb("orn", [128, NT])
        osq = orn
        on = sb("on", [128, NT])
        x_r = sb("x_r", [128, J, D])
        bn6f = sb("bn6f", [128, J, 6])
        mvf = sb("mvf", [128, J, 2])
        rstdf = sb("rstdf", [128, J])
        xf = sb("xf", [128, J, D])
        xfT = sb("xfT", [128, NT])
        logit = sb("logit", [128, J, E])
        lmax = sb("lmax", [128, J])
        lsub = sb("lsub", [128, J, E])
        above = sb("above", [128, J, E, E])
        same = sb("same", [128, J, E, E])
        rank = sb("rank", [128, J, E])
        chosen = sb("chosen", [128, J, E])
        pexp = sb("pexp", [128, J, E])
        pick = sb("pick", [128, J, E])
        psum = sb("psum", [128, J])
        rsum = sb("rsum", [128, J])
        gate = sb("gate", [128, J, E])
        gate_now = sb("gate_now", [128, J, E])
        xT_h = sb("xT_h", [128, NT], F32R)
        xT_l = sb("xT_l", [128, NT], F32R)
        hid = sb("hid", [128, 2, FC, NT])
        x2 = sb("x2", [128, J, D])
        x_odd = sb("x_odd", [128, J, D])
        y_odd = sb("y_odd", [128, J, D])
        y_even = sb("y_even", [128, J, D])
        x_b = sb("x_b", [128, J, D])
        x_keep = x_in
        phi_min = sb("phi_min", [128, 2, NT])
        phi_k = sb("phi_k", [128, B, 2, CH])
        q_bd = hist_mem[:, 0:HD * NT].rearrange("p (h t) -> p h t", h=HD)
        phi_q = hist_mem[:, HD * NT:(HD + 1) * NT]
        v_bd = sb("v_bd", [128, B, NP, 2, HV])
        att_size, ktok_size, state_size = 2 * NP * 2 * CH, B * D, B * H * HV
        att = prod_mem[:, 0:att_size].rearrange("p (k r b i t) -> p k r b i t", k=2, r=2, b=2, i=4)
        k_tok = prod_mem[:, att_size:att_size + ktok_size].rearrange("p (b f) -> p b f", b=B)
        dstate = prod_mem[:, att_size + ktok_size:att_size + ktok_size + state_size].rearrange(
            "p (b h e) -> p b h e", b=B, h=H)
        state = sb("state", [128, B, H, HV])
        den = sb("den", [128, J, H])
        rden = sb("rden", [128, J, H])
        lin_at = [slice(oq_size + NT * k, oq_size + NT * (k + 1)) for k in range(3)]
        lin = oq_mem[:, lin_at[0]].rearrange("p (j d) -> p j d", j=J)
        linT = oq_mem[:, lin_at[1]]
        x3 = oq_mem[:, lin_at[2]].rearrange("p (j d) -> p j d", j=J)

        bank = ctx.enter_context(nc.psum_tensor("bank", [128, 8, 512], F32))
        TB, QB, KB, MB, XB, ZB, YB = 0, 1, 2, 3, 4, 5, 7

        s_qkv = nc.dram_tensor("s_qkv", [NCH, 3, B, D, CH], F32, kind="Internal").ap()
        s_beta = nc.dram_tensor("s_beta", [NCH, B, H, CH], F32, kind="Internal").ap()
        s_o = nc.dram_tensor("s_o", [B, H, HD, CH], F32, kind="Internal").ap()
        s_x = nc.dram_tensor("s_x", [NCH, 128, J * D], F32, kind="Internal").ap()

        go, w_loaded, taps_ready = sem("go"), sem("w_loaded"), sem("taps_ready")
        pool_ready = sem("pool_ready")
        x_loaded, bn_done, mv_ready = sem("x_loaded"), sem("bn_done"), sem("mv_ready")
        rstd_log, rstd_ready, xn_ready = sem("rstd_log"), sem("rstd_ready"), sem("xn_ready")
        mean_ready, xn_centred, xn_squared = sem("mean_ready"), sem("xn_centred"), sem("xn_squared")
        meanf_ready, xf_centred, xf_squared = sem("meanf_ready"), sem("xf_centred"), sem("xf_squared")
        xn_transposed, xnT_ready, halo_kept = sem("xn_transposed"), sem("xnT_ready"), sem("halo_kept")
        xnT_rest, taps_scaled, prep_loaded = sem("xnT_rest"), sem("taps_scaled"), sem("prep_loaded")
        taps_split, w1_split = sem("taps_split"), sem("w1_split")
        projected, sig_exp, sig_log = sem("projected"), sem("sig_exp"), sem("sig_log")
        sig_ready, beta_exp, beta_log = sem("sig_ready"), sem("beta_exp"), sem("beta_log")
        beta_ready, silu_ready = sem("beta_ready"), sem("silu_ready")
        squared, norms, norm_max = sem("squared"), sem("norms"), sem("norm_max")
        norm_log, norm_ready, qk_ready = sem("norm_log"), sem("norm_ready"), sem("qk_ready")
        qkv_stored, kv_loaded, q_loaded = sem("qkv_stored"), sem("kv_loaded"), sem("q_loaded")
        pre, kdot_ready = sem("pre"), sem("kdot_ready")
        taken, step, o_part = sem("taken"), sem("step"), sem("o_part")
        qk_products, qdot_plain, qdot_ready = sem("qk_products"), sem("qdot_plain"), sem("qdot_ready")
        oq_cleared, o_summed = sem("oq_cleared"), sem("o_summed")
        o_stored, o_loaded = sem("o_stored"), sem("o_loaded")
        o_squared, o_norms, o_log = sem("o_squared"), sem("o_norms"), sem("o_log")
        o_rnorm, on_ready, o_projected = sem("o_rnorm"), sem("on_ready"), sem("o_projected")
        xr_loaded = sem("xr_loaded")
        xr_ready, bnf_done, mvf_ready = sem("xr_ready"), sem("bnf_done"), sem("mvf_ready")
        rstdf_log, rstdf_ready, xf_ready = sem("rstdf_log"), sem("rstdf_ready"), sem("xf_ready")
        xf_transposed, xfT_ready, xT_ready, xT_rest = sem("xf_transposed"), sem("xfT_ready"), sem("xT_ready"), sem("xT_rest")
        routed, route, lsub_ready = sem("routed"), sem("route"), sem("lsub_ready")
        pexp_ready, gate_ready, gate_taken = sem("pexp_ready"), sem("gate_ready"), sem("gate_taken")
        z_ready, hid_ready, y_part = sem("z_ready"), sem("hid_ready"), sem("y_part")
        even_scaled, odd_scaled = sem("even_scaled"), sem("odd_scaled")
        added, odd_added = sem("added"), sem("odd_added")
        x2_stored, kept = sem("x2_stored"), sem("kept")
        xb_loaded, qk_projected, phi_low = sem("xb_loaded"), sem("qk_projected"), sem("phi_low")
        phi_exp, phi_ready, v_projected = sem("phi_exp"), sem("phi_ready"), sem("v_projected")
        v_ready, qbd_ready = sem("v_ready"), sem("qbd_ready")
        k_transposed, ktok_ready, scores = sem("k_transposed"), sem("ktok_ready"), sem("scores")
        att_ready, numer, den_ready = sem("att_ready"), sem("numer"), sem("den_ready")
        rden_ready, lin_ready = sem("rden_ready"), sem("lin_ready")
        state_parts, state_masked, state_ready = sem("state_parts"), sem("state_masked"), sem("state_ready")
        lin_transposed, linT_ready, lin_projected = sem("lin_transposed"), sem("linT_ready"), sem("lin_projected")
        x3_ready = sem("x3_ready")
        psum_inv = sem("psum_inv")

        WEIGHTS = [(ident[:], d["ident"]), (wqkv[:], d["wqkv"]), (wtap[:, 0:3 * KC], d["conv"]), (wtap[:, 3 * KC], d["wbeta"]),
                   (ones_block[:], d["ones_block"]),
                   (w1, d["w1"]), (wo_a[:], d["wo_a"]), (onorm[:], d["onorm"]), (wg[:], d["wg"]),
                   (lower[:], d["lower"]), (w2[:], d["w2"]), (causal[:], d["causal"]),
                   (state_mask[:], d["state_mask"]), (head_mask[:], d["head_mask"]), (wqk_b[:], d["wqk_b"]),
                   (wv_b[:], d["wv_b"]), (wo_b[:], d["wo_b"]), (bo_rows[:], d["bo_rows"])]
        PREP_W = 5

        POOL_ALL = 10
        TAKES = 4
        FIRST = [i * (BS - 1) - i * (i - 1) // 2 for i in range(BS)]
        PRE_OPS = 2 + (BS - 1) + 2 * (BS - 1)
        GROUP_OPS = BS + 5
        NG = len(O_GROUPS)

        block = ctx.enter_context(nc.Block())

        @block.sync
        def _(sp):
            def load_x(c):
                taken = held(sp, J * c)
                sp.wait_ge(go, 1)
                if due(taken):
                    sp.wait_ge(xn_ready, taken)
                sp.dma_start(x_in[:].rearrange("p j d -> p (j d)"), d["x"][c]).then_inc(x_loaded, 16)

            def pairs_out(c):
                one, two, three = held(sp, c + 1), held(sp, 2 * (c + 1)), held(sp, 3 * (c + 1))
                sp.wait_ge(go, 1)
                sp.wait_ge(qk_ready, two)
                sp.wait_ge(silu_ready, three)
                sp.wait_ge(beta_ready, one)
                for z in range(3):
                    sp.dma_start(s_qkv[c, z].rearrange("b p t -> p b t"),
                                 qkv[:, z, :].rearrange("p (b t) -> p b t", b=B)).then_inc(qkv_stored, 16)
                sp.dma_start(s_beta[c].rearrange("b h t -> h b t"),
                             beta_T[:].rearrange("h (b t) -> h b t", b=B)).then_inc(qkv_stored, 16)

            def pairs_in(c):
                stored, last = held(sp, 16 * 4 * (c + 1)), held(sp, TAKES * c)
                sp.wait_ge(go, 1)
                sp.wait_ge(qkv_stored, stored)
                if due(last):
                    sp.wait_ge(taken, last)
                for z in range(2):
                    sp.dma_start(pin[:, z].rearrange("p d t -> p (d t)"),
                                 s_qkv[c, z + 1].rearrange("b (h d) t -> (b h) (d t)", h=H)).then_inc(kv_loaded, 16)
                sp.dma_start(beta_p[:], s_beta[c].rearrange("b h t -> (b h) t")).then_inc(kv_loaded, 16)

            def q_in(c):
                last, stored = held(sp, NG * GROUP_OPS * c), held(sp, 16 * 4 * (c + 1))
                sp.wait_ge(go, 1)
                sp.wait_ge(qkv_stored, stored)
                if due(last):
                    sp.wait_ge(o_part, last)
                sp.dma_start(q_p[:].rearrange("p d t -> p (d t)"),
                             s_qkv[c, 0].rearrange("b (h d) t -> (b h) (d t)", h=H)).then_inc(q_loaded, 16)

            def heads_out(c):
                last, this, stored = held(sp, c), held(sp, NG * (c + 1)), held(sp, 16 * (c + 1))
                added_to = held(sp, EV * (c - 1) + 1)
                sp.wait_ge(go, 1)
                sp.wait_ge(o_summed, this)
                sp.dma_start(s_o.rearrange("b h m t -> (b h) (m t)"),
                             o_p[:].rearrange("p m t -> p (m t)")).then_inc(o_stored, 16)
                sp.wait_ge(go, 1)
                sp.wait_ge(o_stored, stored)
                if due(last):
                    sp.wait_ge(on_ready, last)
                sp.dma_start(o_T[:].rearrange("p (b t) -> p b t", b=B),
                             s_o.rearrange("b h m t -> (h m) b t")).then_inc(o_loaded, 16)
                sp.wait_ge(go, 1)
                if due(added_to):
                    sp.wait_ge(added, added_to)
                sp.dma_start(x_r[:].rearrange("p j d -> p (j d)"), d["x"][c]).then_inc(xr_loaded, 16)

            def store_mid(c):
                this = held(sp, EV * (c + 1))
                sp.wait_ge(go, 1)
                sp.wait_ge(odd_added, this)
                sp.dma_start(s_x[c], x_odd[:].rearrange("p j d -> p (j d)")).then_inc(x2_stored, 16)

            def load_mid(c):
                last, stored = held(sp, c), held(sp, 16 * (c + 1))
                sp.wait_ge(go, 1)
                sp.wait_ge(x2_stored, stored)
                if due(last):
                    sp.wait_ge(kept, last)
                sp.dma_start(x_b[:].rearrange("p j d -> p (j d)"), s_x[c]).then_inc(xb_loaded, 16)

            def store_out(c):
                this = held(sp, EV * (NCH + c + 1))
                sp.wait_ge(go, 1)
                sp.wait_ge(odd_added, this)
                sp.dma_start(out[c], x_odd[:].rearrange("p j d -> p (j d)")).then_inc(x2_stored, 16)

            load_x(0)
            for dst, src in WEIGHTS[:PREP_W]:
                sp.dma_start(dst, src).then_inc(prep_loaded, 16)
            load_x(1)
            for dst, src in WEIGHTS[PREP_W:]:
                sp.dma_start(dst, src).then_inc(w_loaded, 16)
            pairs_out(0)
            pairs_in(0)
            load_x(2)
            q_in(0)
            pairs_out(1)
            pairs_in(1)
            load_x(3)
            pairs_out(2)
            for i in (1, 2):
                pairs_in(i + 1)
                q_in(i)
                heads_out(i - 1)
                load_x(i + 3)
                pairs_out(i + 2)
            with sp.Fori(3, NCH - 3) as i:
                pairs_in(i + 1)
                store_mid(i - 3)
                q_in(i)
                heads_out(i - 1)
                load_x(i + 3)
                pairs_out(i + 2)
            pairs_in(NCH - 2)
            store_mid(NCH - 6)
            q_in(NCH - 3)
            heads_out(NCH - 4)
            pairs_out(NCH - 1)
            pairs_in(NCH - 1)
            store_mid(NCH - 5)
            q_in(NCH - 2)
            heads_out(NCH - 3)
            store_mid(NCH - 4)
            q_in(NCH - 1)
            heads_out(NCH - 2)
            load_mid(0)
            store_mid(NCH - 3)
            heads_out(NCH - 1)
            store_mid(NCH - 2)
            load_mid(1)
            store_mid(NCH - 1)
            load_mid(2)
            with sp.Fori(2, NCH - 1) as i:
                store_out(i - 2)
                load_mid(i + 1)
            for c in range(NCH - 3, NCH):
                store_out(c)
            sp.wait_ge(x2_stored, 16 * 2 * NCH)

        @block.gpsimd
        def _(pool):
            nc.gpsimd.memset(one_col[:], 1.0).then_inc(go, 1)
            nc.gpsimd.memset(xnT_h[:, :, 0:KC - 1].bitcast(F32), 0.0).then_inc(pool_ready, 1)
            nc.gpsimd.memset(xnT_l[:, :, 0:KC - 1].bitcast(F32), 0.0).then_inc(pool_ready, 1)
            nc.gpsimd.memset(eps_ln[:], LN_EPS).then_inc(pool_ready, 1)
            nc.gpsimd.memset(eps_on[:], DELTA_EPS).then_inc(pool_ready, 1)
            nc.gpsimd.memset(eps_l2[:], DELTA_EPS ** 2).then_inc(pool_ready, 1)
            nc.gpsimd.memset(neg_l2[:], -DELTA_EPS ** 2).then_inc(pool_ready, 1)
            nc.gpsimd.memset(state[:].rearrange("p b h e -> p (b h e)"), 0.0).then_inc(pool_ready, 1)
            nc.gpsimd.memset(v_bd[:].rearrange("p b n r e -> p (b n r e)"), 0.0).then_inc(pool_ready, 1)
            pool.wait_ge(pool_ready, 8)
            for par in range(2):
                nc.gpsimd.memset(v_bd[64 * par:64 * par + 64, :, :, par, HD], 1.0).then_inc(pool_ready, 1)

            tt = nc.gpsimd.tensor_tensor

            keys, values = wv[:, 0:HD], wv[:, HD:2 * HD]
            by_step = wv[:].rearrange("p f (n j) -> p f j n", j=BS)
            k_step = pin[:, 0].rearrange("p d (n j) -> p d j n", j=BS)
            q_step = q_p[:].rearrange("p d (n j) -> p d j n", j=BS)
            kp_step = k_p[:].rearrange("p d (n j) -> p d j n", j=BS)

            def delta_keys(c):
                base = PRE_OPS * c
                pool.wait_ge(kv_loaded, 16 * 3 * (c + 1))
                if due(c):
                    pool.wait_ge(taken, TAKES * c)
                tt(keys, pin[:, 0], bc(beta_p[:], 1, HD), ALU.mult).then_inc(pre, 1)
                pool.wait_ge(pre, base + 1)
                for i in range(BS - 1):
                    last = tt(kk[:, :, FIRST[i]:FIRST[i + 1]], by_step[:, 0:HD, i + 1:], bc(k_step[:, :, i], 2, BS - 1 - i),
                              ALU.mult)
                    last.then_inc(pre, 1)
                tt(values, pin[:, 1], bc(beta_p[:], 1, HD), ALU.mult).then_inc(pre, 1)

            def delta_solve(c):
                base = PRE_OPS * c + 2 + BS - 1
                pool.wait_ge(kdot_ready, c + 1)
                for i in range(BS - 1):
                    part = wv_part[:, :, 0:BS - 1 - i]
                    pool.wait_ge(pre, base + 2 * i)
                    tt(part, bc(by_step[:, :, i], 2, BS - 1 - i), bc(kdot[:, FIRST[i]:FIRST[i + 1]], 1, 2 * HD), ALU.mult
                       ).then_inc(pre, 1)
                    pool.wait_ge(pre, base + 2 * i + 1)
                    tt(by_step[:, :, i + 1:], by_step[:, :, i + 1:], part, ALU.subtract).then_inc(pre, 1)

            def delta_queries(c):
                pool.wait_ge(q_loaded, 16 * (c + 1))
                pool.wait_ge(taken, TAKES * (c + 1))
                tt(qk[:, :, 0], q_step[:, :, 0], kp_step[:, :, 0], ALU.mult).then_inc(qk_products, 1)
                tt(qk[:, :, 1:3], bc(q_step[:, :, 1], 2, 2), kp_step[:, :, 2:4], ALU.mult).then_inc(qk_products, 1)
                tt(qk[:, :, 3], q_step[:, :, 2], kp_step[:, :, 3], ALU.mult).then_inc(qk_products, 1)

            def delta_outputs(c, g):
                first, end = O_GROUPS[g]
                n, at = slice(first, end), GROUP_OPS * (NG * c + g)
                oq = oq_mem[:, oq_size * (g % 2):oq_size * (g % 2) + (end - first) * BS * HD * (HD + 1)].rearrange(
                    "p (n j m d) -> p n j m d", j=BS, m=HD, d=HD + 1)
                later = later_u[:, :, 0:end - first]
                last_use = NG * c + (0, -1, 1)[g]
                if due(last_use):
                    pool.wait_ge(o_summed, last_use)
                pool.wait_ge(qdot_ready, 2 * (c + 1))
                pool.wait_ge(step, 4 * (NB * c + end))
                if due(at):
                    pool.wait_ge(o_part, at)
                for i in range(2):
                    tt(later[:, i], u[:, n, 2 + i], bc(qdot[:, 1 + i, n], 2, HD), ALU.mult).then_inc(o_part, 1)
                for j in range(BS):
                    s_at = hist[:, first + (j > 0):end + (j > 0), :, :, BS]
                    tt(oq[:, :, j, :, 0:HD], s_at, bc(q_step[:, :, j, n].rearrange("p d n -> p n d"), 2, HD), ALU.mult
                       ).then_inc(o_part, 1)
                for j, k in ((0, 0), (2, 3)):
                    tt(oq[:, :, j, :, HD], u[:, n, k], bc(qdot[:, k, n], 2, HD), ALU.mult).then_inc(o_part, 1)
                pool.wait_ge(o_part, at + 2)
                tt(oq[:, :, 1, :, HD], later[:, 0], later[:, 1], ALU.add).then_inc(o_part, 1)

            def moe_add(n, e):
                pool.wait_ge(odd_scaled, EV * n + e // 2 + 1)
                if e > 3:
                    pool.wait_ge(odd_added, EV * n + e // 2 - 1)
                tt(x_odd[:], x_odd[:], y_odd[:], ALU.add).then_inc(odd_added, 1)

            def moe_finish(n):
                moe_add(n, E - 1)
                pool.wait_ge(odd_added, EV * n + EV - 1)
                pool.wait_ge(added, EV * (n + 1))
                tt(x_odd[:], x_odd[:], x2[:], ALU.add).then_inc(odd_added, 1)

            def step1(i, ahead=True, moe=True):
                delta_queries(i)
                if ahead:
                    delta_keys(i + 1)
                if not moe:
                    delta_outputs(i, 0)
                if ahead:
                    delta_solve(i + 1)
                if moe:
                    delta_outputs(i, 0)
                    moe_add(i - 2, 3)
                delta_outputs(i, 1)
                if moe:
                    moe_add(i - 2, 5)
                    moe_finish(i - 2)
                delta_outputs(i, 2)

            delta_keys(0)
            delta_solve(0)
            pool.wait_ge(w1_split, 2)
            for g in range(2):
                column = oq_mem[:, oq_size * g:oq_size * (g + 1)].rearrange("p (n j m d) -> p n j m d", j=BS, m=HD, d=HD + 1)
                nc.gpsimd.memset(column[:, :, BS - 1, :, HD], 0.0).then_inc(oq_cleared, 1)
            step1(0, moe=False)
            step1(1, moe=False)
            with pool.Fori(2, NCH - 1) as i:
                step1(i)
            step1(NCH - 1, ahead=False)
            with pool.Fori(NCH - 2, 2 * NCH) as n:
                moe_add(n, 3)
                moe_add(n, 5)
                moe_finish(n)

        @block.scalar
        def _(act):
            def norm_rows(src, dst, neg_mean, square_sum, rstd, c, mean_ready, centred, squared, log, ready, done):
                for j in range(J):
                    nc.scalar.activation(dst[:, j], src[:, j], ACT.Copy, scale=-1.0 / D, accum_out=neg_mean[:, j:j + 1]
                                         ).then_inc(mean_ready, 1)
                for j in range(J):
                    act.wait_ge(mean_ready, J * c + j + 1)
                    nc.scalar.activation(dst[:, j], src[:, j], ACT.Identity, bias=neg_mean[:, j:j + 1]).then_inc(centred, 1)
                for j in range(J):
                    act.wait_ge(centred, J * c + j + 1)
                    nc.scalar.activation(squares[:, j], dst[:, j], ACT.Square, accum_out=square_sum[:, j:j + 1]
                                         ).then_inc(squared, 1)
                act.wait_ge(squared, J * (c + 1))
                nc.scalar.activation(rstd[:], square_sum[:], ACT.Ln, bias=eps_ln[:], scale=1.0 / D).then_inc(log, 1)
                act.wait_ge(log, c + 1)
                nc.scalar.activation(rstd[:], rstd[:], ACT.Exp, scale=-0.5).then_inc(ready, 1)
                act.wait_ge(ready, c + 1)
                for j in range(J):
                    nc.scalar.activation(dst[:, j], dst[:, j], ACT.Copy, scale=rstd[:, j:j + 1]).then_inc(done, 1)

            def prep_xn(c, first=False):
                act.wait_ge(x_loaded, 16 * (c + 1))
                if due(c):
                    act.wait_ge(xn_transposed, c)
                if not first:
                    act.wait_ge(silu_ready, 3 * c)
                norm_rows(x_in, xn, neg_mean, square_sum, rstd, c, mean_ready, xn_centred, xn_squared, rstd_log, rstd_ready,
                          xn_ready)

            def lin_rstd(c):
                act.wait_ge(mv_ready, J * (c + 1))
                nc.scalar.activation(rstd[:], mv[:, :, 1], ACT.Ln, bias=eps_ln[:]).then_inc(rstd_log, 1)
                act.wait_ge(rstd_log, NCH + c + 1)
                nc.scalar.activation(rstd[:], rstd[:], ACT.Exp, scale=-0.5).then_inc(rstd_ready, 1)

            def prep_xnT(c, first=False):
                act.wait_ge(xn_transposed, c + 1)
                if due(4 * c):
                    act.wait_ge(projected, 4 * c)
                if not first:
                    for x in (xnT_h, xnT_l):
                        nc.scalar.copy(x[:, :, 0:KC - 1], x[:, :, CH:CH + KC - 1]).then_inc(halo_kept, 1)
                    act.wait_ge(halo_kept, 2 * c)
                nc.scalar.copy(xnT_h[:, :, KC - 1:], bank[:, TB, :].rearrange("p (b t) -> p b t", b=B)
                               ).then_inc(xnT_ready, 1)

            def prep_sigmoid(c, z):
                src = bank[:, (QB, KB, QB)[z], :]
                act.wait_ge(projected, 4 * c + z + 1)
                nc.scalar.activation(sig[:, z], src, ACT.Exp, scale=-1.0).then_inc(sig_exp, 1)
                act.wait_ge(sig_exp, 3 * c + z + 1)
                nc.scalar.activation(sig[:, z], sig[:, z], ACT.Ln, bias=one_col[:]).then_inc(sig_log, 1)
                act.wait_ge(sig_log, 3 * c + z + 1)
                nc.scalar.activation(sig[:, z], sig[:, z], ACT.Exp, scale=-1.0).then_inc(sig_ready, 1)

            def prep_beta(c):
                act.wait_ge(projected, 4 * c + 4)
                if due(16 * 4 * c):
                    act.wait_ge(qkv_stored, 16 * 4 * c)
                nc.scalar.activation(beta_T[:], bank[0:H, KB, :], ACT.Exp, scale=-1.0).then_inc(beta_exp, 1)
                act.wait_ge(beta_exp, c + 1)
                nc.scalar.activation(beta_T[:], beta_T[:], ACT.Ln, bias=one_col[0:H]).then_inc(beta_log, 1)
                act.wait_ge(beta_log, c + 1)
                nc.scalar.activation(beta_T[:], beta_T[:], ACT.Exp, scale=-1.0).then_inc(beta_ready, 1)

            def prep_square(c):
                act.wait_ge(silu_ready, 3 * c + 2)
                nc.scalar.activation(sq, qkv[:, 0:2], ACT.Square).then_inc(squared, 1)

            def prep_norm(c):
                act.wait_ge(norms, c + 1)
                nc.scalar.activation(rqk[:], bank[:, QB:QB + 2, :], ACT.Relu, bias=neg_l2[:]).then_inc(norm_max, 1)
                act.wait_ge(norm_max, c + 1)
                nc.scalar.activation(rqk[:], rqk[:], ACT.Ln, bias=eps_l2[:]).then_inc(norm_log, 1)
                act.wait_ge(norm_log, c + 1)
                nc.scalar.activation(rqk[:], rqk[:], ACT.Exp, scale=-0.5).then_inc(norm_ready, 1)

            def out_square(c):
                act.wait_ge(o_loaded, 16 * (c + 1))
                nc.scalar.activation(osq[:], o_T[:], ACT.Square).then_inc(o_squared, 1)

            def out_norm(c):
                act.wait_ge(o_norms, c + 1)
                nc.scalar.activation(orn[:], bank[:, MB, :], ACT.Ln, bias=eps_on[:], scale=1.0 / HD).then_inc(o_log, 1)
                act.wait_ge(o_log, c + 1)
                nc.scalar.activation(orn[:], orn[:], ACT.Exp, scale=-0.5).then_inc(o_rnorm, 1)

            def lin_rstdf(n):
                act.wait_ge(mvf_ready, J * (n - NCH + 1))
                nc.scalar.activation(rstdf[:], mvf[:, :, 1], ACT.Ln, bias=eps_ln[:]).then_inc(rstdf_log, 1)
                act.wait_ge(rstdf_log, n + 1)
                nc.scalar.activation(rstdf[:], rstdf[:], ACT.Exp, scale=-0.5).then_inc(rstdf_ready, 1)

            def moe_xfT(n):
                act.wait_ge(xf_transposed, n + 1)
                if due(n):
                    act.wait_ge(xT_rest, n)
                nc.scalar.copy(xfT[:], bank[:, MB, :]).then_inc(xfT_ready, 1)

            def moe_exp(n):
                act.wait_ge(lsub_ready, n + 1)
                nc.scalar.activation(pexp[:].rearrange("p j e -> p (j e)"), lsub[:].rearrange("p j e -> p (j e)"),
                                     ACT.Exp).then_inc(pexp_ready, 1)

            def moe_split(n):
                act.wait_ge(xfT_ready, n + 1)
                if due(FC * E * n):
                    act.wait_ge(z_ready, FC * E * n)
                nc.scalar.copy(xT_h[:], xfT[:]).then_inc(xT_ready, 1)

            def moe_expert(n, e):
                if due(E * n + e - 1):
                    act.wait_ge(y_part, E * n + e - 1)
                for f in range(FC):
                    act.wait_ge(z_ready, FC * (E * n + e) + f + 1)
                    nc.scalar.activation(hid[:, e % 2, f], bank[:, ZB + f, :], ACT.Relu).then_inc(hid_ready, 1)

            def moe_xf(n):
                act.wait_ge(xr_ready, n + 1)
                if due(n):
                    act.wait_ge(xf_transposed, n)
                norm_rows(x_r, xf, neg_meanf, square_sumf, rstdf, n, meanf_ready, xf_centred, xf_squared, rstdf_log,
                          rstdf_ready, xf_ready)

            def moe_scale(n, e):
                act.wait_ge(y_part, E * n + e + 1)
                if e == 0:
                    act.wait_ge(gate_taken, n + 1)
                if e % 2 == 0:
                    if due(EV * n + e // 2):
                        act.wait_ge(added, EV * n + e // 2)
                elif e == 1:
                    if due(n):
                        act.wait_ge(x2_stored, 16 * n)
                elif e > 3:
                    act.wait_ge(odd_added, EV * n + e // 2 - 1)
                for j in range(J):
                    last = nc.scalar.activation((x_odd if e == 1 else y_odd if e % 2 else y_even)[:, j],
                                                bank[:, (XB, YB)[e % 2], 128 * j:128 * j + 128], ACT.Copy,
                                                scale=gate_now[:, j, e:e + 1])
                last.then_inc((even_scaled, odd_scaled)[e % 2], 1)

            def step1(i, prep=True, out=True, moe=True, tail=True):
                c, o, n = i + 2, i - 1, i - 2
                if moe:
                    moe_expert(n, 0)
                    if tail:
                        moe_scale(n - 1, 7)
                    moe_exp(n)
                    moe_expert(n, 1)
                if prep:
                    prep_xn(c)
                if moe:
                    moe_expert(n, 2)
                    moe_scale(n, 0)
                if prep:
                    prep_xnT(c)
                if moe:
                    moe_scale(n, 1)
                if out:
                    out_square(o)
                if moe:
                    moe_expert(n, 3)
                    moe_scale(n, 2)
                if prep:
                    prep_sigmoid(c, 0)
                if out:
                    out_norm(o)
                if moe:
                    moe_expert(n, 4)
                    moe_scale(n, 3)
                if prep:
                    prep_sigmoid(c, 1)
                if moe:
                    moe_expert(n, 5)
                if out:
                    moe_xf(o)
                if moe:
                    moe_expert(n, 6)
                    moe_scale(n, 4)
                if out:
                    moe_xfT(o)
                if prep:
                    prep_sigmoid(c, 2)
                if moe:
                    moe_scale(n, 5)
                if prep:
                    prep_square(c)
                    prep_beta(c)
                if out:
                    moe_split(o)
                if moe:
                    moe_expert(n, 7)
                    moe_scale(n, 6)
                if prep:
                    prep_norm(c)

            def lin_xT(c):
                act.wait_ge(xn_transposed, NCH + c + 1)
                if due(c):
                    act.wait_ge(lin_projected, c)
                nc.scalar.copy(linT, bank[:, TB, :]).then_inc(xnT_ready, 1)

            def lin_exp(c):
                act.wait_ge(phi_low, c + 1)
                nc.scalar.activation(phi_min[:], phi_min[:], ACT.Exp).then_inc(phi_exp, 1)

            def lin_v(c):
                act.wait_ge(v_projected, c + 1)
                if due(c):
                    act.wait_ge(state_parts, c)
                for par in range(2):
                    h = slice(64 * par, 64 * par + 64)
                    nc.scalar.copy(v_bd[h, :, :, par, 0:HD], bank[h, TB, :].rearrange(
                        "p (b n e) -> p b n e", b=B, n=NP)).then_inc(v_ready, 1)

            def lin_ktok(c):
                for half in range(2):
                    act.wait_ge(k_transposed, 2 * c + half + 1)
                    if half == 0:
                        if due(c):
                            act.wait_ge(state_parts, c)
                    nc.scalar.copy(k_tok[:, 4 * half:4 * half + 4], bank[:, (MB, TB)[half], :].rearrange(
                        "p (b f) -> p b f", b=4)).then_inc(ktok_ready, 1)

            def lin_outT(c):
                act.wait_ge(lin_transposed, c + 1)
                nc.scalar.copy(linT, bank[:, MB, :]).then_inc(linT_ready, 1)

            nc.scalar.preload_act_table_set("natural_log_exp_and_others")
            act.wait_ge(go, 1)
            act.wait_ge(pool_ready, POOL_ALL)
            act.wait_ge(prep_loaded, 16 * PREP_W)
            act.wait_ge(taps_scaled, 1)
            nc.scalar.copy(wtap_h[:], wtap).then_inc(taps_split, 1)
            prep_xn(0, first=True)
            prep_xnT(0, first=True)
            prep_xn(1, first=True)
            for z in range(3):
                prep_sigmoid(0, z)
            prep_beta(0)
            prep_square(0)
            prep_xnT(1)
            prep_norm(0)
            for z in range(3):
                prep_sigmoid(1, z)
            prep_beta(1)
            prep_square(1)
            act.wait_ge(w_loaded, 16 * (len(WEIGHTS) - PREP_W))
            nc.scalar.copy(w1_h[:], w1).then_inc(w1_split, 1)
            prep_norm(1)
            step1(0, out=False, moe=False)
            step1(1, moe=False)
            step1(2, tail=False)
            with act.Fori(3, NCH - 2) as i:
                step1(i)
            for i in range(NCH - 2, NCH):
                step1(i, prep=False)
            def step2(i, lin=True, pre=True):
                n = NCH + i - 1
                moe_expert(n, 0)
                moe_scale(n - 1, 7)
                if lin:
                    lin_v(i)
                moe_expert(n, 1)
                if lin:
                    lin_ktok(i)
                moe_scale(n, 0)
                moe_expert(n, 2)
                moe_scale(n, 1)
                moe_expert(n, 3)
                moe_scale(n, 2)
                if pre:
                    lin_rstd(i + 1)
                moe_expert(n, 4)
                moe_scale(n, 3)
                moe_expert(n, 5)
                if lin:
                    lin_outT(i)
                moe_scale(n, 4)
                moe_expert(n, 6)
                if lin:
                    lin_rstdf(n + 1)
                moe_scale(n, 5)
                moe_expert(n, 7)
                if pre:
                    lin_xT(i + 1)
                moe_scale(n, 6)
                if lin:
                    moe_xfT(n + 1)
                    moe_split(n + 1)
                if pre:
                    lin_exp(i + 1)
                if lin:
                    moe_exp(n + 1)
                else:
                    moe_scale(n, 7)

            o, n = NCH - 1, NCH - 2
            moe_expert(n, 0)
            moe_scale(n - 1, 7)
            moe_exp(n)
            moe_expert(n, 1)
            lin_rstd(0)
            moe_expert(n, 2)
            moe_scale(n, 0)
            moe_scale(n, 1)
            moe_expert(n, 3)
            lin_xT(0)
            moe_scale(n, 2)
            moe_expert(n, 4)
            moe_scale(n, 3)
            out_square(o)
            out_norm(o)
            moe_expert(n, 5)
            lin_exp(0)
            moe_scale(n, 4)
            moe_expert(n, 6)
            moe_xf(o)
            moe_scale(n, 5)
            moe_expert(n, 7)
            moe_xfT(o)
            moe_split(o)
            moe_scale(n, 6)
            moe_exp(o)
            step2(0)
            with act.Fori(1, NCH - 1) as i:
                step2(i)
            step2(NCH - 1, pre=False)
            step2(NCH, lin=False, pre=False)

        @block.tensor
        def _(pe):
            def prep_transpose(c):
                pe.wait_ge(xn_ready, J * (c + 1))
                if due(c):
                    pe.wait_ge(xnT_ready, c)
                for j in range(J):
                    last = nc.tensor.transpose(bank[:, TB, 128 * j:128 * j + 128], xn[:, j], ident[:])
                last.then_inc(xn_transposed, 1)

            def split_matmul(out_bank, terms):
                passes = [(wt, x, k, times) for k, times in terms
                          for wt, x in ((wtap_h, xnT_h), (wtap_h, xnT_l), (wtap_l, xnT_h))]
                for p, (wt, x, k, times) in enumerate(passes):
                    last = nc.tensor.matmul(out_bank, wt[:, k], x[:, :, times], start=(p == 0), stop=(p == len(passes) - 1))
                return last

            def prep_project(c, z):
                if z == 0:
                    pe.wait_ge(xnT_ready, c + 1)
                    pe.wait_ge(xnT_rest, c + 1)
                if z < 2:
                    if due(c):
                        pe.wait_ge(norm_max, c)
                else:
                    pe.wait_ge(silu_ready, 3 * c + 1)
                split_matmul(bank[:, (QB, KB, QB)[z], :],
                             [(KC * z + k, slice(k, k + CH)) for k in range(KC)]).then_inc(projected, 1)

            def prep_beta(c):
                pe.wait_ge(silu_ready, 3 * c + 2)
                split_matmul(bank[:, KB, :], [(3 * KC, slice(KC - 1, KC - 1 + CH))]).then_inc(projected, 1)

            def prep_norms(c):
                pe.wait_ge(squared, c + 1)
                pe.wait_ge(silu_ready, 3 * c + 3)
                pe.wait_ge(beta_exp, c + 1)
                for z in range(2):
                    last = nc.tensor.matmul(bank[:, QB + z, :], ones_block[:], sq[:, z], start=True, stop=True)
                last.then_inc(norms, 1)

            def out_norms(c):
                pe.wait_ge(o_squared, c + 1)
                if due(c):
                    pe.wait_ge(routed, c)
                if due(c):
                    pe.wait_ge(lsub_ready, c)
                nc.tensor.matmul(bank[:, MB, :], ones_block[:], osq[:], start=True, stop=True).then_inc(o_norms, 1)

            def out_project(c):
                pe.wait_ge(on_ready, c + 1)
                for j in range(J):
                    last = nc.tensor.matmul(bank[:, MB, 128 * j:128 * j + 128], on[:, 128 * j:128 * j + 128], wo_n[:],
                                            start=True, stop=True)
                last.then_inc(o_projected, 1)

            def moe_transpose(n):
                pe.wait_ge(xf_ready, J * (n + 1))
                for j in range(J):
                    last = nc.tensor.transpose(bank[:, MB, 128 * j:128 * j + 128], xf[:, j], ident[:])
                last.then_inc(xf_transposed, 1)

            def moe_route(n):
                pe.wait_ge(xfT_ready, n + 1)
                for j in range(J):
                    last = nc.tensor.matmul(bank[:, MB, E * j:E * j + E], xfT[:, 128 * j:128 * j + 128], wg[:],
                                            start=True, stop=True)
                last.then_inc(routed, 1)

            def moe_up(n, e):
                if e == 0:
                    pe.wait_ge(xT_ready, n + 1)
                    pe.wait_ge(xT_rest, n + 1)
                for f in range(FC):
                    if due(FC * (E * n + e - 1) + f + 1):
                        pe.wait_ge(hid_ready, FC * (E * n + e - 1) + f + 1)
                    part = slice(128 * f, 128 * f + 128)
                    nc.tensor.matmul(bank[:, ZB + f, :], w1_h[:, e, part], xT_h[:], start=True, stop=False)
                    nc.tensor.matmul(bank[:, ZB + f, :], w1_h[:, e, part], xT_l[:], start=False, stop=False)
                    nc.tensor.matmul(bank[:, ZB + f, :], w1_l[:, e, part], xT_h[:], start=False, stop=True
                                     ).then_inc(z_ready, 1)

            def moe_down(n, e):
                pe.wait_ge(hid_ready, FC * (E * n + e + 1))
                if due(EV * n + e // 2):
                    if e % 2 == 0:
                        pe.wait_ge(even_scaled, EV * n + e // 2)
                    else:
                        pe.wait_ge(odd_scaled, EV * n + e // 2)
                for j in range(J):
                    tokens = slice(128 * j, 128 * j + 128)
                    for f in range(FC):
                        last = nc.tensor.matmul(bank[:, (XB, YB)[e % 2], tokens], hid[:, e % 2, f, tokens], w2[:, e, f],
                                                start=(f == 0), stop=(f == FC - 1))
                last.then_inc(y_part, 1)

            def moe_expert(n, e):
                moe_up(n, e)
                if e >= 1:
                    moe_down(n, e - 1)

            def step1(i, prep=True, out=True, moe=True):
                c, o, n = i + 2, i - 1, i - 2
                for e in range(3):
                    if moe:
                        moe_expert(n, e)
                if prep:
                    prep_transpose(c)
                if moe:
                    moe_expert(n, 3)
                if prep:
                    prep_project(c, 0)
                if out:
                    out_norms(o)
                if moe:
                    moe_expert(n, 4)
                if prep:
                    prep_project(c, 1)
                if out:
                    out_project(o)
                if moe:
                    moe_expert(n, 5)
                if prep:
                    prep_project(c, 2)
                if moe:
                    moe_expert(n, 6)
                if out:
                    moe_transpose(o)
                if prep:
                    prep_beta(c)
                if moe:
                    moe_expert(n, 7)
                if out:
                    moe_route(o)
                if prep:
                    prep_norms(c)
                if moe:
                    moe_down(n, E - 1)

            pe.wait_ge(prep_loaded, 16 * PREP_W)
            pe.wait_ge(pool_ready, POOL_ALL)
            pe.wait_ge(taps_split, 2)
            prep_transpose(0)
            for z in range(3):
                prep_project(0, z)
            prep_beta(0)
            prep_transpose(1)
            prep_norms(0)
            for z in range(3):
                prep_project(1, z)
            prep_beta(1)
            prep_norms(1)
            pe.wait_ge(w_loaded, 16 * (len(WEIGHTS) - PREP_W))
            pe.wait_ge(w1_split, 2)
            pe.wait_ge(taps_ready, 1)
            step1(0, out=False, moe=False)
            step1(1, moe=False)
            step1(2)
            with pe.Fori(3, NCH - 2) as i:
                step1(i)
            for i in range(NCH - 2, NCH):
                step1(i, prep=False)

            def lin_project(c):
                pe.wait_ge(xnT_ready, NCH + c + 1)
                if due(3 * c):
                    pe.wait_ge(state_masked, 3 * c)
                for z in range(2):
                    last = nc.tensor.matmul(bank[:, QB + z, :], wqk_b[:, z], linT, start=True, stop=True)
                last.then_inc(qk_projected, 1)
                for b in range(B):
                    for par in range(2):
                        last = nc.tensor.matmul(bank[64 * par:64 * par + 64, TB, 64 * b:64 * b + 64],
                                                linT[:, CH * b:CH * b + CH], wv_b[:, par], start=True, stop=True)
                last.then_inc(v_projected, 1)

            def lin_ktok(c):
                pe.wait_ge(phi_ready, 3 * c + 2)
                pe.wait_ge(lsub_ready, NCH + c)
                for half in range(2):
                    if half == 1:
                        pe.wait_ge(v_ready, 2 * (c + 1))
                    for q in range(4):
                        b = 4 * half + q
                        last = nc.tensor.transpose(bank[:, (MB, TB)[half], 128 * q:128 * q + 128],
                                                   phi_k[:, b].rearrange("p r t -> p (r t)"), ident[:])
                    last.then_inc(k_transposed, 1)

            def lin_scores(c, j):
                if j == 0:
                    taken = held(pe, c + 1)
                    pe.wait_ge(go, 1)
                    pe.wait_ge(qbd_ready, taken)
                else:
                    read = held(pe, J * c + j)
                    pe.wait_ge(go, 1)
                    pe.wait_ge(att_ready, read)
                for p in range(2):
                    b = 2 * j + p
                    for par in range(2):
                        for r in range(2):
                            h = slice(64 * r, 64 * r + 64)
                            last = nc.tensor.matmul(
                                bank[64 * par:64 * par + 64, QB + r, 256 * p:256 * p + 256],
                                phi_k[h, b, 0], q_bd[h, par::2, CH * b:CH * b + CH],
                                start=True, stop=True)
                last.then_inc(scores, 1)

            def lin_numer(c, j):
                pe.wait_ge(att_ready, J * c + j + 1)
                if j == 0:
                    pe.wait_ge(v_ready, 2 * (c + 1))
                    pe.wait_ge(ktok_ready, 2 * (c + 1))
                    if due(c):
                        pe.wait_ge(state_ready, c)
                if j >= 2:
                    if due(J * c + j - 1):
                        pe.wait_ge(lin_ready, J * c + j - 1)
                for p in range(2):
                    b = 2 * j + p
                    o = bank[64 * p:64 * p + 64, (TB, MB)[j % 2], 0:H * HV]
                    for r in range(2):
                        for i4 in range(4):
                            n = 4 * r + i4
                            nc.tensor.matmul(o[:, 2 * HV * n:2 * HV * n + 2 * HV], att[:, j % 2, r, p, i4],
                                             v_bd[:, b, n].rearrange("p r e -> p (r e)"), start=(n == 0), stop=False,
                                             skip_group_check=True)
                    last = nc.tensor.matmul(o, phi_q[:, CH * b:CH * b + CH], state[:, b].rearrange("p h e -> p (h e)"),
                                            start=False, stop=True, skip_group_check=True)
                last.then_inc(numer, 1)

            def lin_state(c):
                pe.wait_ge(lin_ready, J * c + J - 1)
                for b in range(B):
                    o = bank[:, b // 3, H * HV * (b % 3):H * HV * (b % 3) + H * HV]
                    last = nc.tensor.matmul(o, k_tok[:, b], v_bd[:, b].rearrange("p n r e -> p (n r e)"),
                                            start=True, stop=True)
                last.then_inc(state_parts, 1)

            def lin_transpose(c):
                pe.wait_ge(lin_ready, J * (c + 1))
                for j in range(J):
                    last = nc.tensor.transpose(bank[:, MB, 128 * j:128 * j + 128], lin[:, j], ident[:])
                last.then_inc(lin_transposed, 1)

            def lin_project_out(c):
                pe.wait_ge(linT_ready, c + 1)
                for j in range(J):
                    o = bank[:, MB, 128 * j:128 * j + 128]
                    last = nc.tensor.matmul(o, linT[:, 128 * j:128 * j + 128], wo_b[:], start=True, stop=True)
                last.then_inc(lin_projected, 1)

            def lin_pre(c):
                if due(c):
                    pe.wait_ge(state_masked, 3 * c)
                prep_transpose(NCH + c)

            def step2(i, lin=True, pre=True):
                n = NCH + i - 1
                moe_up(n, 0)
                moe_up(n, 1)
                if lin:
                    lin_ktok(i)
                moe_down(n, 0)
                if lin:
                    lin_scores(i, 0)
                moe_expert(n, 2)
                if lin:
                    lin_scores(i, 1)
                    lin_numer(i, 0)
                moe_expert(n, 3)
                if lin:
                    lin_scores(i, 2)
                    lin_numer(i, 1)
                    lin_scores(i, 3)
                moe_expert(n, 4)
                if lin:
                    lin_numer(i, 2)
                    lin_numer(i, 3)
                moe_up(n, 5)
                if lin:
                    lin_state(i)
                    lin_transpose(i)
                moe_down(n, 4)
                moe_up(n, 6)
                if lin:
                    lin_project_out(i)
                moe_down(n, 5)
                moe_up(n, 7)
                if pre:
                    lin_pre(i + 1)
                moe_down(n, 6)
                if lin:
                    moe_transpose(n + 1)
                if pre:
                    lin_project(i + 1)
                if lin:
                    moe_route(n + 1)
                moe_down(n, 7)

            o, n = NCH - 1, NCH - 2
            for e in range(4):
                moe_expert(n, e)
            lin_pre(0)
            moe_expert(n, 4)
            out_norms(o)
            lin_project(0)
            moe_expert(n, 5)
            out_project(o)
            moe_expert(n, 6)
            moe_expert(n, 7)
            moe_transpose(o)
            moe_down(n, E - 1)
            moe_route(o)
            step2(0)
            with pe.Fori(1, NCH - 1) as i:
                step2(i)
            step2(NCH - 1, pre=False)
            step2(NCH, lin=False, pre=False)

        @block.vector
        def _(dve):
            tt, ts, stt, red = (nc.vector.tensor_tensor, nc.vector.tensor_scalar, nc.vector.scalar_tensor_tensor,
                                nc.vector.tensor_reduce)

            def stats(src, b6, out_mv, bn_done, mv_ready, c):
                for j in range(J):
                    nc.vector.bn_stats(b6[:, j], src[:, j]).then_inc(bn_done, 1)
                done = held(dve, J * (c + 1))
                dve.wait_ge(go, 1)
                dve.wait_ge(bn_done, done)
                for j in range(J):
                    nc.vector.bn_aggr(out_mv[:, j], b6[:, j]).then_inc(mv_ready, 1)

            def normed(dst, src, mvt, r, j, done):
                ts(dst[:, j], src[:, j], mvt[:, j, 0:1], r[:, j:j + 1], ALU.subtract, ALU.mult).then_inc(done, 1)

            def prep_xnT_rest(c):
                dve.wait_ge(xnT_ready, c + 1)
                tt(xnT_l[:, :, KC - 1:], bank[:, TB, :].rearrange("p (b t) -> p b t", b=B),
                   xnT_h[:, :, KC - 1:].bitcast(F32), ALU.subtract).then_inc(xnT_rest, 1)

            def prep_silu(c, z):
                dve.wait_ge(sig_ready, 3 * c + z + 1)
                if z == 0:
                    if due(16 * 4 * c):
                        dve.wait_ge(qkv_stored, 16 * 4 * c)
                tt(qkv[:, z], bank[:, (QB, KB, QB)[z], :], sig[:, z], ALU.mult).then_inc(silu_ready, 1)

            def prep_qk(c):
                dve.wait_ge(norm_ready, c + 1)
                stt(qkv[:, 0], qkv[:, 0], QSCALE, rqk[:, 0], ALU.mult, ALU.mult).then_inc(qk_ready, 1)
                tt(qkv[:, 1], qkv[:, 1], rqk[:, 1], ALU.mult).then_inc(qk_ready, 1)

            def delta_take(c, first=False):
                dve.wait_ge(pre, PRE_OPS * (c + 1))
                if not first:
                    dve.wait_ge(step, 4 * NB * c)
                nc.vector.tensor_copy(prod[:, :, :, HD].rearrange("p t m -> p m t"), wv[:, HD:2 * HD]).then_inc(taken, 1)
                ts(nw[:], wv[:, 0:HD], -1.0, None, ALU.mult).then_inc(taken, 1)
                if first:
                    nc.vector.memset(hist[:, 0, :, :, BS], 0.0).then_inc(taken, 1)
                else:
                    dve.wait_ge(o_part, GROUP_OPS * (NG * (c - 1) + 1))
                    nc.vector.tensor_copy(hist[:, 0, :, :, BS], hist[:, NB, :, :, BS]).then_inc(taken, 1)
                nc.vector.tensor_copy(k_p[:], pin[:, 0]).then_inc(taken, 1)
                dve.wait_ge(taken, TAKES * (c + 1))

            def delta_products(c, n, first=False):
                t = slice(BS * n, BS * n + BS)
                for g, (begin, _) in enumerate(O_GROUPS):
                    if g and n == begin - 1 and not first:
                        dve.wait_ge(o_part, GROUP_OPS * (NG * (c - 1) + g + 1))
                if n:
                    dve.wait_ge(step, 4 * (NB * c + n))
                tt(prod[:, t, :, 0:HD], bc(hist[:, n, :, :, BS], 1, BS), bc(nw[:, :, t].rearrange("p d t -> p t d"), 2, HD),
                   ALU.mult).then_inc(step, 1)

            def delta_u(c, n):
                dve.wait_ge(step, 4 * (NB * c + n) + 1)
                red(u[:, n], prod[:, BS * n:BS * n + BS], AX_X, ALU.add).then_inc(step, 1)

            def delta_outer(c, n):
                dve.wait_ge(step, 4 * (NB * c + n) + 2)
                tt(hist[:, n, :, :, 0:BS].rearrange("p m d s -> p s m d"), bc(u[:, n], 3, HD),
                   bc(k_p[:, :, BS * n:BS * n + BS].rearrange("p d t -> p t d"), 2, HD), ALU.mult).then_inc(step, 1)

            def delta_state(c, n):
                dve.wait_ge(step, 4 * (NB * c + n) + 3)
                red(hist[:, n + 1, :, :, BS], hist[:, n], AX_X, ALU.add).then_inc(step, 1)

            def delta_kdot(c):
                dve.wait_ge(pre, PRE_OPS * c + BS)
                red(kdot[:], kk[:].rearrange("p d k n -> p k n d"), AX_X, ALU.add).then_inc(kdot_ready, 1)

            def delta_qdot(c):
                dve.wait_ge(qk_products, 3 * (c + 1))
                red(qdot[:, 0], qk[:, :, 0].rearrange("p d n -> p n d"), AX_X, ALU.add).then_inc(qdot_ready, 1)
                red(qdot[:, 1:], qk[:, :, 1:].rearrange("p d k n -> p k n d"), AX_X, ALU.add).then_inc(qdot_plain, 1)

            def delta_qdot_sign(c):
                dve.wait_ge(qdot_plain, c + 1)
                ts(qdot[:, 1:], qdot[:, 1:], -1.0, None, ALU.mult).then_inc(qdot_ready, 1)

            def delta_sum(c, g):
                first, end = O_GROUPS[g]
                dve.wait_ge(o_part, GROUP_OPS * (NG * c + g + 1))
                dve.wait_ge(oq_cleared, 2)
                if g == 0:
                    if due(c):
                        dve.wait_ge(o_stored, 16 * c)
                red(o_p[:, :, BS * first:BS * end].rearrange("p m t -> p t m"),
                    oq_mem[:, oq_size * (g % 2):oq_size * (g % 2) + (end - first) * BS * HD * (HD + 1)].rearrange(
                        "p (t m d) -> p t m d", m=HD, d=HD + 1), AX_X, ALU.add).then_inc(o_summed, 1)

            def out_on(c):
                dve.wait_ge(o_rnorm, c + 1)
                tt(on[:], o_T[:], orn[:], ALU.mult).then_inc(on_ready, 1)

            def out_residual(c):
                dve.wait_ge(o_projected, c + 1)
                dve.wait_ge(xr_loaded, 16 * (c + 1))
                tt(x_r[:], x_r[:], bank[:, MB, :].rearrange("p (j d) -> p j d", j=J), ALU.add).then_inc(xr_ready, 1)

            def moe_xn(n, src, j):
                if j == 0:
                    dve.wait_ge(rstdf_ready, n + 1)
                    if due(n):
                        dve.wait_ge(xf_transposed, n)
                normed(xf, src, mvf, rstdf, j, xf_ready)

            def moe_logits(n):
                dve.wait_ge(routed, n + 1)
                lp = bank[:, MB, 0:J * E].rearrange("p (j e) -> p j e", j=J)
                nc.vector.tensor_copy(logit[:], lp).then_inc(route, 1)
                red(lmax[:], lp, AX_X, ALU.max).then_inc(route, 1)

            def moe_above(n):
                dve.wait_ge(route, 9 * n + 2)
                tt(lsub[:], logit[:], bc(lmax[:], 2, E), ALU.subtract).then_inc(lsub_ready, 1)
                other, own = bc(logit[:], 2, E), bc(logit[:], 3, E)
                tt(above[:], other, own, ALU.is_gt).then_inc(route, 1)
                tt(same[:], other, own, ALU.is_equal).then_inc(route, 1)

            def moe_ties(n):
                dve.wait_ge(route, 9 * n + 4)
                tt(same[:], same[:], bc(lower[:], 1, J), ALU.mult).then_inc(route, 1)

            def moe_level(n):
                dve.wait_ge(route, 9 * n + 5)
                tt(above[:], above[:], same[:], ALU.add).then_inc(route, 1)

            def moe_ranks(n):
                dve.wait_ge(route, 9 * n + 6)
                red(rank[:], above[:], AX_X, ALU.add).then_inc(route, 1)

            def moe_pick(n):
                dve.wait_ge(pexp_ready, n + 1)
                dve.wait_ge(route, 9 * n + 7)
                stt(pick[:], rank[:], 1.5, pexp[:], ALU.is_lt, ALU.mult).then_inc(route, 1)

            def moe_pick_sum(n):
                dve.wait_ge(route, 9 * n + 8)
                red(psum[:], pick[:], AX_X, ALU.add).then_inc(route, 1)

            def moe_pick_inverse(n):
                dve.wait_ge(route, 9 * n + 9)
                nc.vector.reciprocal(rsum[:], psum[:]).then_inc(psum_inv, 1)

            def moe_weights(n):
                dve.wait_ge(psum_inv, n + 1)
                if due(n):
                    dve.wait_ge(gate_taken, n)
                tt(gate[:], pick[:], bc(rsum[:], 2, E), ALU.mult).then_inc(gate_ready, 1)

            def moe_rank(n):
                moe_logits(n)
                moe_above(n)
                moe_ties(n)
                moe_level(n)
                moe_ranks(n)

            def moe_gate(n):
                moe_pick(n)
                moe_pick_sum(n)
                moe_pick_inverse(n)
                moe_weights(n)

            def moe_split(n):
                dve.wait_ge(xT_ready, n + 1)
                tt(xT_l[:], xfT[:], xT_h[:].bitcast(F32), ALU.subtract).then_inc(xT_rest, 1)

            def moe_take(n):
                dve.wait_ge(gate_ready, n + 1)
                if due(EV * n):
                    dve.wait_ge(even_scaled, EV * n)
                    dve.wait_ge(odd_scaled, EV * n)
                nc.vector.tensor_copy(gate_now[:], gate[:]).then_inc(gate_taken, 1)
                dve.wait_ge(gate_taken, n + 1)

            def moe_add(n, e, src=x2):
                dve.wait_ge(even_scaled, EV * n + e // 2 + 1)
                if e:
                    dve.wait_ge(added, EV * n + e // 2)
                elif due(EV * n):
                    dve.wait_ge(odd_added, EV * n)
                tt(x2[:], y_even[:], src if src is x3 else src[:], ALU.add).then_inc(added, 1)

            dve.wait_ge(prep_loaded, 16 * PREP_W)
            tt(wtap[:, 0:3 * KC].rearrange("p (z k) f -> p z k f", k=KC), bc(wqkv[:], 2, KC),
               wtap[:, 0:3 * KC].rearrange("p (z k) f -> p z k f", k=KC), ALU.mult).then_inc(taps_scaled, 1)
            dve.wait_ge(pool_ready, POOL_ALL)
            dve.wait_ge(taps_split, 1)
            tt(wtap_l[:], wtap, wtap_h[:].bitcast(F32), ALU.subtract).then_inc(taps_split, 1)

            def between(i, blk, gap, prep, out, moe, ahead):
                c, o, n = i + 2, i - 1, i - 2
                if prep:
                    if blk == 2 and gap == 3:
                        prep_xnT_rest(c)
                    elif out and (blk, gap) in ((6, 2), (9, 3), (13, 0)):
                        prep_silu(c, (6, 9, 13).index(blk))
                    elif not out and (blk, gap) in ((5, 2), (8, 0), (10, 0)):
                        prep_silu(c, (5, 8, 10).index(blk))
                    elif blk == 15 and gap == 3:
                        prep_qk(c)
                if moe:
                    if blk == 0:
                        if gap == 0:
                            moe_level(n)
                        elif gap == 1:
                            moe_ranks(n)
                        elif gap == 2:
                            moe_pick(n)
                        else:
                            moe_pick_sum(n)
                    elif blk == 1:
                        if gap == 0:
                            moe_pick_inverse(n)
                        elif gap == 1:
                            moe_weights(n)
                        elif gap == 2:
                            moe_take(n)
                    elif (blk, gap) in ((3, 0), (8, 0), (13, 3), (15, 0)):
                        e = 2 * (3, 8, 13, 15).index(blk)
                        moe_add(n, e, x2 if e else x_r)
                if ahead and blk == (6 if moe else 9) and gap == 0:
                    delta_kdot(i + 1)
                if blk == 4 and gap == 2:
                    delta_qdot(i)
                elif blk == 4 and gap == 3:
                    delta_qdot_sign(i)
                elif blk == 14 and gap == 2:
                    delta_sum(i, 0)
                if out:
                    if blk == 1 and gap == 3:
                        delta_sum(o, 1)
                    elif blk == 2 and gap == 0:
                        delta_sum(o, 2)
                    elif blk == 7 and gap == 0:
                        out_on(o)
                    elif blk == 9 and gap == 0:
                        out_residual(o)
                    elif blk == 14 and gap == 0:
                        moe_split(o)
                    elif blk == 15:
                        if gap == 1:
                            moe_logits(o)
                        elif gap == 2:
                            moe_above(o)
                        elif gap == 3:
                            moe_ties(o)

            def step1(i, prep=True, out=True, moe=True, ahead=True, first=False):
                delta_take(i, first)
                for blk in range(NB):
                    delta_products(i, blk, first)
                    between(i, blk, 0, prep, out, moe, ahead)
                    delta_u(i, blk)
                    between(i, blk, 1, prep, out, moe, ahead)
                    delta_outer(i, blk)
                    between(i, blk, 2, prep, out, moe, ahead)
                    delta_state(i, blk)
                    between(i, blk, 3, prep, out, moe, ahead)

            prep_xnT_rest(0)
            for z in range(3):
                prep_silu(0, z)
            prep_xnT_rest(1)
            prep_qk(0)
            for z in range(2):
                prep_silu(1, z)
            delta_kdot(0)
            prep_silu(1, 2)
            dve.wait_ge(w1_split, 1)
            tt(w1_l[:], w1, w1_h[:].bitcast(F32), ALU.subtract).then_inc(w1_split, 1)
            ts(wo_n[:], wo_a[:], onorm[:], None, ALU.mult).then_inc(taps_ready, 1)
            prep_qk(1)
            dve.wait_ge(taps_split, 2)
            step1(0, out=False, moe=False, first=True)
            step1(1, moe=False)
            step1(2)
            with dve.Fori(3, NCH - 2) as i:
                step1(i)
            step1(NCH - 2, prep=False)
            step1(NCH - 1, prep=False, ahead=False)

            def lin_pre(c):
                dve.wait_ge(xb_loaded, 16 * (c + 1))
                stats(x_b, bn6, mv, bn_done, mv_ready, c)

            def lin_xn(c):
                dve.wait_ge(rstd_ready, NCH + c + 1)
                if due(NCH + c):
                    dve.wait_ge(xn_transposed, NCH + c)
                for j in range(J):
                    normed(xn, x_b, mv, rstd, j, xn_ready)

            def lin_phi_low(c):
                dve.wait_ge(qk_projected, c + 1)
                ts(phi_min[:], bank[:, QB:QB + 2, :], 0.0, None, ALU.min).then_inc(phi_low, 1)

            def lin_phi(c):
                dve.wait_ge(phi_exp, c + 1)
                for r in range(2):
                    stt(phi_k[:, :, r], bank[:, KB, :].rearrange("p (b t) -> p b t", b=B), 0.0,
                        phi_min[:, 1].rearrange("p (b t) -> p b t", b=B), ALU.max, ALU.add).then_inc(phi_ready, 1)
                stt(phi_q, bank[:, QB, :], 0.0, phi_min[:, 0], ALU.max, ALU.add).then_inc(phi_ready, 1)
                dve.wait_ge(phi_ready, 3 * c + 3)
                for h in range(HD):
                    last = ts(q_bd[:, h], phi_q, head_mask[:, h:h + 1], None, ALU.mult)
                last.then_inc(qbd_ready, 1)

            def lin_att(c, j):
                dve.wait_ge(scores, J * c + j + 1)
                if due(J * c + j - 1):
                    dve.wait_ge(numer, J * c + j - 1)
                tt(att[:, j % 2].rearrange("p r b i t -> p (r b i) t"),
                   bank[:, QB:QB + 2, :].rearrange("p r (n t) -> p (r n) t", t=CH),
                   bc(causal[:], 1, 16), ALU.mult).then_inc(att_ready, 1)

            def lin_out(c, j):
                dve.wait_ge(numer, J * c + j + 1)
                src = bank[:, (TB, MB)[j % 2], 0:H * HV].rearrange("p (h e) -> p h e", h=H)
                ts(den[:, j], src[:, :, HD], LIN_EPS, None, ALU.add).then_inc(den_ready, 1)
                dve.wait_ge(den_ready, J * c + j + 1)
                nc.vector.reciprocal(rden[:, j], den[:, j]).then_inc(rden_ready, 1)
                dve.wait_ge(rden_ready, J * c + j + 1)
                tt(lin[:, j].rearrange("p (h e) -> p h e", h=H), src[:, :, 0:HD], bc(rden[:, j], 2, HD), ALU.mult
                   ).then_inc(lin_ready, 1)

            def lin_state(c):
                dve.wait_ge(state_parts, c + 1)
                for k in range(3):
                    nb = min(3, B - 3 * k)
                    tt(dstate[:, 3 * k:3 * k + nb].rearrange("p b h e -> p b (h e)"),
                       bank[:, k, 0:nb * H * HV].rearrange("p (b f) -> p b f", b=nb),
                       bc(state_mask[:].rearrange("p h e -> p (h e)"), 1, nb), ALU.mult).then_inc(state_masked, 1)
                dve.wait_ge(state_masked, 3 * (c + 1))
                tt(state[:], state[:], dstate, ALU.add).then_inc(state_ready, 1)

            def lin_residual(c):
                dve.wait_ge(lin_projected, c + 1)
                dve.wait_ge(kept, c + 1)
                if due(c):
                    dve.wait_ge(added, EV * (NCH + c - 1) + 1)
                tt(x3, x_keep[:], bank[:, MB, :].rearrange("p (j d) -> p j d", j=J), ALU.add).then_inc(x3_ready, 1)
                dve.wait_ge(x3_ready, c + 1)
                stats(x3, bn6f, mvf, bnf_done, mvf_ready, c)

            def lin_keep(c):
                if due(c):
                    dve.wait_ge(x3_ready, c)
                tt(x_keep[:], x_b[:], bc(bo_rows[:], 1, J), ALU.add).then_inc(kept, 1)

            def step2(i, lin=True, pre=True, src=x3):
                n = NCH + i - 1
                moe_take(n)
                if lin:
                    lin_att(i, 0)
                moe_add(n, 0, src)
                if lin:
                    lin_att(i, 1)
                    lin_out(i, 0)
                if lin:
                    lin_att(i, 2)
                    lin_out(i, 1)
                    lin_att(i, 3)
                if pre:
                    lin_pre(i + 1)
                moe_add(n, 2)
                if lin:
                    lin_out(i, 2)
                    lin_out(i, 3)
                if lin:
                    lin_state(i)
                if pre:
                    lin_xn(i + 1)
                moe_add(n, 4)
                if lin:
                    lin_residual(i)
                if pre:
                    lin_keep(i + 1)
                if lin:
                    for j in range(J):
                        moe_xn(n + 1, x3, j)
                moe_add(n, 6)
                if lin:
                    moe_split(n + 1)
                if pre:
                    lin_phi_low(i + 1)
                if lin:
                    moe_rank(n + 1)
                if pre:
                    lin_phi(i + 1)
                if lin:
                    moe_gate(n + 1)

            o, n = NCH - 1, NCH - 2
            moe_level(n)
            moe_ranks(n)
            moe_gate(n)
            moe_take(n)
            lin_pre(0)
            delta_sum(o, 1)
            lin_xn(0)
            lin_keep(0)
            moe_add(n, 0, x_r)
            delta_sum(o, 2)
            moe_add(n, 2)
            out_on(o)
            lin_phi_low(0)
            out_residual(o)
            lin_phi(0)
            moe_add(n, 4)
            moe_split(o)
            moe_rank(o)
            moe_add(n, 6)
            moe_gate(o)
            step2(0, src=x_r)
            with dve.Fori(1, NCH - 1) as i:
                step2(i)
            step2(NCH - 1, pre=False)
            step2(NCH, lin=False, pre=False)


def kernel(**inputs):
    import numpy as np
    import concourse.bacc as bacc
    from concourse.bass_utils import run_bass_kernel_spmd

    def a(name):
        return np.asarray(inputs["L0_" + name])

    f = np.float32

    def rows(x):
        x = x.reshape(J, 2, NCH, CH, D).transpose(2, 1, 3, 0, 4)
        return np.ascontiguousarray(x.reshape(NCH, 128, J * D))

    p = np.arange(128)
    convs = np.stack([a("attn_a_conv_q").T, a("attn_a_conv_k").T, a("attn_a_conv_v").T])
    arrays = {
        "x": rows(a("attn_a_x")),
        "wqkv": np.stack([a("attn_a_Wq").T, a("attn_a_Wk").T, a("attn_a_Wv").T], axis=1),
        "conv": np.broadcast_to(convs[None], (128, 3, KC, D)).reshape(128, 3 * KC, D),
        "wbeta": np.pad(a("attn_a_Wb").T, ((0, 0), (0, D - H))),
        "wo_a": a("attn_a_Wo").T,
        "onorm": np.tile(a("attn_a_o_norm_w"), H)[:, None],
        "wqk_b": np.stack([a("attn_b_Wq").T, a("attn_b_Wk").T], axis=1),
        "wv_b": a("attn_b_Wv").T.reshape(D, NP, 2, HD).transpose(0, 2, 1, 3).reshape(D, 2, NP * HD),
        "wo_b": a("attn_b_Wo").T,
        "bo_rows": np.broadcast_to(a("attn_b_bo")[None], (128, D)),
        "wg": a("ffn_Wg"),
        "w1": a("ffn_W1").transpose(1, 0, 2),
        "w2": a("ffn_W2").reshape(E, FC, 128, D).transpose(2, 0, 1, 3),
        "ident": np.eye(128, dtype=f),
        "ones_block": (p[:, None] // HD == p[None] // HD).astype(f),
        "causal": (p[:, None] % CH <= np.arange(CH)[None]).astype(f),
        "lower": np.broadcast_to((np.arange(E)[None] < np.arange(E)[:, None]).astype(f), (128, E, E)),
        "state_mask": np.broadcast_to((p[:, None, None] // HD == np.arange(H)[None, :, None]), (128, H, HV)).astype(f),
        "head_mask": (p[:, None] // HD % HD == np.arange(HD)[None]).astype(f),
    }
    arrays = {k: np.ascontiguousarray(v) for k, v in arrays.items()}
    nc = bacc.Bacc("TRN2", target_bir_lowering=False, num_devices=1)
    d = {k: nc.dram_tensor("in_" + k, v.shape, mybir.dt.from_np(v.dtype), kind="ExternalInput").ap()
         for k, v in arrays.items()}
    out = nc.dram_tensor("out_x", (NCH, 128, J * D), F32, kind="ExternalOutput").ap()
    build(nc, d, out)
    r = run_bass_kernel_spmd(nc, [{"in_" + k: v for k, v in arrays.items()}], core_ids=[0])
    y = r.results[0]["out_x"].reshape(NCH, 2, CH, J, D).transpose(3, 1, 0, 2, 4)
    return np.ascontiguousarray(y.reshape(B, L, D))
```
